# Optimizing a Trainium2 kernel written in Bass

```python
import numpy as np
import jax
import jax.numpy as jnp

def _softmax(x, axis=-1):
    return jax.nn.softmax(x, axis=axis)

def _gelu(x):
    return jax.nn.gelu(x, approximate=True)

def _silu(x):
    return jax.nn.silu(x)

def _sigmoid(x):
    return jax.nn.sigmoid(x)

def _layernorm(x, axis=-1, eps=1e-05):
    m = jnp.mean(x, axis=axis, keepdims=True)
    v = jnp.var(x, axis=axis, keepdims=True)
    return (x - m) / jnp.sqrt(v + eps)

def _scatter_add(tgt, idx, src, axis=0):
    return tgt.at[idx].add(src)

def _segment_sum(src, seg, n):
    return jax.ops.segment_sum(src, seg, n)
kernel_name = 'mk_adaln_ffn_d4_seqx_r8_f31e35'

def setup_inputs(seed: int=0):
    np.random.seed(seed)
    _w = jnp.asarray

    def _rec_inputs():
        import jax
        import jax.numpy as jnp
        _rk = jax.random.key(seed)
        x = 7.22e-05 + 1 * jax.random.normal(jax.random.fold_in(_rk, 1), (128, 32, 128), jnp.float32)
        _lenS = 32 - jax.random.randint(jax.random.fold_in(_rk, 7), (128,), 0, max(1, 32 // 4) + 1, jnp.int32)
        _lenS2 = 32 - jax.random.randint(jax.random.fold_in(_rk, 8), (128,), 0, max(1, 32 // 4) + 1, jnp.int32)
        cond_1024 = 0.0061147 + 1.02565 * jax.random.normal(jax.random.fold_in(_rk, 11), (128, 128), jnp.float32)
        return (x, cond_1024)
    x, cond_1024 = _rec_inputs()

    def _L0_cond_setup():
        import jax, jax.numpy as jnp
        import numpy as np
        D_MODEL = 128
        D_FF = 512
        N_EXPERTS = 8
        TOP_K = 2
        N_SHARED = 2
        B, T = (4, 256)
        key = jax.random.key(seed)
        ks = jax.random.split(key, 9)
        Hs = D_FF // 2
        Hr = D_FF // 4
        inp = {'x': jax.random.normal(ks[0], (B, T, D_MODEL), dtype=jnp.float32), 't_emb': jax.random.normal(ks[1], (B, D_MODEL), dtype=jnp.float32), 'W_router': 0.01 * jax.random.normal(ks[2], (N_EXPERTS, 2 * D_MODEL), dtype=jnp.float32), 'router_bias': jnp.zeros((N_EXPERTS,), dtype=jnp.float32), 's_w1': 0.02 * jax.random.normal(ks[3], (N_SHARED, Hs, D_MODEL), dtype=jnp.float32), 's_w3': 0.02 * jax.random.normal(ks[4], (N_SHARED, Hs, D_MODEL), dtype=jnp.float32), 's_w2': 0.02 * jax.random.normal(ks[5], (N_SHARED, D_MODEL, Hs), dtype=jnp.float32), 'r_w1': 0.02 * jax.random.normal(ks[6], (N_EXPERTS, Hr, D_MODEL), dtype=jnp.float32), 'r_w2': 0.02 * jax.random.normal(ks[7], (N_EXPERTS, D_MODEL, Hr), dtype=jnp.float32)}
        return inp
    _L0_cond_all = _L0_cond_setup()
    _L0_cond_in = {k: v for k, v in _L0_cond_all.items() if k in ('W_router', 'router_bias', 's_w1', 's_w3', 's_w2', 'r_w1', 'r_w2')}
    del _L0_cond_all

    def _L0_ffn_setup():
        import jax, jax.numpy as jnp
        import numpy as np
        NUM_EXPERTS = 8
        EXPERT_CAPACITY = 2.0
        key = jax.random.key(seed)
        k1, k2, k3, k4 = jax.random.split(key, 4)
        B, T, C, H, E = (4, 512, 128, 512, NUM_EXPERTS)
        x = jax.random.normal(k1, (B, T, C), jnp.float32)
        gate_w = jax.random.normal(k2, (C, E), jnp.float32) * 0.02
        w1 = jax.random.normal(k3, (E, C, H), jnp.float32) * 0.02
        w2 = jax.random.normal(k4, (E, H, C), jnp.float32) * 0.02
        return {'x': x, 'gate_w': gate_w, 'w1': w1, 'w2': w2}
    _L0_ffn_all = _L0_ffn_setup()
    _L0_ffn_in = {k: v for k, v in _L0_ffn_all.items() if k in ('gate_w', 'w1', 'w2')}
    del _L0_ffn_all

    def _L1_cond_setup():
        import jax, jax.numpy as jnp
        import numpy as np
        import math
        N, T, D, H = (64, 64, 128, 128)
        key = jax.random.key(seed)
        k1, k2, k3, k4 = jax.random.split(key, 4)
        x = jax.random.normal(k1, (N, T, D), dtype=jnp.float32)
        h0 = jax.random.normal(k2, (N, H), dtype=jnp.float32)
        Wx = jax.random.normal(k3, (D, 4 * H), dtype=jnp.float32) / math.sqrt(D)
        Wh = jax.random.normal(k4, (H, 4 * H), dtype=jnp.float32) / math.sqrt(H)
        b = jnp.zeros((4 * H,), dtype=jnp.float32)
        return {'x': x, 'h0': h0, 'Wx': Wx, 'Wh': Wh, 'b': b}
    _L1_cond_all = _L1_cond_setup()
    _L1_cond_in = {k: v for k, v in _L1_cond_all.items() if k in ('Wx', 'Wh', 'b')}
    del _L1_cond_all

    def _L1_ffn_setup():
        import jax, jax.numpy as jnp
        import numpy as np
        B, S, D_MODEL, D_HIDDEN = (4, 256, 128, 512)

        def act_quant(x):
            scale = 127.0 / jnp.clip(jnp.max(jnp.abs(x), axis=-1, keepdims=True), 1e-05)
            return jnp.clip(jnp.round(x * scale), -128, 127) / scale

        def weight_quant(w):
            scale = 1.0 / jnp.clip(jnp.mean(jnp.abs(w)), 1e-05)
            return jnp.clip(jnp.round(w * scale), -1, 1) / scale

        def bit_linear(x, w):
            xq = x + jax.lax.stop_gradient(act_quant(x) - x)
            wq = w + jax.lax.stop_gradient(weight_quant(w) - w)
            return jnp.einsum('bsd,hd->bsh', xq, wq)

        def depthwise_conv1d(x_bcl, w, b):
            y = jax.lax.conv_general_dilated(x_bcl, w, window_strides=(1,), padding=[(1, 1)], dimension_numbers=('NCH', 'OIH', 'NCH'), feature_group_count=x_bcl.shape[1])
            return y + b[None, :, None]
        key = jax.random.key(seed)
        ks = jax.random.split(key, 5)
        lim1 = 1.0 / np.sqrt(D_MODEL)
        lim2 = 1.0 / np.sqrt(D_HIDDEN)
        limc = 1.0 / np.sqrt(3.0)
        return {'x': jax.random.normal(ks[0], (B, S, D_MODEL), dtype=jnp.float32), 'w1': jax.random.uniform(ks[1], (D_HIDDEN, D_MODEL), jnp.float32, -lim1, lim1), 'conv_w': jax.random.uniform(ks[2], (D_HIDDEN, 1, 3), jnp.float32, -limc, limc), 'conv_b': jax.random.uniform(ks[3], (D_HIDDEN,), jnp.float32, -limc, limc), 'w2': jax.random.uniform(ks[4], (D_MODEL, D_HIDDEN), jnp.float32, -lim2, lim2)}
    _L1_ffn_all = _L1_ffn_setup()
    _L1_ffn_in = {k: v for k, v in _L1_ffn_all.items() if k in ('w1', 'conv_w', 'conv_b', 'w2')}
    del _L1_ffn_all

    def _L2_cond_setup():
        import jax, jax.numpy as jnp
        import numpy as np
        N, T, D, H = (128, 64, 128, 128)
        key = jax.random.key(seed)
        k1, k2, k3, k4 = jax.random.split(key, 4)
        x = jax.random.normal(k1, (N, T, D), dtype=jnp.float32)
        h0 = jax.random.normal(k2, (N, H), dtype=jnp.float32)
        Wx = jax.random.normal(k3, (D, H), dtype=jnp.float32) / np.sqrt(D)
        Wh = jax.random.normal(k4, (H, H), dtype=jnp.float32) / np.sqrt(H)
        b = jnp.zeros((H,), dtype=jnp.float32)
        return {'x': x, 'h0': h0, 'Wx': Wx, 'Wh': Wh, 'b': b}
    _L2_cond_all = _L2_cond_setup()
    _L2_cond_in = {k: v for k, v in _L2_cond_all.items() if k in ('Wx', 'Wh', 'b')}
    del _L2_cond_all

    def _L2_ffn_setup():
        import jax, jax.numpy as jnp
        import numpy as np
        EMB = 128
        FF = 4 * EMB

        def _ternary(w):
            scale = jnp.maximum(jnp.mean(jnp.abs(w)), 1e-08)
            w_t = jnp.clip(jnp.round(w / scale), -1.0, 1.0)
            return w + jax.lax.stop_gradient(w_t - w)
        key = jax.random.key(seed)
        kx, k1, k2, kb1, kb2 = jax.random.split(key, 5)
        x = jax.random.normal(kx, (4, 256, EMB), dtype=jnp.float32)
        lim1 = 1.0 / np.sqrt(EMB)
        lim2 = 1.0 / np.sqrt(FF)
        W1 = jax.random.uniform(k1, (FF, EMB), jnp.float32, -lim1, lim1)
        b1 = jax.random.uniform(kb1, (FF,), jnp.float32, -lim1, lim1)
        W2 = jax.random.uniform(k2, (EMB, FF), jnp.float32, -lim2, lim2)
        b2 = jax.random.uniform(kb2, (EMB,), jnp.float32, -lim2, lim2)
        return {'x': x, 'W1': W1, 'b1': b1, 'W2': W2, 'b2': b2}
    _L2_ffn_all = _L2_ffn_setup()
    _L2_ffn_in = {k: v for k, v in _L2_ffn_all.items() if k in ('W1', 'b1', 'W2', 'b2')}
    del _L2_ffn_all

    def _L3_cond_setup():
        import jax, jax.numpy as jnp
        import numpy as np
        LATENT = 128
        key = jax.random.key(seed)
        k1, k2, k3, k4 = jax.random.split(key, 4)
        B, T, D = (64, 64, LATENT)
        h_t = jax.random.normal(k1, (B, D), dtype=jnp.float32)
        z = jax.random.normal(k2, (B, T, D), dtype=jnp.float32)
        bound = 1.0 / np.sqrt(2 * D)
        W = jax.random.uniform(k3, (D, 2 * D), minval=-bound, maxval=bound, dtype=jnp.float32)
        b = jax.random.uniform(k4, (D,), minval=-bound, maxval=bound, dtype=jnp.float32)
        alpha = jnp.full((D,), 0.1, dtype=jnp.float32)
        return {'h_t': h_t, 'z': z, 'W': W, 'b': b, 'alpha': alpha}
    _L3_cond_all = _L3_cond_setup()
    _L3_cond_in = {k: v for k, v in _L3_cond_all.items() if k in ('W', 'b', 'alpha')}
    del _L3_cond_all

    def _L3_ffn_setup():
        import jax, jax.numpy as jnp
        import numpy as np
        DIM = 128

        def _reference_tuple_inner(x, W_r, W_k, W_v, mu_r, mu_k):
            B, T, C = x.shape
            x_prev = jnp.concatenate([jnp.zeros((B, 1, C), x.dtype), x[:, :-1, :]], axis=1)
            xr = mu_r * x + (1.0 - mu_r) * x_prev
            xk = mu_k * x + (1.0 - mu_k) * x_prev
            r = jax.nn.sigmoid(jnp.einsum('btc,dc->btd', xr, W_r))
            k = jnp.einsum('btc,dc->btd', xk, W_k)
            k_act = jnp.square(jax.nn.relu(k))
            out = r * jnp.einsum('btc,dc->btd', k_act, W_v)
            new_state = x[:, -1, :]
            return (out, new_state)
        key = jax.random.key(seed)
        ks = jax.random.split(key, 6)
        B, T, C = (8, 256, DIM)
        x = jax.random.normal(ks[0], (B, T, C), dtype=jnp.float32)
        s = 1.0 / np.sqrt(C)
        W_r = jax.random.uniform(ks[1], (C, C), jnp.float32, -s, s)
        W_k = jax.random.uniform(ks[2], (C, C), jnp.float32, -s, s)
        W_v = jax.random.uniform(ks[3], (C, C), jnp.float32, -s, s)
        mu_r = jax.random.uniform(ks[4], (C,), jnp.float32)
        mu_k = jax.random.uniform(ks[5], (C,), jnp.float32)
        return {'x': x, 'W_r': W_r, 'W_k': W_k, 'W_v': W_v, 'mu_r': mu_r, 'mu_k': mu_k}
    _L3_ffn_all = _L3_ffn_setup()
    _L3_ffn_in = {k: v for k, v in _L3_ffn_all.items() if k in ('W_r', 'W_k', 'W_v', 'mu_r', 'mu_k')}
    del _L3_ffn_all
    return {'x': x, 'cond_1024': cond_1024, 'L0_cond_W_router': _L0_cond_in['W_router'], 'L0_cond_router_bias': _L0_cond_in['router_bias'], 'L0_cond_s_w1': _L0_cond_in['s_w1'], 'L0_cond_s_w3': _L0_cond_in['s_w3'], 'L0_cond_s_w2': _L0_cond_in['s_w2'], 'L0_cond_r_w1': _L0_cond_in['r_w1'], 'L0_cond_r_w2': _L0_cond_in['r_w2'], 'L0_ffn_gate_w': _L0_ffn_in['gate_w'], 'L0_ffn_w1': _L0_ffn_in['w1'], 'L0_ffn_w2': _L0_ffn_in['w2'], 'L1_cond_Wx': _L1_cond_in['Wx'], 'L1_cond_Wh': _L1_cond_in['Wh'], 'L1_cond_b': _L1_cond_in['b'], 'L1_ffn_w1': _L1_ffn_in['w1'], 'L1_ffn_conv_w': _L1_ffn_in['conv_w'], 'L1_ffn_conv_b': _L1_ffn_in['conv_b'], 'L1_ffn_w2': _L1_ffn_in['w2'], 'L2_cond_Wx': _L2_cond_in['Wx'], 'L2_cond_Wh': _L2_cond_in['Wh'], 'L2_cond_b': _L2_cond_in['b'], 'L2_ffn_W1': _L2_ffn_in['W1'], 'L2_ffn_b1': _L2_ffn_in['b1'], 'L2_ffn_W2': _L2_ffn_in['W2'], 'L2_ffn_b2': _L2_ffn_in['b2'], 'L3_cond_W': _L3_cond_in['W'], 'L3_cond_b': _L3_cond_in['b'], 'L3_cond_alpha': _L3_cond_in['alpha'], 'L3_ffn_W_r': _L3_ffn_in['W_r'], 'L3_ffn_W_k': _L3_ffn_in['W_k'], 'L3_ffn_W_v': _L3_ffn_in['W_v'], 'L3_ffn_mu_r': _L3_ffn_in['mu_r'], 'L3_ffn_mu_k': _L3_ffn_in['mu_k']}

def reference(x, cond_1024, L0_cond_W_router, L0_cond_router_bias, L0_cond_s_w1, L0_cond_s_w3, L0_cond_s_w2, L0_cond_r_w1, L0_cond_r_w2, L0_ffn_gate_w, L0_ffn_w1, L0_ffn_w2, L1_cond_Wx, L1_cond_Wh, L1_cond_b, L1_ffn_w1, L1_ffn_conv_w, L1_ffn_conv_b, L1_ffn_w2, L2_cond_Wx, L2_cond_Wh, L2_cond_b, L2_ffn_W1, L2_ffn_b1, L2_ffn_W2, L2_ffn_b2, L3_cond_W, L3_cond_b, L3_cond_alpha, L3_ffn_W_r, L3_ffn_W_k, L3_ffn_W_v, L3_ffn_mu_r, L3_ffn_mu_k):
    import jax
    import jax.numpy as jnp

    def _L0_cond_ref(x, t_emb, W_router, router_bias, s_w1, s_w3, s_w2, r_w1, r_w2):
        import jax, jax.numpy as jnp
        import numpy as np
        D_MODEL = 128
        D_FF = 512
        N_EXPERTS = 8
        TOP_K = 2
        N_SHARED = 2
        B, T = (4, 256)
        Bn, Tn, C = x.shape
        N = Bn * Tn
        x_flat = x.reshape(N, C)
        t_flat = jnp.broadcast_to(t_emb[:, None, :], (Bn, Tn, C)).reshape(N, C)
        shared_out = jnp.zeros_like(x_flat)
        for e in range(N_SHARED):
            h = jax.nn.silu(x_flat @ s_w1[e].T) * (x_flat @ s_w3[e].T)
            shared_out = shared_out + h @ s_w2[e].T
        shared_out = shared_out / N_SHARED
        router_in = jnp.concatenate([x_flat, t_flat], axis=-1)
        s = jax.nn.sigmoid((router_in @ W_router.T).astype(jnp.float32))
        sel_scores = s + router_bias
        _, topk_idx = jax.lax.top_k(sel_scores, TOP_K)
        s_sel = jnp.take_along_axis(s, topk_idx, axis=1)
        denom = jnp.sum(s_sel, axis=1, keepdims=True)
        gates = jnp.where(denom > 1e-09, s_sel / (denom + 1e-09), 1.0 / TOP_K).astype(x.dtype)
        gates_full = jnp.sum(jax.nn.one_hot(topk_idx, N_EXPERTS, dtype=x.dtype) * gates[..., None], axis=1)
        routed_out = jnp.zeros_like(x_flat)
        for e in range(N_EXPERTS):
            h = jax.nn.gelu(x_flat @ r_w1[e].T, approximate=False)
            routed_out = routed_out + h @ r_w2[e].T * gates_full[:, e:e + 1]
        out = (shared_out + routed_out) / (N_SHARED + TOP_K)
        return out.reshape(Bn, Tn, C)

    def _L0_ffn_ref(x, gate_w, w1, w2):
        import jax, jax.numpy as jnp
        import numpy as np
        NUM_EXPERTS = 8
        EXPERT_CAPACITY = 2.0
        B, T, C = x.shape
        E = gate_w.shape[1]
        cap = int(EXPERT_CAPACITY * T / E)
        scores = jnp.einsum('BTC,CE->BTE', x, gate_w)
        probs = jax.nn.softmax(scores, axis=-1)
        probs_et = jnp.transpose(probs, (0, 2, 1))
        top_p, top_idx = jax.lax.top_k(probs_et, cap)
        xin = jnp.take_along_axis(x[:, None, :, :], top_idx[..., None], axis=2)
        h = jax.nn.gelu(jnp.einsum('BElC,ECH->BElH', xin, w1), approximate=False)
        y = jnp.einsum('BElH,EHC->BElC', h, w2)
        y = y * top_p[..., None]
        b_idx = jnp.arange(B)[:, None, None]
        out = jnp.zeros((B, T, C), x.dtype).at[b_idx, top_idx].add(y)
        return out

    def _L1_cond_ref(x, h0, Wx, Wh, b):
        import jax, jax.numpy as jnp
        import numpy as np
        import math
        N, T, D, H = (64, 64, 128, 128)
        Hdim = h0.shape[1]
        c0 = jnp.zeros_like(h0)
        xW = jnp.einsum('ntd,dk->tnk', x, Wx) + b

        def step(carry, xw_t):
            prev_h, prev_c = carry
            a = xw_t + prev_h @ Wh
            i = jax.nn.sigmoid(a[:, :Hdim])
            f = jax.nn.sigmoid(a[:, Hdim:2 * Hdim])
            o = jax.nn.sigmoid(a[:, 2 * Hdim:3 * Hdim])
            g = jnp.tanh(a[:, 3 * Hdim:])
            next_c = f * prev_c + i * g
            next_h = o * jnp.tanh(next_c)
            return ((next_h, next_c), next_h)
        _, hs = jax.lax.scan(step, (h0, c0), xW)
        return jnp.transpose(hs, (1, 0, 2))

    def _L1_ffn_ref(x, w1, conv_w, conv_b, w2):
        import jax, jax.numpy as jnp
        import numpy as np
        B, S, D_MODEL, D_HIDDEN = (4, 256, 128, 512)

        def act_quant(x):
            scale = 127.0 / jnp.clip(jnp.max(jnp.abs(x), axis=-1, keepdims=True), 1e-05)
            return jnp.clip(jnp.round(x * scale), -128, 127) / scale

        def weight_quant(w):
            scale = 1.0 / jnp.clip(jnp.mean(jnp.abs(w)), 1e-05)
            return jnp.clip(jnp.round(w * scale), -1, 1) / scale

        def bit_linear(x, w):
            xq = x + jax.lax.stop_gradient(act_quant(x) - x)
            wq = w + jax.lax.stop_gradient(weight_quant(w) - w)
            return jnp.einsum('bsd,hd->bsh', xq, wq)

        def depthwise_conv1d(x_bcl, w, b):
            y = jax.lax.conv_general_dilated(x_bcl, w, window_strides=(1,), padding=[(1, 1)], dimension_numbers=('NCH', 'OIH', 'NCH'), feature_group_count=x_bcl.shape[1])
            return y + b[None, :, None]
        h = bit_linear(x, w1)
        h = depthwise_conv1d(h.transpose(0, 2, 1), conv_w, conv_b)
        h = h.transpose(0, 2, 1)
        h = jax.nn.silu(h)
        return bit_linear(h, w2)

    def _L2_cond_ref(x, h0, Wx, Wh, b):
        import jax, jax.numpy as jnp
        import numpy as np
        N, T, D, H = (128, 64, 128, 128)
        xW = jnp.einsum('ntd,dh->tnh', x, Wx) + b

        def step(h, xw_t):
            h_next = jnp.tanh(h @ Wh + xw_t)
            return (h_next, h_next)
        _, hs = jax.lax.scan(step, h0, xW)
        return jnp.swapaxes(hs, 0, 1)

    def _L2_ffn_ref(x, W1, b1, W2, b2):
        import jax, jax.numpy as jnp
        import numpy as np
        EMB = 128
        FF = 4 * EMB

        def _ternary(w):
            scale = jnp.maximum(jnp.mean(jnp.abs(w)), 1e-08)
            w_t = jnp.clip(jnp.round(w / scale), -1.0, 1.0)
            return w + jax.lax.stop_gradient(w_t - w)
        h = jnp.einsum('bsd,fd->bsf', x, _ternary(W1)) + b1
        h = jax.nn.gelu(h, approximate=False)
        out = jnp.einsum('bsf,df->bsd', h, _ternary(W2)) + b2
        return out

    def _L3_cond_ref(h_t, z, W, b, alpha):
        import jax, jax.numpy as jnp
        import numpy as np
        LATENT = 128
        D = h_t.shape[-1]
        Wh = W[:, :D]
        Wz = W[:, D:]
        leak = 1.0 - alpha

        def step(h, z_t):
            gate = jax.nn.sigmoid(h @ Wh.T + z_t @ Wz.T + b)
            h_new = jnp.tanh(h * leak + gate * z_t)
            return (h_new, h_new)
        _, hs = jax.lax.scan(step, h_t, jnp.swapaxes(z, 0, 1))
        return jnp.swapaxes(hs, 0, 1)

    def _L3_ffn_ref(x, W_r, W_k, W_v, mu_r, mu_k):
        import jax, jax.numpy as jnp
        import numpy as np
        DIM = 128

        def _reference_tuple_inner(x, W_r, W_k, W_v, mu_r, mu_k):
            B, T, C = x.shape
            x_prev = jnp.concatenate([jnp.zeros((B, 1, C), x.dtype), x[:, :-1, :]], axis=1)
            xr = mu_r * x + (1.0 - mu_r) * x_prev
            xk = mu_k * x + (1.0 - mu_k) * x_prev
            r = jax.nn.sigmoid(jnp.einsum('btc,dc->btd', xr, W_r))
            k = jnp.einsum('btc,dc->btd', xk, W_k)
            k_act = jnp.square(jax.nn.relu(k))
            out = r * jnp.einsum('btc,dc->btd', k_act, W_v)
            new_state = x[:, -1, :]
            return (out, new_state)
        return _reference_tuple_inner(x, W_r, W_k, W_v, mu_r, mu_k)[0]
    x = x + _L0_ffn_ref(_L0_cond_ref(x, cond_1024, L0_cond_W_router, L0_cond_router_bias, L0_cond_s_w1, L0_cond_s_w3, L0_cond_s_w2, L0_cond_r_w1, L0_cond_r_w2), L0_ffn_gate_w, L0_ffn_w1, L0_ffn_w2)
    x = x + _L1_ffn_ref(_L1_cond_ref(x, cond_1024, L1_cond_Wx, L1_cond_Wh, L1_cond_b), L1_ffn_w1, L1_ffn_conv_w, L1_ffn_conv_b, L1_ffn_w2)
    x = x + _L2_ffn_ref(_L2_cond_ref(x, cond_1024, L2_cond_Wx, L2_cond_Wh, L2_cond_b), L2_ffn_W1, L2_ffn_b1, L2_ffn_W2, L2_ffn_b2)
    x = x + _L3_ffn_ref(_L3_cond_ref(cond_1024, x, L3_cond_W, L3_cond_b, L3_cond_alpha), L3_ffn_W_r, L3_ffn_W_k, L3_ffn_W_v, L3_ffn_mu_r, L3_ffn_mu_k)
    return x

_drawn_inputs = setup_inputs


def setup_inputs(seed=0):
    import zlib

    import numpy as np

    out = dict(_drawn_inputs(seed))
    spreads = {'L0_cond_router_bias': (0.0, 0.8),
     'L1_cond_b': (0.0, 0.8),
     'L2_cond_b': (0.0, 0.1),
     'L3_cond_alpha': (0.10000000149011612, 0.6)}
    factors = {'L0_cond_W_router': 8.0,
     'L0_cond_s_w1': 8.0,
     'L0_cond_s_w3': 8.0,
     'L0_cond_s_w2': 8.0,
     'L0_cond_r_w1': 8.0,
     'L0_cond_r_w2': 8.0,
     'L0_ffn_gate_w': 8.0,
     'L0_ffn_w1': 8.0,
     'L0_ffn_w2': 8.0,
     'L1_cond_Wx': 4.287,
     'L1_cond_Wh': 8.0,
     'L1_ffn_w1': 4.269,
     'L1_ffn_conv_w': 4.045,
     'L2_ffn_b1': 8.0,
     'L2_ffn_b2': 8.0,
     'L3_cond_W': 8.0,
     'L3_cond_b': 28.027,
     'L3_ffn_W_r': 8.0,
     'L3_ffn_W_k': 8.0,
     'L3_ffn_W_v': 8.0,
     'L3_ffn_mu_r': 8.0,
     'L3_ffn_mu_k': 8.0}
    for name, (base, spread) in spreads.items():
        noise = np.random.default_rng([zlib.crc32(name.encode()), seed]).standard_normal(out[name].shape)
        drawn = base * np.exp(spread * noise) if base else spread * noise
        out[name] = jnp.asarray(drawn.astype(out[name].dtype))
    for name, factor in factors.items():
        out[name] = (out[name] * factor).astype(out[name].dtype)
    return out
```

```python
from contextlib import ExitStack

import concourse.bass as bass
from concourse import mybir

F32 = mybir.dt.float32
BF16 = mybir.dt.bfloat16
U32 = mybir.dt.uint32
ALU = mybir.AluOpType
ACT = mybir.ActivationFunctionType
X = mybir.AxisListType.X

N, T, C = 128, 32, 128
P = 128
TOK = N * T
NTILE = TOK // P
SEQ_TILE = P // T
E = 8
BANK = 512

HS_TILES = 4
CHUNK = 512
NCHUNK = TOK // CHUNK
TILES_CHUNK = CHUNK // P

CAP = 2 * T // E
H0 = 512
HT = H0 // P
SLOT_TILE = SEQ_TILE * E * CAP
SLOT_E = SEQ_TILE * CAP
GROUPS = 4
TILES_GROUP = NTILE // GROUPS
SLOT_GE = TILES_GROUP * SLOT_E

MAGIC = 1.5 * 2.0 ** 23


class Lin:

    def __init__(self, i, a, b):
        self.i, self.a, self.b = i, a, b

    def __add__(self, n):
        return Lin(self.i, self.a, self.b + n)

    def __sub__(self, n):
        return Lin(self.i, self.a, self.b - n)

    def __mul__(self, n):
        return Lin(self.i, self.a * n, self.b * n)

    __radd__, __rmul__ = __add__, __mul__


def val(x):
    return x.i * x.a + x.b if isinstance(x, Lin) else x


def below(x, n):
    return isinstance(x, int) and x < n


def turn(x):
    return Lin(x.i, x.a // 2, x.b // 2) if isinstance(x, Lin) else x // 2


def ds(start, size):
    return bass.ds(val(start), size)


def build_program(nc, t, out):
    ctx = ExitStack()

    def sb(name, shape, dt=F32):
        return ctx.enter_context(nc.sbuf_tensor(name, shape, dt))

    def sem(name):
        return ctx.enter_context(nc.semaphore(name))

    with ctx:
        pe, act, dve, pool, sp = nc.tensor, nc.scalar, nc.vector, nc.gpsimd, nc.sync
        bank = [ctx.enter_context(nc.psum_tensor(f"bank{i}", [P, BANK], F32)) for i in range(8)]

        xT = sb("xT", [P, TOK])
        x1 = sb("x1", [P, T, N])
        condT = sb("condT", [P, N])
        ident = sb("ident", [P, P])

        lstm_wx, lstm_wh = sb("lstm_wx", [P, 4 * P]), sb("lstm_wh", [P, 4 * P])
        ffn1_w1, ffn1_w2 = sb("ffn1_w1", [P, HT * P]), sb("ffn1_w2", [P, HT, C], BF16)
        ffn2_w1, ffn2_w2 = sb("ffn2_w1", [P, HT * P]), sb("ffn2_w2", [P, HT, C])
        rnn_wx, rnn_wh, leak_wz, leak_wh, ffn3_wr, ffn3_wk, ffn3_wv = (sb(n, [P, P]) for n in (
            "rnn_wx", "rnn_wh", "leak_wz", "leak_wh", "ffn3_wr", "ffn3_wk", "ffn3_wv"))
        rnn_b, ffn2_b2, leak_b, alpha, mu_r, mu_k = (sb(n, [P, 1]) for n in (
            "rnn_b", "ffn2_b2", "leak_b", "alpha", "mu_r", "mu_k"))
        conv_w, conv_b = sb("conv_w", [P, HT, 3]), sb("conv_b", [P, HT])
        lstm_bias, ffn2_bias = sb("lstm_bias", [P, P], BF16), sb("ffn2_bias", [P, P], BF16)
        sel_lstm, sel_rows = sb("sel_lstm", [P, 4 * N], BF16), sb("sel_rows", [P, 4 * N], BF16)
        leak, leak_b_half, half_ws2 = sb("leak", [P, 1]), sb("leak_b_half", [P, 1]), sb("half_ws2", [P, 1])
        wsum, wmean, winv = sb("wsum", [P, 4]), sb("wmean", [P, 4]), sb("winv", [P, 4])
        row_mod = sb("row_mod", [P, 1])
        late = {"lstm_wx": lstm_wx, "lstm_wh": lstm_wh, "ffn1_w1": ffn1_w1, "ffn1_w2": ffn1_w2,
                "ffn2_w1": ffn2_w1, "ffn2_w2": ffn2_w2, "rnn_wx": rnn_wx, "rnn_wh": rnn_wh, "leak_wz": leak_wz,
                "leak_wh": leak_wh, "ffn3_wr": ffn3_wr, "ffn3_wk": ffn3_wk, "ffn3_wv": ffn3_wv, "rnn_b": rnn_b,
                "ffn2_b2": ffn2_b2, "leak_b": leak_b, "alpha": alpha, "mu_r": mu_r, "mu_k": mu_k,
                "conv_w": conv_w, "conv_b": conv_b}

        with ExitStack() as layer0:
            def sb0(name, shape, dt=F32):
                return layer0.enter_context(nc.sbuf_tensor(name, shape, dt))

            wr_x, wr_t = sb0("wr_x", [P, E]), sb0("wr_t", [P, E])
            rbias = sb0("rbias", [P, E])
            sw1, sw3 = sb0("sw1", [P, HS_TILES * P]), sb0("sw3", [P, HS_TILES * P])
            sw2 = sb0("sw2", [P, HS_TILES * P])
            rw1, rw2 = sb0("rw1", [P, E * P]), sb0("rw2", [P, E * P])
            gate_w = sb0("gate_w", [P, E])
            w1 = sb0("w1", [P, E, H0])
            w2 = sb0("w2", [P, E, HT, C])
            big = sb0("big", [P, E * N * CAP])
            gate_rows = [big[:, k * CHUNK * E:(k + 1) * CHUNK * E].rearrange("p (i e k) -> p i e k", i=TILES_CHUNK, e=E)
                         for k in range(2)]
            xin = big[:, :].rearrange("p (g e s) -> p g e s", g=GROUPS, e=E)
            ctok = sb0("ctok", [P, NTILE, C])

            x1_flat = x1[:, :, :].rearrange("p t n -> p (t n)")
            w2_raw = x1_flat[:, 2048:2560]
            group_of = x1_flat[:, 2560:3072]
            scratch = x1_flat[:, 3072:3328].rearrange("p (k n) -> p k n", k=2)
            ones = x1_flat[:, 3328:3456]
            part_bf = x1_flat[:, 3456:3520].bitcast(BF16)

            g_dram = nc.dram_tensor("gates_scratch", [NTILE * E, P], F32, kind="Internal").ap()
            v_dram = nc.dram_tensor("topv_scratch", [NTILE, SLOT_TILE], F32, kind="Internal").ap()
            i_dram = nc.dram_tensor("topi_scratch", [NTILE, SLOT_TILE], F32, kind="Internal").ap()

            s_small, s_x = sem("s_small"), [sem(f"s_xin{i}") for i in range(4)]
            s_wmoe, s_wffn, s_sw2 = sem("s_wmoe"), sem("s_wffn"), sem("s_sw2")
            small = [(wr_x[:, :], t["wr_x"]), (wr_t[:, :], t["wr_t"]), (condT[:, :], t["condT"]),
                     (rbias[:, :], t["router_bias"].partition_broadcast(P))]
            for dst, src in small:
                act.dma_start(dst, src).then_inc(s_small, 16)
            for i in range(4):
                sp.dma_start(xT[:, i * 1024:(i + 1) * 1024], t["xT"][:, i * 1024:(i + 1) * 1024]).then_inc(s_x[i], 16)
            act.dma_start(sw2[:, :], t["s_w2T"]).then_inc(s_sw2, 16)
            moe = [(sw1, t["s_w1T"]), (sw3, t["s_w3T"]), (rw1, t["r_w1T"]), (rw2, t["r_w2T"]), (gate_w, t["gate_w"])]
            for dst, src in moe:
                act.dma_start(dst[:, :], src).then_inc(s_wmoe, 16)
            sp.dma_start(w1[:, :, :], t["f_w1"]).then_inc(s_wffn, 16)
            sp.dma_start(w2[:, :, :, :], t["f_w2"]).then_inc(s_wffn, 16)

            s_id = sem("s_id")
            iota_tok = sb0("iota_tok", [P, P])
            part = sb0("part", [P, 1])
            seq_off = sb0("seq_off", [P, 2, SEQ_TILE, CAP])
            pool.memset(ident[:, :], 0.0).then_inc(s_id, 1)
            pool.wait_ge(s_id, val(1))
            pool.affine_select(out=ident[:, :], in_=ident[:, :], compare_op=ALU.not_equal, fill=1.0,
                               base=0, pattern=[[-1, P]], channel_multiplier=1).then_inc(s_id, 1)
            pool.iota(iota_tok[:, :], [[1, P]], base=0, channel_multiplier=0,
                      allow_small_or_imprecise_dtypes=True).then_inc(s_id, 1)
            pool.iota(part[:, :], [[0, 1]], base=0, channel_multiplier=1,
                      allow_small_or_imprecise_dtypes=True).then_inc(s_id, 1)
            pool.iota(seq_off[:, :, :, :], [[0, 2], [T, SEQ_TILE], [0, CAP]], base=0, channel_multiplier=0,
                      allow_small_or_imprecise_dtypes=True).then_inc(s_id, 1)
            ID_READY, CONSTS_READY = 2, 5

            s_w1, s_prep, s_pw = sem("s_w1"), sem("s_prep"), sem("s_pw")
            for name, dst in late.items():
                if name not in ("lstm_b", "ffn2_b1", "ffn1_w2"):
                    sp.dma_start(dst[:, :] if len(dst.shape) == 2 else dst[:, :, :], t[name]).then_inc(s_w1, 16)
            sp.dma_start(w2_raw, t["ffn1_w2"]).then_inc(s_w1, 16)
            n_pool = [0]

            def prep_pool(ins):
                n_pool[0] += 1
                ins.then_inc(s_pw, 1)

            rows_lstm, rows_ffn2 = scratch[:, 0, :], scratch[:, 1, :]
            for r in (rows_lstm, rows_ffn2):
                prep_pool(pool.memset(r, 0.0))
            prep_pool(pool.memset(row_mod[:, :], 99.0))
            prep_pool(pool.iota(group_of, [[1, 4], [0, N]], base=0, channel_multiplier=0,
                                allow_small_or_imprecise_dtypes=True))
            prep_pool(pool.memset(ones[:, :], 1.0))
            pool.wait_ge(s_pw, n_pool[0])
            for k in range(3):
                prep_pool(pool.iota(row_mod[32 * k:32 * k + 32, :], [[0, 1]], base=0, channel_multiplier=1,
                                    allow_small_or_imprecise_dtypes=True))
            sp.wait_ge(s_pw, n_pool[0])
            for k in range(3):
                sp.dma_start(rows_lstm[32 * k:32 * k + 4, :], t["lstm_b"]).then_inc(s_w1, 16)
                sp.dma_start(rows_ffn2[32 * k:32 * k + 4, :], t["ffn2_b1"]).then_inc(s_w1, 16)
            n_late = 16 * (len(late) + 6)

            step_p = [0]

            def dve_p(ins):
                step_p[0] += 1
                ins.then_inc(s_prep, 1)
                dve.wait_ge(s_prep, step_p[0])

            dve.wait_ge(s_w1, n_late)
            dve.wait_ge(s_pw, n_pool[0])
            ternary = [(ffn1_w1[:, :], ffn1_w1[:, :], 1e-5), (w2_raw, ffn1_w2[:, :, :].rearrange("p f c -> p (f c)"), 1e-5),
                       (ffn2_w1[:, :], ffn2_w1[:, :], 1e-8),
                       (ffn2_w2[:, :, :].rearrange("p f c -> p (f c)"), ffn2_w2[:, :, :].rearrange("p f c -> p (f c)"), 1e-8)]
            for k, (w, _, _) in enumerate(ternary):
                dve_p(dve.tensor_reduce(wsum[:, k:k + 1], w, X, ALU.add, apply_absolute_value=True))
            pe.wait_ge(s_prep, step_p[0])
            pe.matmul(bank[7][:, 0:4], ones[:, :], wsum[:, :], start=True, stop=True).then_inc(s_pw, 1)
            dve.wait_ge(s_pw, n_pool[0] + 1)
            for k, (_, _, floor) in enumerate(ternary):
                dve_p(dve.tensor_scalar(wmean[:, k:k + 1], bank[7][:, k:k + 1], 1.0 / (HT * P * P), floor, ALU.mult, ALU.max))
            dve_p(dve.reciprocal(winv[:, :], wmean[:, :]))
            for k, (w, dst, _) in enumerate(ternary):
                dve_p(dve.tensor_scalar(w, w, winv[:, k:k + 1], MAGIC, ALU.mult, ALU.add))
                dve_p(dve.tensor_scalar(w, w, MAGIC, 1.0, ALU.subtract, ALU.min))
                dve_p(dve.tensor_scalar(dst, w, -1.0, None, ALU.max))
            dve_p(dve.tensor_scalar(half_ws2[:, :], wmean[:, 1:2], 0.5, None, ALU.mult))
            dve_p(dve.tensor_scalar(conv_w[:, :, :], conv_w[:, :, :], wmean[:, 0:1], 0.5, ALU.mult, ALU.mult))
            dve_p(dve.tensor_scalar(lstm_wh[:, 0:3 * P], lstm_wh[:, 0:3 * P], 0.5, None, ALU.mult))
            dve_p(dve.tensor_scalar(lstm_wx[:, 3 * P:4 * P], lstm_wx[:, 3 * P:4 * P], 2.0, None, ALU.mult))
            dve_p(dve.tensor_scalar(ffn3_wv[:, :], ffn3_wv[:, :], 0.5, None, ALU.mult))
            dve_p(dve.tensor_scalar(leak_b_half[:, :], leak_b[:, :], 0.5, None, ALU.mult))
            dve_p(dve.tensor_scalar(leak[:, :], alpha[:, :], -1.0, 1.0, ALU.mult, ALU.add))
            dve_p(dve.tensor_scalar(sel_rows[:, :], group_of, row_mod[:, 0:1], None, ALU.is_equal))
            dve_p(dve.tensor_copy(sel_lstm[:, 0:3 * N], sel_rows[:, 0:3 * N]))
            dve_p(dve.tensor_scalar(sel_lstm[:, 3 * N:4 * N], sel_rows[:, 3 * N:4 * N], 2.0, None, ALU.mult))
            for rows, dst in ((rows_lstm, lstm_bias), (rows_ffn2, ffn2_bias)):
                dve_p(dve.tensor_scalar(dst[96:128, :], rows[96:128, :], 1.0, None, ALU.mult))
                dve_p(dve.tensor_copy(part_bf, rows))
                dve_p(dve.tensor_copy(dst[0:32, :], part_bf[0:32, :]))
                dve_p(dve.tensor_tensor(rows, rows, part_bf, ALU.subtract))
                dve_p(dve.tensor_copy(part_bf, rows))
                dve_p(dve.tensor_copy(dst[32:64, :], part_bf[32:64, :]))
                dve_p(dve.tensor_tensor(rows, rows, part_bf, ALU.subtract))
                dve_p(dve.tensor_copy(dst[64:96, :], rows[64:96, :]))

            s_pa, s_aa, s_da, s_ga = sem("s_pa"), sem("s_aa"), sem("s_da"), sem("s_ga")
            logits = bank[0][:, 0:NTILE * E]
            s_cr = sem("s_cr")
            cond_rep = big[:, 0:TOK]
            dve.wait_ge(s_small, val(16 * len(small)))
            dve.tensor_copy(cond_rep.rearrange("p (n k) -> p n k", k=T),
                            condT[:, :].rearrange("p (n o) -> p n o", o=1).to_broadcast([P, N, T])).then_inc(s_cr, 1)
            pe.wait_ge(s_cr, val(1))
            for i in range(NTILE):
                if i % 8 == 0:
                    pe.wait_ge(s_x[i // 8], 16)
                pe.matmul(logits[:, i * E:(i + 1) * E], xT[:, i * P:(i + 1) * P], wr_x[:, :], start=True, stop=False)
                mm = pe.matmul(logits[:, i * E:(i + 1) * E], cond_rep[:, i * P:(i + 1) * P], wr_t[:, :],
                               start=False, stop=True)
            mm.then_inc(s_pa, 1)

            sig = sb0("sig", [P, NTILE, E])
            sel = sb0("sel", [P, NTILE, E])
            cmp = x1_flat[:, 0:NTILE * E * E].rearrange("p (i e f) -> p i e f", i=NTILE, e=E)
            rank = sb0("rank", [P, NTILE, E])
            den, dpos, half_w = sb0("den", [P, NTILE, 1]), sb0("dpos", [P, NTILE, 1]), sb0("half_w", [P, NTILE, 1])
            gates = sb0("gates", [P, NTILE, E])
            gatesT = sb0("gatesT", [P, 2, P])
            all3 = [P, NTILE, E]

            act.wait_ge(s_pa, val(1))
            act.activation(sig[:, :, :].rearrange("p i e -> p (i e)"), logits, ACT.Exp, scale=-1.0).then_inc(s_aa, 1)

            step_a = [0]

            def dve_a(ins):
                step_a[0] += 1
                ins.then_inc(s_da, 1)
                dve.wait_ge(s_da, val(step_a[0]))

            dve.wait_ge(s_aa, val(1))
            dve_a(dve.tensor_scalar(sig[:, :, :], sig[:, :, :], 1.0, None, ALU.add))
            dve_a(dve.reciprocal(sig[:, :, :], sig[:, :, :]))
            dve.wait_ge(s_small, val(16 * len(small)))
            dve_a(dve.tensor_tensor(sel[:, :, :], sig[:, :, :],
                                    rbias[:, :].rearrange("p (o e) -> p o e", o=1).to_broadcast(all3), ALU.add))
            for e in range(E):
                if e:
                    dve.tensor_tensor(cmp[:, :, e, 0:e], sel[:, :, 0:e], sel[:, :, e:e + 1].to_broadcast([P, NTILE, e]),
                                      ALU.is_ge).then_inc(s_da, 1)
                    step_a[0] += 1
                last = dve.tensor_tensor(cmp[:, :, e, e:E], sel[:, :, e:E],
                                         sel[:, :, e:e + 1].to_broadcast([P, NTILE, E - e]), ALU.is_gt)
                if e < E - 1:
                    last.then_inc(s_da, 1)
                    step_a[0] += 1
            dve_a(last)
            dve_a(dve.tensor_reduce(rank[:, :, :], cmp[:, :, :, :], X, ALU.add))
            dve_a(dve.tensor_scalar(rank[:, :, :], rank[:, :, :], 1.5, None, ALU.is_lt))
            dve_a(dve.tensor_tensor(gates[:, :, :], sig[:, :, :], rank[:, :, :], ALU.mult))
            dve_a(dve.tensor_reduce(den[:, :, :], gates[:, :, :], X, ALU.add))
            dve_a(dve.tensor_scalar(dpos[:, :, :], den[:, :, :], 1e-9, 0.25, ALU.is_gt, ALU.mult))
            dve_a(dve.tensor_scalar(den[:, :, :], den[:, :, :], 1e-9, None, ALU.add))
            dve_a(dve.reciprocal(den[:, :, :], den[:, :, :]))
            dve_a(dve.tensor_tensor(den[:, :, :], den[:, :, :], dpos[:, :, :], ALU.mult))
            dve_a(dve.tensor_scalar(half_w[:, :, :], dpos[:, :, :], -0.5, 0.125, ALU.mult, ALU.add))
            dve_a(dve.tensor_tensor(gates[:, :, :], gates[:, :, :], den[:, :, :].to_broadcast(all3), ALU.mult))
            dve_a(dve.tensor_tensor(rank[:, :, :], rank[:, :, :], half_w[:, :, :].to_broadcast(all3), ALU.mult))
            dve_a(dve.tensor_tensor(gates[:, :, :], gates[:, :, :], rank[:, :, :], ALU.add))
            pe.wait_ge(s_da, val(step_a[0]))
            pe.wait_ge(s_id, val(ID_READY))
            gates_flat = gates[:, :, :].rearrange("p i e -> p (i e)")
            for h in range(2):
                pe.transpose(bank[1][:, h * P:(h + 1) * P], gates_flat[:, h * P:(h + 1) * P], ident[:, :]).then_inc(s_pa, 1)
            act.wait_ge(s_pa, val(3))
            act.copy(gatesT[:, :, :].rearrange("p h k -> p (h k)"), bank[1][:, 0:2 * P]).then_inc(s_aa, 1)
            sp.wait_ge(s_aa, val(2))
            for h in range(2):
                sp.dma_start(g_dram[h * P:(h + 1) * P, :], gatesT[:, h, :]).then_inc(s_ga, 16)
            dve.wait_ge(s_sw2, val(16))
            dve.tensor_scalar(sw2[:, :], sw2[:, :], 1.0 / 16.0, None, ALU.mult).then_inc(s_sw2, 1)

            cst = sb0("cst", [P, CHUNK])
            th = [sb0(f"th{k}", [P, CHUNK]) for k in range(2)]
            pb = [sb0(f"pb{k}", [P, CHUNK]) for k in range(2)]
            qb = [sb0(f"qb{k}", [P, CHUNK]) for k in range(2)]
            gl = [sb0(f"gl{k}", [P, CHUNK]) for k in range(2)]
            gg = [sb0(f"gg{k}", [P, CHUNK]) for k in range(2)]
            score = sb0("score", [P, NTILE, E])
            s_ab, s_th, s_p, s_q, s_sh = sem("s_ab"), sem("s_th"), sem("s_p"), sem("s_q"), sem("s_sh")
            s_r, s_gelu, s_gg, s_ro = sem("s_r"), sem("s_gelu"), sem("s_gg"), sem("s_ro")
            s_gr, s_acc, s_tr, s_ct, s_sc, s_sce = ([sem("s_gr0"), sem("s_gr1")], sem("s_acc"), sem("s_tr"), sem("s_ct"),
                                                    sem("s_sc"), sem("s_sce"))
            NSH, NRO = HS_TILES, E
            UNITS = [u for j in range(NSH) for u in (("sh", j), ("ro", 2 * j), ("ro", 2 * j + 1))]
            LEAD = 2
            ab_bank, r_bank, acc_bank = [(bank[0], bank[1]), (bank[2], bank[3])], bank[4:6], bank[6:8]

            def first_products(c, u):
                kind, j = UNITS[u]
                xc = xT[:, ds(c * CHUNK, CHUNK)]
                if kind == "sh":
                    k = c * NSH + j
                    for b, w in zip(ab_bank[j % 2], (sw1, sw3)):
                        if b is ab_bank[j % 2][0] and not (below(c, 1) and j < 2):
                            pe.wait_ge(s_q, val(k - 1))
                        pe.matmul(b[:, :], w[:, j * P:(j + 1) * P], xc, start=True, stop=True).then_inc(s_ab, 1)
                else:
                    k = c * NRO + j
                    if not (below(c, 1) and j < 2):
                        pe.wait_ge(s_gelu, val(k - 1))
                    pe.matmul(r_bank[j % 2][:, :], rw1[:, j * P:(j + 1) * P], xc, start=True, stop=True).then_inc(s_r, 1)

            def second_product(c, par, u):
                kind, j = UNITS[u]
                a = acc_bank[par]
                if kind == "sh":
                    pe.wait_ge(s_q, val(c * NSH + j + 1))
                    if u == 0 and not (below(c, 2)):
                        pe.wait_ge(s_sce, val(c - 1))
                    pe.matmul(a[:, :], sw2[:, j * P:(j + 1) * P], qb[j % 2][:, :], start=(u == 0),
                              stop=False).then_inc(s_sh, 1)
                else:
                    pe.wait_ge(s_gg, val(c * NRO + j + 1))
                    pe.matmul(a[:, :], rw2[:, j * P:(j + 1) * P], gg[j % 2][:, :], start=False,
                              stop=(u == len(UNITS) - 1)).then_inc(s_ro, 1)

            def chunk_transposes(c, par):
                pe.wait_ge(s_acc, val(c + 1))
                for i in range(TILES_CHUNK):
                    mm = pe.transpose(acc_bank[par][:, i * P:(i + 1) * P], cst[:, i * P:(i + 1) * P], ident[:, :])
                mm.then_inc(s_tr, 1)

            def chunk_scores(c, par):
                pe.wait_ge(s_ct, val(c + 1))
                for i in range(TILES_CHUNK):
                    mm = pe.matmul(acc_bank[par][:, i * E:(i + 1) * E], cst[:, i * P:(i + 1) * P], gate_w[:, :],
                                   start=True, stop=True)
                mm.then_inc(s_sc, 1)

            def chunk_evacuate(c, par):
                act.wait_ge(s_ro, val((c + 1) * NRO))
                if not (below(c, 1)):
                    act.wait_ge(s_sc, val(c))
                act.copy(cst[:, :], acc_bank[par][:, :]).then_inc(s_acc, 1)

            def chunk_store_tokens(c, par):
                dve.wait_ge(s_tr, val(c + 1))
                dve.tensor_copy(ctok[:, ds(c * TILES_CHUNK, TILES_CHUNK), :].rearrange("p i k -> p (i k)"),
                                acc_bank[par][:, :]).then_inc(s_ct, 1)

            def chunk_store_scores(c, par):
                dve.wait_ge(s_sc, val(c + 1))
                dve.tensor_copy(score[:, ds(c * TILES_CHUNK, TILES_CHUNK), :].rearrange("p i k -> p (i k)"),
                                acc_bank[par][:, 0:TILES_CHUNK * E]).then_inc(s_sce, 1)

            def load_gate_rows(c, par):
                if not (below(c, 2)):
                    sp.wait_ge(s_gg, val((c - 1) * NRO))
                src = g_dram[ds(c * TILES_CHUNK * E, TILES_CHUNK * E), :].rearrange("r k -> (r k)")
                sp.dma_start(gate_rows[par].rearrange("p i e k -> p (i e k)"),
                             src.partition_broadcast(P)).then_inc(s_gr[par], 16)

            def chunk(c, par, first=False, last=False):
                n = len(UNITS)
                for u in range(n):
                    if u + LEAD < n:
                        first_products(c, u + LEAD)
                    elif not last:
                        first_products(c + 1, u + LEAD - n)
                    second_product(c, par, u)
                    if not first and u == 4:
                        chunk_transposes(c - 1, 1 - par)
                    if not first and u == 7:
                        chunk_scores(c - 1, 1 - par)
                for u, (kind, j) in enumerate(UNITS):
                    if kind == "sh":
                        k = c * NSH + j
                        act.wait_ge(s_ab, val(2 * k + 1))
                        if not (first and j < 2):
                            act.wait_ge(s_p, val(k - 1))
                        act.activation(th[j % 2][:, :], ab_bank[j % 2][0][:, :], ACT.Tanh, scale=0.5).then_inc(s_th, 1)
                    else:
                        k = c * NRO + j
                        act.wait_ge(s_r, val(k + 1))
                        if not (first and j < 2):
                            act.wait_ge(s_gg, val(k - 1))
                        act.activation(gl[j % 2][:, :], r_bank[j % 2][:, :], ACT.Gelu).then_inc(s_gelu, 1)
                    if not first and u == 2:
                        chunk_evacuate(c - 1, 1 - par)
                for u, (kind, j) in enumerate(UNITS):
                    if kind == "sh":
                        k = c * NSH + j
                        dve.wait_ge(s_th, val(k + 1))
                        dve.scalar_tensor_tensor(pb[j % 2][:, :], th[j % 2][:, :], 1.0, ab_bank[j % 2][0][:, :],
                                                 ALU.add, ALU.mult).then_inc(s_p, 1)
                        dve.wait_ge(s_p, val(k + 1))
                        dve.wait_ge(s_ab, val(2 * k + 2))
                        if not (first and j < 2):
                            dve.wait_ge(s_sh, val(k - 1))
                        dve.tensor_tensor(qb[j % 2][:, :], pb[j % 2][:, :], ab_bank[j % 2][1][:, :],
                                          ALU.mult).then_inc(s_q, 1)
                    else:
                        k = c * NRO + j
                        dve.wait_ge(s_gelu, val(k + 1))
                        if j == 0:
                            dve.wait_ge(s_gr[par], val(16 * (turn(c) + 1)))
                        if not (first and j < 2):
                            dve.wait_ge(s_ro, val(k - 1))
                        dve.tensor_tensor(gg[j % 2][:, :].rearrange("p (i k) -> p i k", k=P),
                                          gl[j % 2][:, :].rearrange("p (i k) -> p i k", k=P),
                                          gate_rows[par][:, :, j, :], ALU.mult).then_inc(s_gg, 1)
                    if not first and u == 6:
                        chunk_store_tokens(c - 1, 1 - par)
                    if not first and u == 9:
                        chunk_store_scores(c - 1, 1 - par)
                if not last:
                    load_gate_rows(c + 1, 1 - par)

            pe.wait_ge(s_wmoe, val(16 * len(moe)))
            pe.wait_ge(s_sw2, val(17))
            pe.wait_ge(s_aa, val(2))
            sp.wait_ge(s_ga, val(32))
            load_gate_rows(0, 0)
            for u in range(LEAD):
                first_products(0, u)
            chunk(0, 0, first=True)
            with nc.Fori(0, (NCHUNK - 2) // 2) as i:
                chunk(Lin(i, 2, 1), 1)
                chunk(Lin(i, 2, 2), 0)
            chunk(NCHUNK - 1, 1, last=True)
            chunk_evacuate(NCHUNK - 1, 1)
            chunk_transposes(NCHUNK - 1, 1)
            chunk_store_tokens(NCHUNK - 1, 1)
            chunk_scores(NCHUNK - 1, 1)
            chunk_store_scores(NCHUNK - 1, 1)

            s_dc, s_ac, s_pc, s_vc = sem("s_dc"), sem("s_ac"), sem("s_pc"), sem("s_vc")
            smax, ssum = sb0("smax", [P, NTILE, 1]), sb0("ssum", [P, NTILE, 1])
            probT = sb0("probT", [P, 2, P])
            topv = sb0("topv", [P, 2, SEQ_TILE, CAP])
            topi = sb0("topi", [P, 2, SEQ_TILE, CAP], U32)
            topf = sb0("topf", [P, 2, SEQ_TILE, CAP])
            step_c = [0]

            def dve_c(ins):
                step_c[0] += 1
                ins.then_inc(s_dc, 1)
                dve.wait_ge(s_dc, val(step_c[0]))

            dve.wait_ge(s_sce, val(NCHUNK))
            dve_c(dve.tensor_reduce(smax[:, :, :], score[:, :, :], X, ALU.max))
            dve_c(dve.tensor_tensor(score[:, :, :], score[:, :, :], smax[:, :, :].to_broadcast(all3), ALU.subtract))
            act.wait_ge(s_dc, val(step_c[0]))
            act.activation(sel[:, :, :].rearrange("p i e -> p (i e)"), score[:, :, :].rearrange("p i e -> p (i e)"),
                           ACT.Exp).then_inc(s_ac, 1)
            dve.wait_ge(s_ac, val(1))
            dve_c(dve.tensor_reduce(ssum[:, :, :], sel[:, :, :], X, ALU.add))
            dve_c(dve.reciprocal(ssum[:, :, :], ssum[:, :, :]))
            dve_c(dve.tensor_tensor(sel[:, :, :], sel[:, :, :], ssum[:, :, :].to_broadcast(all3), ALU.mult))
            pe.wait_ge(s_dc, val(step_c[0]))
            prob_flat = sel[:, :, :].rearrange("p i e -> p (i e)")
            for h in range(2):
                mm = pe.transpose(bank[0][:, h * P:(h + 1) * P], prob_flat[:, h * P:(h + 1) * P], ident[:, :])
            mm.then_inc(s_pc, 1)
            dve.wait_ge(s_pc, val(1))
            dve_c(dve.tensor_copy(probT[:, :, :].rearrange("p h k -> p (h k)"), bank[0][:, 0:2 * P]))
            for h in range(2):
                for b in range(SEQ_TILE):
                    seq = probT[:, h, b * T:(b + 1) * T]
                    dve_c(dve.max(topv[:, h, b, :], seq))
                    dve.max_index(topi[:, h, b, :], topv[:, h, b, :], seq).then_inc(s_dc, 1)
                    step_c[0] += 1
            dve.wait_ge(s_dc, val(step_c[0]))
            dve.wait_ge(s_id, val(CONSTS_READY))
            dve_c(dve.tensor_copy(topf[:, :, :, :], topi[:, :, :, :]))
            dve_c(dve.tensor_tensor(topf[:, :, :, :], topf[:, :, :, :], seq_off[:, :, :, :], ALU.add))
            sp.wait_ge(s_dc, val(step_c[0]))
            for dram, src in ((i_dram, topf), (v_dram, topv)):
                rows = dram.rearrange("i (e k) -> (i e) k", e=E)
                for h in range(2):
                    sp.dma_start(rows[h * P:(h + 1) * P, :],
                                 src[:, h, :, :].rearrange("p b j -> p (b j)")).then_inc(s_vc, 16)
            sp.wait_ge(s_vc, val(64))
            slot_rows = [sb0(f"slot_rows{k}", [2 * NTILE, P]) for k in range(2)]
            slot_cols = sb0("slot_cols", [P, 2, 2 * NTILE])
            s_sr = sem("s_sr")
            for k, dram in enumerate((i_dram, v_dram)):
                act.wait_ge(s_vc, val(64))
                act.dma_start(slot_rows[k][:, :], dram.rearrange("i (h k) -> (i h) k", h=2)).then_inc(s_sr, 16)
            pe.wait_ge(s_sr, val(32))
            for k in range(2):
                mm = pe.transpose(bank[4][:, k * 2 * NTILE:(k + 1) * 2 * NTILE], slot_rows[k][:, :],
                                  ident[0:2 * NTILE, 0:2 * NTILE])
            mm.then_inc(s_sr, 1)

            HALF_TILES = 4
            NHALF = NTILE // HALF_TILES
            cgt = [sb0(f"cgt{k}", [P, HALF_TILES, C]) for k in range(2)]
            onehot = [sb0(f"onehot{k}", [P, HALF_TILES * SLOT_TILE]) for k in range(2)]
            s_ld, s_oh, s_ga2, s_gx = [sem("s_ld0"), sem("s_ld1")], sem("s_oh"), sem("s_ga2"), sem("s_gx")
            def gather_loads(k, par):
                if not (below(k, 2)):
                    sp.wait_ge(s_ga2, val(2 * k - 2))
                rows = i_dram[ds(k * HALF_TILES, HALF_TILES), :].rearrange("i s -> (i s)")
                sp.dma_start(onehot[par][:, :], rows.partition_broadcast(P)).then_inc(s_ld[par], 16)
                sp.dma_start(cgt[par][:, :, :], ctok[:, ds(k * HALF_TILES, HALF_TILES), :]).then_inc(s_ld[par], 16)

            def gather_step(g, par):
                k = g * 2 + par
                group_x = big[:, ds(g * (E * SLOT_GE), E * SLOT_GE)].rearrange("p (e k) -> p e k", e=E)
                dve.wait_ge(s_ld[par], val(32 * (g + 1)))
                dve.tensor_scalar(onehot[par][:, :], onehot[par][:, :], part[:, 0:1], None,
                                  ALU.is_equal).then_inc(s_oh, 1)
                pe.wait_ge(s_oh, val(k + 1))
                for b in range(2):
                    dst = bank[2 * par + b]
                    if not below(k, 2):
                        pe.wait_ge(s_gx, val(2 * (k - 2) + b + 1))
                    for i in range(2):
                        tile = 2 * b + i
                        mm = pe.matmul(dst[:, i * SLOT_TILE:(i + 1) * SLOT_TILE], cgt[par][:, tile, :],
                                       onehot[par][:, tile * SLOT_TILE:(tile + 1) * SLOT_TILE],
                                       start=True, stop=True)
                    mm.then_inc(s_ga2, 1)
                    act.wait_ge(s_ga2, val(2 * k + b + 1))
                    for i in range(2):
                        at = (par * HALF_TILES + 2 * b + i) * SLOT_E
                        cp = act.copy(group_x[:, :, at:at + SLOT_E],
                                      dst[:, i * SLOT_TILE:(i + 1) * SLOT_TILE].rearrange("p (e k) -> p e k", e=E))
                    cp.then_inc(s_gx, 1)

            pe.wait_ge(s_sce, val(NCHUNK))
            dve.wait_ge(s_sr, val(33))
            dve.tensor_copy(slot_cols[:, :, :].rearrange("p a b -> p (a b)"), bank[4][:, 0:4 * NTILE]).then_inc(s_sr, 1)
            gather_loads(0, 0)

            def gather_pair(i, last=False):
                gather_loads(i * 2 + 1, 1)
                gather_step(i, 0)
                if not last:
                    gather_loads(i * 2 + 2, 0)
                gather_step(i, 1)

            gather_pair(0)
            with nc.Fori(0, NHALF // 2 - 2) as i:
                gather_pair(Lin(i, 1, 1))
            gather_pair(NHALF // 2 - 1, last=True)

            hb = th + pb
            yT = ctok[:, 0:2 * TILES_GROUP, :].rearrange("p i k -> p (i k)").rearrange(
                "p (i e k) -> p i e k", i=TILES_GROUP, e=E)
            ysl = ctok[:, 2 * TILES_GROUP:4 * TILES_GROUP, :]
            scat = sb0("scat", [P, 2 * TILES_GROUP, P])
            s_h, s_hg, s_y2, s_y, s_ye, s_yt, s_yl, s_st, s_so, s_res = (sem(n) for n in (
                "s_h", "s_hg", "s_y2", "s_y", "s_ye", "s_yt", "s_yl", "s_st", "s_so", "s_res"))
            U2 = 2 * E
            h_bank, y_bank, m_bank = bank[0:4], bank[4:6], bank[6:8]

            def isfirst(g, cond):
                return below(g, 1) and cond

            def expert_up(g, u):
                w = g * U2 + u
                e, b = u // 2, u % 2
                if not isfirst(g, u < 4):
                    pe.wait_ge(s_hg, val(w - 3))
                for i in range(2):
                    ht = 2 * b + i
                    mm = pe.matmul(h_bank[u % 4][:, i * SLOT_GE:(i + 1) * SLOT_GE], w1[:, e, ht * P:(ht + 1) * P],
                                   big[:, ds(g * (E * SLOT_GE) + e * SLOT_GE, SLOT_GE)], start=True, stop=True)
                mm.then_inc(s_h, 1)

            def expert_down(g, u):
                w = g * U2 + u
                e, b = u // 2, u % 2
                pe.wait_ge(s_hg, val(w + 1))
                if b == 0 and not isfirst(g, e < 2):
                    pe.wait_ge(s_ye, val(g * E + e - 1))
                for i in range(2):
                    ht = 2 * b + i
                    mm = pe.matmul(y_bank[e % 2][:, 0:SLOT_GE], w2[:, e, ht, :], hb[u % 4][:, i * SLOT_GE:(i + 1) * SLOT_GE],
                                   start=(ht == 0), stop=(ht == HT - 1))
                mm.then_inc(s_y2, 1)

            def group(g, last=False):
                for u in range(U2):
                    if u + LEAD < U2:
                        expert_up(g, u + LEAD)
                    elif not last:
                        expert_up(g + 1, u + LEAD - U2)
                    expert_down(g, u)
                for u in range(U2):
                    act.wait_ge(s_h, val(g * U2 + u + 1))
                    if not isfirst(g, u < 4):
                        act.wait_ge(s_y2, val(g * U2 + u - 3))
                    act.activation(hb[u % 4][:, :], h_bank[u % 4][:, :], ACT.Gelu).then_inc(s_hg, 1)
                for k in range(2 * TILES_GROUP):
                    if k == 0 and not isfirst(g, True):
                        dve.wait_ge(s_so, val(2 * g))
                    col = g * (2 * TILES_GROUP) + k
                    sc_ap = slot_cols[:, :, :].rearrange("p a b -> p (a b)")
                    last_s = dve.tensor_scalar(scat[:, k, :], iota_tok[:, :], sc_ap[:, ds(col, 1)],
                                               sc_ap[:, ds(col + 2 * NTILE, 1)], ALU.is_equal, ALU.mult)
                    if k % E == E - 1:
                        last_s.then_inc(s_st, 1)
                    if k % 2 == 1:
                        e = k // 2
                        dve.wait_ge(s_y2, val(g * U2 + 2 * e + 2))
                        if e == 0 and not isfirst(g, True):
                            dve.wait_ge(s_yt, val(4 * g))
                        dve.tensor_copy(yT[:, :, e, :], y_bank[e % 2][:, 0:SLOT_GE].rearrange("p (i k) -> p i k", k=SLOT_E)
                                        ).then_inc(s_ye, 1)
                pe.wait_ge(s_ye, val((g + 1) * E))
                yflat = yT[:, :, :, :].rearrange("p i e k -> p (i e k)")
                for b in range(4):
                    m = m_bank[b % 2]
                    if b >= 2:
                        pe.wait_ge(s_yl, val(4 * g + b - 1))
                    elif not isfirst(g, True):
                        pe.wait_ge(s_res, val(2 * g - 1 + b))
                    for i in range(4):
                        mm = pe.transpose(m[:, i * P:(i + 1) * P], yflat[:, (4 * b + i) * P:(4 * b + i + 1) * P], ident[:, :])
                    mm.then_inc(s_yt, 1)
                    act.wait_ge(s_yt, val(4 * g + b + 1))
                    if b == 0 and not isfirst(g, True):
                        act.wait_ge(s_so, val(2 * g))
                    act.copy(ysl[:, 4 * b:4 * b + 4, :].rearrange("p i k -> p (i k)"), m[:, :]).then_inc(s_yl, 1)
                for b in range(2):
                    m = m_bank[b]
                    pe.wait_ge(s_yl, val(4 * g + 4))
                    pe.wait_ge(s_st, val(2 * (g + 1)))
                    for i in range(4):
                        tile = 4 * b + i
                        for h in range(2):
                            mm = pe.matmul(m[:, i * P:(i + 1) * P], ysl[:, 2 * tile + h, :], scat[:, 2 * tile + h, :],
                                           start=(h == 0), stop=(h == 1))
                    mm.then_inc(s_so, 1)
                    dve.wait_ge(s_so, val(2 * g + b + 1))
                    n0 = g * (TILES_GROUP * SEQ_TILE) + b * 16
                    dve.tensor_tensor(x1[:, :, ds(n0, 16)].rearrange("p t n -> p n t"),
                                      xT[:, ds(n0 * T, 16 * T)].rearrange("p (n t) -> p n t", t=T),
                                      m[:, :].rearrange("p (n t) -> p n t", t=T), ALU.add).then_inc(s_res, 1)

            pe.wait_ge(s_wffn, val(32))
            pe.wait_ge(s_gx, val(2 * NHALF))
            pe.wait_ge(s_sr, val(34))
            for u in range(LEAD):
                expert_up(0, u)
            group(0)
            with nc.Fori(0, GROUPS - 2) as i:
                group(Lin(i, 1, 1))
            group(GROUPS - 1, last=True)

        with ExitStack() as layers:
            def sb1(name, shape, dt=F32):
                return layers.enter_context(nc.sbuf_tensor(name, shape, dt))

            sems = {}

            def done(ins, stage):
                if stage not in sems:
                    sems[stage] = sem("t_" + stage)
                return ins.then_inc(sems[stage], 1)

            def need(eng, stage, step):
                if isinstance(step, int):
                    if step < 0:
                        return
                    step = min(step, T - 1)
                if stage not in sems:
                    sems[stage] = sem("t_" + stage)
                eng.wait_ge(sems[stage], val(step + 1))

            HU, HS_BUF = HT * P, [P, HT * P]
            tg, tc = sb1("tg", [P, 4, N]), sb1("tc", [P, N])
            lp, lq, cell, hL = sb1("lp", [P, N]), sb1("lq", [P, N]), sb1("cell", [P, N]), sb1("hL", [P, N])
            mx1, m1, sc1 = sb1("mx1", [P, 1]), sb1("m1", [P, 1]), sb1("sc1", [P, 1])
            mx2, m2, sc2 = sb1("mx2", [P, 1]), sb1("m2", [P, 1]), sb1("sc2", [P, 1])
            v1, xq, xqT = sb1("v1", [P, N]), sb1("xq", [P, N]), sb1("xqT", [P, N])
            u_sb, z_conv, y_part, y_full = (sb1(n, [P, HT, N]) for n in ("u_sb", "z_conv", "y_part", "y_full"))
            th1, hs = sb1("th_ffn1", [P, HT, N]), sb1("hs", [P, HT, N])
            v2 = sb1("v2", [P, HT * P])
            q2T = sb1("q2T", [P, HT, N], BF16)
            ys = sb1("ys", [P, C])
            h2 = sb1("h2", [P, N])
            g2 = sb1("g2", [P, HT, N])
            g3, p3, pre3, h3, h3_prev = (sb1(n, [P, N]) for n in ("g3", "p3", "pre3", "h3", "h3_prev"))
            leaked, z_half, diff = (sb1(n, [P, N]) for n in ("leaked", "z_half", "diff"))
            xr, xk, tr, kr, kk, o1 = (sb1(n, [P, N]) for n in ("xr", "xk", "tr", "kr", "kk", "o1"))
            z_mul, conv_w0, conv_b_full = (sb1(n, [P, HT, N]) for n in ("z_mul", "conv_w0", "conv_b_full"))
            magic, halves, leak_full = sb1("magic", [P, 1]), sb1("halves", [P, N]), sb1("leak_full", [P, N])

            s_i2, STATES = sem("s_i2"), 10
            pool.wait_ge(s_res, 2 * GROUPS)
            pool.memset(cell[:, :], 0.0).then_inc(s_i2, 1)
            pool.memset(magic[:, :], MAGIC).then_inc(s_i2, 1)
            pool.memset(halves[:, :], 0.5).then_inc(s_i2, 1)
            pool.memset(h3_prev[:, :], 0.0).then_inc(s_i2, 1)
            dve.tensor_scalar(hL[:, :], condT[:, :], 2.0, None, ALU.mult).then_inc(s_i2, 1)
            dve.tensor_copy(h2[:, :], condT[:, :]).then_inc(s_i2, 1)
            dve.tensor_copy(conv_w0[:, :, :], conv_w[:, :, 0:1].to_broadcast([P, HT, N])).then_inc(s_i2, 1)
            dve.tensor_copy(conv_b_full[:, :, :],
                            conv_b[:, :].rearrange("p (f o) -> p f o", o=1).to_broadcast([P, HT, N])).then_inc(s_i2, 1)
            dve.tensor_copy(leak_full[:, :], leak[:, 0:1].to_broadcast([P, N])).then_inc(s_i2, 1)
            dve.tensor_copy(h3[:, :], condT[:, :]).then_inc(s_i2, 1)
            for eng in (pe, act, dve, pool):
                eng.wait_ge(s_i2, STATES)
                eng.wait_ge(s_res, 2 * GROUPS)

            B_GATE, B_U, B_V, B_F2, B_TR, B_R2, B_R3 = bank[0:7]

            def x_at(step):
                return x1[:, ds(step, 1), :].rearrange("p o n -> p (o n)")

            def live(step):
                return not isinstance(step, int) or 0 <= step < T

            def gates_from_x(t):
                need(pe, "tg", t - 1)
                pe.matmul(B_GATE[:, :], lstm_bias[:, :], sel_lstm[:, :], start=True, stop=False, skip_group_check=True)
                for q in range(4):
                    mm = pe.matmul(B_GATE[:, q * N:(q + 1) * N], lstm_wx[:, q * P:(q + 1) * P], x_at(t),
                                   start=False, stop=False, skip_group_check=True)
                return mm

            def iteration(i):
                lag = lambda n: i - n
                t = lag(0)
                if live(t):
                    need(pe, "hL", t - 1)
                    for q in range(4):
                        mm = pe.matmul(B_GATE[:, q * N:(q + 1) * N], lstm_wh[:, q * P:(q + 1) * P], hL[:, :],
                                       start=False, stop=True, skip_group_check=True)
                    done(mm, "gates")
                t = lag(1)
                if live(t):
                    need(pe, "hL", t)
                    need(pe, "x2", t - 3)
                    done(pe.transpose(B_TR[:, 0:P], hL[:, :], ident[:, :]), "tr1")
                t = lag(0)
                if live(t):
                    need(act, "gates", t)
                    need(act, "hL", t - 1)
                    done(act.activation(tg[:, :, :].rearrange("p q n -> p (q n)"), B_GATE[:, :], ACT.Tanh, scale=0.5), "tg")
                t = lag(1)
                if live(t):
                    need(dve, "tr1", t)
                    need(dve, "m1", t - 1)
                    done(dve.tensor_reduce(mx1[:, :], B_TR[:, 0:P], X, ALU.max, apply_absolute_value=True), "mx1")
                    need(dve, "mx1", t)
                    need(dve, "xq", t - 1)
                    done(dve.tensor_scalar(m1[:, :], mx1[:, :], 2e-5, 1.0 / 127.0, ALU.max, ALU.mult), "m1")
                    need(dve, "m1", t)
                    need(dve, "v1", t - 1)
                    done(dve.reciprocal(sc1[:, :], m1[:, :]), "sc1")
                    need(act, "sc1", t)
                    need(act, "xq", t - 1)
                    done(act.activation(v1[:, :], B_TR[:, 0:P], ACT.Identity, bias=magic[:, 0:1], scale=sc1[:, 0:1]), "v1")
                t = lag(8)
                if live(t):
                    need(pe, "kk", t)
                    need(pe, "tr", t)
                    done(pe.matmul(B_R3[:, 0:N], ffn3_wv[:, :], kk[:, :], start=True, stop=True), "v")
                t = lag(3)
                if live(t):
                    need(pe, "hs", t)
                    need(pe, "q2T", t - 1)
                    for f in range(HT):
                        mm = pe.transpose(B_V[:, f * P:(f + 1) * P], hs[:, f, :], ident[:, :])
                    done(mm, "V")
                t = lag(5)
                if live(t):
                    need(pe, "h2", t)
                    need(pe, "g2", t - 1)
                    pe.matmul(B_F2[:, :], ffn2_bias[:, :], sel_rows[:, :], start=True, stop=False, skip_group_check=True)
                    for f in range(HT):
                        mm = pe.matmul(B_F2[:, f * N:(f + 1) * N], ffn2_w1[:, f * P:(f + 1) * P], h2[:, :],
                                       start=False, stop=True, skip_group_check=True)
                    done(mm, "F2up")
                t = lag(1)
                if live(t):
                    need(dve, "v1", t)
                    need(dve, "tr2", t - 1)
                    done(dve.tensor_scalar(xq[:, :], v1[:, :], MAGIC, m1[:, 0:1], ALU.subtract, ALU.mult), "xq")
                t = lag(0)
                if live(t):
                    need(dve, "tg", t)
                    need(dve, "cell", t - 1)
                    done(dve.scalar_tensor_tensor(lp[:, :], tg[:, 1, :], 1.0, cell[:, :], ALU.add, ALU.mult), "lp")
                    done(dve.scalar_tensor_tensor(lq[:, :], tg[:, 0, :], 1.0, tg[:, 3, :], ALU.add, ALU.mult), "lq")
                    need(dve, "lp", t)
                    need(dve, "lq", t)
                    need(dve, "tc", t - 1)
                    done(dve.scalar_tensor_tensor(cell[:, :], lp[:, :], 0.5, lq[:, :], ALU.mult, ALU.add), "cell")
                t = lag(1)
                if live(t):
                    need(pe, "xq", t)
                    done(pe.transpose(B_TR[:, P:2 * P], xq[:, :], ident[:, :]), "tr2")
                    need(act, "tr2", t)
                    need(act, "u", t - 1)
                    done(act.copy(xqT[:, :], B_TR[:, P:2 * P]), "xqT")
                t = lag(0)
                if live(t):
                    need(act, "cell", t)
                    need(act, "hL", t - 1)
                    done(act.activation(tc[:, :], cell[:, :], ACT.Tanh, scale=0.5), "tc")
                t = lag(3)
                if live(t):
                    need(dve, "V", t)
                    need(dve, "m2", t - 1)
                    done(dve.tensor_reduce(mx2[:, :], B_V[:, :], X, ALU.max, apply_absolute_value=True), "mx2")
                    need(dve, "mx2", t)
                    need(dve, "ys", t - 1)
                    done(dve.tensor_scalar(m2[:, :], mx2[:, :], 2e-5, 1.0 / 127.0, ALU.max, ALU.mult), "m2")
                    need(dve, "m2", t)
                    need(dve, "v2", t - 1)
                    done(dve.reciprocal(sc2[:, :], m2[:, :]), "sc2")
                t = lag(0)
                if live(t):
                    need(dve, "tc", t)
                    need(dve, "tr1", t - 1)
                    need(dve, "gates", t)
                    done(dve.scalar_tensor_tensor(hL[:, :], tg[:, 2, :], 1.0, tc[:, :], ALU.add, ALU.mult), "hL")
                t = lag(3)
                if live(t):
                    need(act, "sc2", t)
                    need(act, "V2", t - 1)
                    done(act.activation(v2[:, :], B_V[:, :], ACT.Identity, bias=magic[:, 0:1], scale=sc2[:, 0:1]), "v2")
                if live(i) and not (isinstance(i, int) and i == T - 1):
                    done(gates_from_x(i + 1), "gx")
                t = lag(1)
                if live(t):
                    need(pe, "xqT", t)
                    need(pe, "u_sb", t - 1)
                    for f in range(HT):
                        mm = pe.matmul(B_U[:, f * N:(f + 1) * N], ffn1_w1[:, f * P:(f + 1) * P], xqT[:, :],
                                       start=True, stop=True)
                    done(mm, "u")
                t = lag(8)
                if live(t):
                    need(dve, "v", t)
                    need(dve, "out", t - 1)
                    done(dve.scalar_tensor_tensor(o1[:, :], tr[:, :], 1.0, B_R3[:, 0:N], ALU.add, ALU.mult), "o1")
                    pool.wait_ge(s_i2, STATES)
                    need(pool, "o1", t)
                    done(pool.tensor_tensor(x_at(t), x_at(t), o1[:, :], ALU.add), "out")
                    need(sp, "out", t)
                    sp.dma_start(out[:, ds(t, 1), :], x1[:, ds(t, 1), :]).then_inc(s_out, 16)
                t = lag(5)
                if live(t):
                    need(act, "F2up", t)
                    need(act, "F2down", t - 1)
                    done(act.activation(g2[:, :, :].rearrange("p f n -> p (f n)"), B_F2[:, :], ACT.Gelu), "g2")
                t = lag(7)
                if live(t):
                    pool.wait_ge(s_i2, STATES)
                    need(pool, "h3", t)
                    need(pool, "xk", t - 1)
                    need(pool, "h3_prev", t - 1)
                    done(pool.tensor_tensor(diff[:, :], h3[:, :], h3_prev[:, :], ALU.subtract), "diff")
                    need(dve, "diff", t)
                    need(dve, "rk", t - 1)
                    done(dve.scalar_tensor_tensor(xr[:, :], diff[:, :], mu_r[:, 0:1], h3_prev[:, :], ALU.mult, ALU.add), "xr")
                    done(dve.scalar_tensor_tensor(xk[:, :], diff[:, :], mu_k[:, 0:1], h3_prev[:, :], ALU.mult, ALU.add), "xk")
                    pool.wait_ge(s_i2, STATES)
                    need(pool, "xk", t)
                    done(pool.tensor_copy(h3_prev[:, :], h3[:, :]), "h3_prev")
                t = lag(6)
                if live(t):
                    pool.wait_ge(s_i2, STATES)
                    need(pool, "h3", t - 1)
                    need(pool, "pre3", t - 1)
                    need(pool, "x3", t)
                    done(pool.tensor_tensor(leaked[:, :], h3[:, :], leak_full[:, :], ALU.mult), "leaked")
                    done(pool.tensor_tensor(z_half[:, :], x_at(t), halves[:, :], ALU.mult), "z_half")
                t = lag(3)
                if live(t):
                    need(pe, "v2", t)
                    for f in range(HT):
                        mm = pe.transpose(B_V[:, f * P:(f + 1) * P], v2[:, f * P:(f + 1) * P], ident[:, :])
                    done(mm, "V2")
                t = lag(4)
                if live(t):
                    need(pe, "x2", t)
                    need(pe, "h2", t - 1)
                    need(pe, "x3", t - 2)
                    pe.matmul(B_R2[:, 0:N], rnn_wx[:, :], x_at(t), start=True, stop=False)
                    done(pe.matmul(B_R2[:, 0:N], rnn_wh[:, :], h2[:, :], start=False, stop=True), "r2")
                t = lag(1)
                if live(t):
                    need(act, "u", t)
                    need(act, "y_part", t - 1)
                    need(act, "z_conv", t - 1)
                    done(act.copy(u_sb[:, :, :].rearrange("p f n -> p (f n)"), B_U[:, :]), "u_sb")
                t = lag(4)
                if live(t):
                    need(act, "r2", t)
                    need(act, "F2up", t - 1)
                    done(act.activation(h2[:, :], B_R2[:, 0:N], ACT.Tanh, bias=rnn_b[:, 0:1]), "h2")
                t = lag(3)
                if live(t):
                    need(dve, "V2", t)
                    need(dve, "y", t - 1)
                    done(dve.tensor_scalar(q2T[:, :, :].rearrange("p f n -> p (f n)"), B_V[:, :], MAGIC, 127.0,
                                           ALU.subtract, ALU.min), "q2T")
                t = lag(6)
                if live(t):
                    need(pe, "h3", t - 1)
                    need(pe, "x3", t)
                    need(pe, "o1", t - 2)
                    pe.matmul(B_R3[:, 0:N], leak_wz[:, :], x_at(t), start=True, stop=False)
                    done(pe.matmul(B_R3[:, 0:N], leak_wh[:, :], h3[:, :], start=False, stop=True), "r3")
                    need(act, "r3", t)
                    need(act, "p3", t - 1)
                    done(act.activation(g3[:, :], B_R3[:, 0:N], ACT.Tanh, bias=leak_b_half[:, 0:1], scale=0.5), "g3")
                t = lag(1)
                if live(t):
                    need(dve, "u_sb", t)
                    if not (isinstance(t, int) and t == 0):
                        need(dve, "hs", t - 2)
                        need(dve, "y_part", t - 1)
                        for f in range(HT):
                            op = dve.scalar_tensor_tensor(y_full[:, f, :], u_sb[:, f, :], conv_w[:, f, 2:3],
                                                          y_part[:, f, :], ALU.mult, ALU.add)
                        done(op, "y_full")
                    need(dve, "z_conv", t - 1)
                    need(dve, "y_full", t - 1)
                    for f in range(HT):
                        if isinstance(t, int) and t == 0:
                            op = dve.tensor_scalar(y_part[:, f, :], u_sb[:, f, :], conv_w[:, f, 1:2], conv_b[:, f:f + 1],
                                                   ALU.mult, ALU.add)
                        else:
                            op = dve.scalar_tensor_tensor(y_part[:, f, :], u_sb[:, f, :], conv_w[:, f, 1:2],
                                                          z_conv[:, f, :], ALU.mult, ALU.add)
                    done(op, "y_part")
                    pool.wait_ge(s_i2, STATES)
                    need(pool, "y_part", t)
                    done(pool.tensor_tensor(z_mul[:, :, :], u_sb[:, :, :], conv_w0[:, :, :], ALU.mult), "z_mul")
                    need(pool, "z_mul", t)
                    done(pool.tensor_tensor(z_conv[:, :, :], z_mul[:, :, :], conv_b_full[:, :, :], ALU.add), "z_conv")
                t = lag(2)
                if isinstance(t, int) and t == T - 1:
                    need(dve, "hs", t - 1)
                    need(dve, "y_part", t)
                    done(dve.tensor_copy(y_full[:, :, :], y_part[:, :, :]), "y_full")
                t = lag(5)
                if live(t):
                    need(pe, "g2", t)
                    need(pe, "h2", t + 1)
                    for f in range(HT):
                        mm = pe.matmul(B_R2[:, N:2 * N], ffn2_w2[:, f, :], g2[:, f, :], start=(f == 0), stop=(f == HT - 1))
                    done(mm, "F2down")
                t = lag(6)
                if live(t):
                    need(dve, "g3", t)
                    need(dve, "z_half", t)
                    need(dve, "pre3", t - 1)
                    done(dve.scalar_tensor_tensor(p3[:, :], g3[:, :], 1.0, z_half[:, :], ALU.add, ALU.mult), "p3")
                    need(dve, "p3", t)
                    need(dve, "h3", t - 1)
                    done(dve.tensor_tensor(pre3[:, :], p3[:, :], leaked[:, :], ALU.add), "pre3")
                    need(act, "pre3", t)
                    need(act, "h3_prev", t - 1)
                    done(act.activation(h3[:, :], pre3[:, :], ACT.Tanh), "h3")
                t = lag(3)
                if live(t):
                    need(pe, "q2T", t)
                    need(pe, "xqT", t + 2)
                    for f in range(HT):
                        mm = pe.matmul(B_TR[:, 2 * P:3 * P], q2T[:, f, :], ffn1_w2[:, f, :], start=(f == 0), stop=(f == HT - 1))
                    done(mm, "y")
                    need(dve, "y", t)
                    need(dve, "ysT", t - 1)
                    done(dve.tensor_scalar(ys[:, :], B_TR[:, 2 * P:3 * P], m2[:, 0:1], half_ws2[:, 0:1], ALU.mult, ALU.mult), "ys")
                t = lag(5)
                if live(t):
                    need(dve, "F2down", t)
                    done(dve.scalar_tensor_tensor(x_at(t), B_R2[:, N:2 * N], ffn2_b2[:, 0:1], x_at(t), ALU.add, ALU.add), "x3")
                t = lag(7)
                if live(t):
                    need(pe, "xk", t)
                    need(pe, "g3", t + 1)
                    pe.matmul(B_R3[:, N:2 * N], ffn3_wr[:, :], xr[:, :], start=True, stop=True)
                    done(pe.matmul(B_R3[:, 2 * N:3 * N], ffn3_wk[:, :], xk[:, :], start=True, stop=True), "rk")
                    need(dve, "rk", t)
                    need(dve, "kk", t - 1)
                    done(dve.tensor_scalar(kr[:, :], B_R3[:, 2 * N:3 * N], 0.0, None, ALU.max), "kr")
                    need(act, "kr", t)
                    need(act, "o1", t - 1)
                    done(act.activation(tr[:, :], B_R3[:, N:2 * N], ACT.Tanh, scale=0.5), "tr")
                    pool.wait_ge(s_i2, STATES)
                    need(pool, "kr", t)
                    need(pool, "v", t - 1)
                    done(pool.tensor_tensor(kk[:, :], kr[:, :], kr[:, :], ALU.mult), "kk")
                t = lag(3)
                if live(t):
                    need(pe, "ys", t)
                    done(pe.transpose(B_TR[:, 3 * P:4 * P], ys[:, :], ident[:, :]), "ysT")
                    need(dve, "ysT", t)
                    done(dve.tensor_tensor(x_at(t), x_at(t), B_TR[:, 3 * P:4 * P], ALU.add), "x2")
                t = lag(2)
                if live(t):
                    need(act, "y_full", t)
                    need(act, "hs", t - 1)
                    done(act.activation(th1[:, :, :], y_full[:, :, :], ACT.Tanh, scale=0.5), "th1")
                    need(dve, "th1", t)
                    need(dve, "V", t - 1)
                    done(dve.scalar_tensor_tensor(hs[:, :, :], th1[:, :, :], 1.0, y_full[:, :, :], ALU.add, ALU.mult), "hs")

            FIRST, LAST_LAG = 10, 8
            s_out = sem("s_out")
            done(gates_from_x(0), "gx")
            for i in range(FIRST):
                iteration(i)
            with nc.Fori(0, T - 1 - FIRST) as j:
                iteration(Lin(j, 1, FIRST))
            for i in range(T - 1, T + LAST_LAG):
                iteration(i)
            sp.wait_ge(s_out, 16 * T)


def kernel(**inputs):
    import numpy as np
    import concourse.bacc as bacc
    from concourse.bass_utils import run_bass_kernel_spmd

    i = {k: np.asarray(v) for k, v in inputs.items()}
    wr = i["L0_cond_W_router"]
    arrays = {
        "xT": i["x"].transpose(2, 0, 1).reshape(C, TOK),
        "condT": i["cond_1024"].T,
        "wr_x": wr[:, :C].T,
        "wr_t": wr[:, C:].T,
        "router_bias": i["L0_cond_router_bias"],
        "s_w1T": i["L0_cond_s_w1"].reshape(-1, C).T,
        "s_w3T": i["L0_cond_s_w3"].reshape(-1, C).T,
        "s_w2T": i["L0_cond_s_w2"].transpose(0, 2, 1).reshape(HS_TILES, P, C).transpose(1, 0, 2).reshape(P, -1),
        "r_w1T": i["L0_cond_r_w1"].reshape(-1, C).T,
        "r_w2T": i["L0_cond_r_w2"].transpose(2, 0, 1).reshape(P, -1),
        "gate_w": i["L0_ffn_gate_w"],
        "f_w1": i["L0_ffn_w1"].transpose(1, 0, 2),
        "f_w2": i["L0_ffn_w2"].reshape(E, HT, P, C).transpose(2, 0, 1, 3),
    }
    lw, cw = i["L3_cond_W"], i["L1_ffn_conv_w"]

    def column(a):
        return a.reshape(-1, P).T

    def hidden_rows(a):
        return a.T.reshape(HT, P, C).transpose(1, 0, 2)

    arrays.update({
        "lstm_wx": i["L1_cond_Wx"], "lstm_wh": i["L1_cond_Wh"], "lstm_b": i["L1_cond_b"].reshape(4, P),
        "ffn1_w1": i["L1_ffn_w1"].T, "ffn1_w2": hidden_rows(i["L1_ffn_w2"]).reshape(P, -1),
        "conv_w": cw.reshape(HT, P, 3).transpose(1, 0, 2), "conv_b": column(i["L1_ffn_conv_b"]),
        "rnn_wx": i["L2_cond_Wx"], "rnn_wh": i["L2_cond_Wh"], "rnn_b": column(i["L2_cond_b"]),
        "ffn2_w1": i["L2_ffn_W1"].T, "ffn2_b1": i["L2_ffn_b1"].reshape(HT, P),
        "ffn2_w2": hidden_rows(i["L2_ffn_W2"]), "ffn2_b2": column(i["L2_ffn_b2"]),
        "leak_wh": lw[:, :C].T, "leak_wz": lw[:, C:].T, "leak_b": column(i["L3_cond_b"]),
        "alpha": column(i["L3_cond_alpha"]),
        "ffn3_wr": i["L3_ffn_W_r"].T, "ffn3_wk": i["L3_ffn_W_k"].T, "ffn3_wv": i["L3_ffn_W_v"].T,
        "mu_r": column(i["L3_ffn_mu_r"]), "mu_k": column(i["L3_ffn_mu_k"]),
    })
    arrays = {k: np.ascontiguousarray(a) for k, a in arrays.items()}
    nc = bacc.Bacc("TRN2", target_bir_lowering=False, num_devices=1)
    aps = {k: nc.dram_tensor("in_" + k, a.shape, mybir.dt.from_np(a.dtype), kind="ExternalInput").ap() for k, a in arrays.items()}
    out = nc.dram_tensor("outT", (C, T, N), F32, kind="ExternalOutput").ap()
    build_program(nc, aps, out)
    r = run_bass_kernel_spmd(nc, [{"in_" + k: a for k, a in arrays.items()}], core_ids=[0])
    return np.ascontiguousarray(r.results[0]["outT"].transpose(2, 1, 0))
```

```python
from contextlib import ExitStack

import concourse.bass as bass
from concourse import mybir

F32 = mybir.dt.float32
BF16 = mybir.dt.bfloat16
U32 = mybir.dt.uint32
ALU = mybir.AluOpType
ACT = mybir.ActivationFunctionType
X = mybir.AxisListType.X

N, T, C = 128, 32, 128
P = 128
TOK = N * T
NTILE = TOK // P
SEQ_TILE = P // T
E = 8
BANK = 512

HS_TILES = 4
CHUNK = 512
NCHUNK = TOK // CHUNK
TILES_CHUNK = CHUNK // P

CAP = 2 * T // E
H0 = 512
HT = H0 // P
SLOT_TILE = SEQ_TILE * E * CAP
SLOT_E = SEQ_TILE * CAP
GROUPS = 4
TILES_GROUP = NTILE // GROUPS
SLOT_GE = TILES_GROUP * SLOT_E

MAGIC = 1.5 * 2.0 ** 23


class Lin:

    def __init__(self, i, a, b):
        self.i, self.a, self.b = i, a, b

    def __add__(self, n):
        return Lin(self.i, self.a, self.b + n)

    def __sub__(self, n):
        return Lin(self.i, self.a, self.b - n)

    def __mul__(self, n):
        return Lin(self.i, self.a * n, self.b * n)

    __radd__, __rmul__ = __add__, __mul__


def val(x):
    return x.i * x.a + x.b if isinstance(x, Lin) else x


def below(x, n):
    return isinstance(x, int) and x < n


def turn(x):
    return Lin(x.i, x.a // 2, x.b // 2) if isinstance(x, Lin) else x // 2


def ds(start, size):
    return bass.ds(val(start), size)


def build_program(nc, t, out):
    ctx = ExitStack()

    def sb(name, shape, dt=F32):
        return ctx.enter_context(nc.sbuf_tensor(name, shape, dt))

    def sem(name):
        return ctx.enter_context(nc.semaphore(name))

    with ctx:
        pe, act, dve, pool, sp = nc.tensor, nc.scalar, nc.vector, nc.gpsimd, nc.sync
        bank = [ctx.enter_context(nc.psum_tensor(f"bank{i}", [P, BANK], F32)) for i in range(8)]

        xT = sb("xT", [P, TOK])
        x1 = sb("x1", [P, T, N])
        condT = sb("condT", [P, N])
        ident = sb("ident", [P, P])

        lstm_wx, lstm_wh = sb("lstm_wx", [P, 4 * P]), sb("lstm_wh", [P, 4 * P])
        ffn1_w1, ffn1_w2 = sb("ffn1_w1", [P, HT * P]), sb("ffn1_w2", [P, HT, C], BF16)
        ffn2_w1, ffn2_w2 = sb("ffn2_w1", [P, HT * P]), sb("ffn2_w2", [P, HT, C])
        rnn_wx, rnn_wh, leak_wz, leak_wh, ffn3_wr, ffn3_wk, ffn3_wv = (sb(n, [P, P]) for n in (
            "rnn_wx", "rnn_wh", "leak_wz", "leak_wh", "ffn3_wr", "ffn3_wk", "ffn3_wv"))
        rnn_b, ffn2_b2, leak_b, alpha, mu_r, mu_k = (sb(n, [P, 1]) for n in (
            "rnn_b", "ffn2_b2", "leak_b", "alpha", "mu_r", "mu_k"))
        conv_w, conv_b = sb("conv_w", [P, HT, 3]), sb("conv_b", [P, HT])
        lstm_bias, ffn2_bias = sb("lstm_bias", [P, P], BF16), sb("ffn2_bias", [P, P], BF16)
        sel_lstm, sel_rows = sb("sel_lstm", [P, 4 * N], BF16), sb("sel_rows", [P, 4 * N], BF16)
        leak, leak_b_half, half_ws2 = sb("leak", [P, 1]), sb("leak_b_half", [P, 1]), sb("half_ws2", [P, 1])
        wsum, wmean, winv = sb("wsum", [P, 4]), sb("wmean", [P, 4]), sb("winv", [P, 4])
        row_mod = sb("row_mod", [P, 1])
        late = {"lstm_wx": lstm_wx, "lstm_wh": lstm_wh, "ffn1_w1": ffn1_w1, "ffn1_w2": ffn1_w2,
                "ffn2_w1": ffn2_w1, "ffn2_w2": ffn2_w2, "rnn_wx": rnn_wx, "rnn_wh": rnn_wh, "leak_wz": leak_wz,
                "leak_wh": leak_wh, "ffn3_wr": ffn3_wr, "ffn3_wk": ffn3_wk, "ffn3_wv": ffn3_wv, "rnn_b": rnn_b,
                "ffn2_b2": ffn2_b2, "leak_b": leak_b, "alpha": alpha, "mu_r": mu_r, "mu_k": mu_k,
                "conv_w": conv_w, "conv_b": conv_b}

        with ExitStack() as layer0:
            def sb0(name, shape, dt=F32):
                return layer0.enter_context(nc.sbuf_tensor(name, shape, dt))

            wr_x, wr_t = sb0("wr_x", [P, E]), sb0("wr_t", [P, E])
            rbias = sb0("rbias", [P, E])
            sw1, sw3 = sb0("sw1", [P, HS_TILES * P]), sb0("sw3", [P, HS_TILES * P])
            sw2 = sb0("sw2", [P, HS_TILES * P])
            rw1, rw2 = sb0("rw1", [P, E * P]), sb0("rw2", [P, E * P])
            gate_w = sb0("gate_w", [P, E])
            w1 = sb0("w1", [P, E, H0])
            w2 = sb0("w2", [P, E, HT, C])
            big = sb0("big", [P, E * N * CAP])
            gate_rows = [big[:, k * CHUNK * E:(k + 1) * CHUNK * E].rearrange("p (i e k) -> p i e k", i=TILES_CHUNK, e=E)
                         for k in range(2)]
            xin = big[:, :].rearrange("p (g e s) -> p g e s", g=GROUPS, e=E)
            ctok = sb0("ctok", [P, NTILE, C])

            x1_flat = x1[:, :, :].rearrange("p t n -> p (t n)")
            w2_raw = x1_flat[:, 2048:2560]
            group_of = x1_flat[:, 2560:3072]
            scratch = x1_flat[:, 3072:3328].rearrange("p (k n) -> p k n", k=2)
            ones = x1_flat[:, 3328:3456]
            part_bf = x1_flat[:, 3456:3520].bitcast(BF16)

            g_dram = nc.dram_tensor("gates_scratch", [NTILE * E, P], F32, kind="Internal").ap()
            v_dram = nc.dram_tensor("topv_scratch", [NTILE, SLOT_TILE], F32, kind="Internal").ap()
            i_dram = nc.dram_tensor("topi_scratch", [NTILE, SLOT_TILE], F32, kind="Internal").ap()

            s_small, s_x = sem("s_small"), [sem(f"s_xin{i}") for i in range(4)]
            s_wmoe, s_wffn, s_sw2 = sem("s_wmoe"), sem("s_wffn"), sem("s_sw2")
            small = [(wr_x[:, :], t["wr_x"]), (wr_t[:, :], t["wr_t"]), (condT[:, :], t["condT"]),
                     (rbias[:, :], t["router_bias"].partition_broadcast(P))]
            for dst, src in small:
                act.dma_start(dst, src).then_inc(s_small, 16)
            for i in range(4):
                sp.dma_start(xT[:, i * 1024:(i + 1) * 1024], t["xT"][:, i * 1024:(i + 1) * 1024]).then_inc(s_x[i], 16)
            act.dma_start(sw2[:, :], t["s_w2T"]).then_inc(s_sw2, 16)
            moe = [(sw1, t["s_w1T"]), (sw3, t["s_w3T"]), (rw1, t["r_w1T"]), (rw2, t["r_w2T"]), (gate_w, t["gate_w"])]
            for dst, src in moe:
                act.dma_start(dst[:, :], src).then_inc(s_wmoe, 16)
            sp.dma_start(w1[:, :, :], t["f_w1"]).then_inc(s_wffn, 16)
            sp.dma_start(w2[:, :, :, :], t["f_w2"]).then_inc(s_wffn, 16)

            s_id = sem("s_id")
            iota_tok = sb0("iota_tok", [P, P])
            part = sb0("part", [P, 1])
            seq_off = sb0("seq_off", [P, 2, SEQ_TILE, CAP])
            pool.memset(ident[:, :], 0.0).then_inc(s_id, 1)
            pool.wait_ge(s_id, val(1))
            pool.affine_select(out=ident[:, :], in_=ident[:, :], compare_op=ALU.not_equal, fill=1.0,
                               base=0, pattern=[[-1, P]], channel_multiplier=1).then_inc(s_id, 1)
            pool.iota(iota_tok[:, :], [[1, P]], base=0, channel_multiplier=0,
                      allow_small_or_imprecise_dtypes=True).then_inc(s_id, 1)
            pool.iota(part[:, :], [[0, 1]], base=0, channel_multiplier=1,
                      allow_small_or_imprecise_dtypes=True).then_inc(s_id, 1)
            pool.iota(seq_off[:, :, :, :], [[0, 2], [T, SEQ_TILE], [0, CAP]], base=0, channel_multiplier=0,
                      allow_small_or_imprecise_dtypes=True).then_inc(s_id, 1)
            ID_READY, CONSTS_READY = 2, 5

            s_w1, s_prep, s_pw = sem("s_w1"), sem("s_prep"), sem("s_pw")
            for name, dst in late.items():
                if name not in ("lstm_b", "ffn2_b1", "ffn1_w2"):
                    sp.dma_start(dst[:, :] if len(dst.shape) == 2 else dst[:, :, :], t[name]).then_inc(s_w1, 16)
            sp.dma_start(w2_raw, t["ffn1_w2"]).then_inc(s_w1, 16)
            n_pool = [0]

            def prep_pool(ins):
                n_pool[0] += 1
                ins.then_inc(s_pw, 1)

            rows_lstm, rows_ffn2 = scratch[:, 0, :], scratch[:, 1, :]
            for r in (rows_lstm, rows_ffn2):
                prep_pool(pool.memset(r, 0.0))
            prep_pool(pool.memset(row_mod[:, :], 99.0))
            prep_pool(pool.iota(group_of, [[1, 4], [0, N]], base=0, channel_multiplier=0,
                                allow_small_or_imprecise_dtypes=True))
            prep_pool(pool.memset(ones[:, :], 1.0))
            pool.wait_ge(s_pw, n_pool[0])
            for k in range(3):
                prep_pool(pool.iota(row_mod[32 * k:32 * k + 32, :], [[0, 1]], base=0, channel_multiplier=1,
                                    allow_small_or_imprecise_dtypes=True))
            sp.wait_ge(s_pw, n_pool[0])
            for k in range(3):
                sp.dma_start(rows_lstm[32 * k:32 * k + 4, :], t["lstm_b"]).then_inc(s_w1, 16)
                sp.dma_start(rows_ffn2[32 * k:32 * k + 4, :], t["ffn2_b1"]).then_inc(s_w1, 16)
            n_late = 16 * (len(late) + 6)

            step_p = [0]

            def dve_p(ins):
                step_p[0] += 1
                ins.then_inc(s_prep, 1)
                dve.wait_ge(s_prep, step_p[0])

            dve.wait_ge(s_w1, n_late)
            dve.wait_ge(s_pw, n_pool[0])
            ternary = [(ffn1_w1[:, :], ffn1_w1[:, :], 1e-5), (w2_raw, ffn1_w2[:, :, :].rearrange("p f c -> p (f c)"), 1e-5),
                       (ffn2_w1[:, :], ffn2_w1[:, :], 1e-8),
                       (ffn2_w2[:, :, :].rearrange("p f c -> p (f c)"), ffn2_w2[:, :, :].rearrange("p f c -> p (f c)"), 1e-8)]
            for k, (w, _, _) in enumerate(ternary):
                dve_p(dve.tensor_reduce(wsum[:, k:k + 1], w, X, ALU.add, apply_absolute_value=True))
            pe.wait_ge(s_prep, step_p[0])
            pe.matmul(bank[7][:, 0:4], ones[:, :], wsum[:, :], start=True, stop=True).then_inc(s_pw, 1)
            dve.wait_ge(s_pw, n_pool[0] + 1)
            for k, (_, _, floor) in enumerate(ternary):
                dve_p(dve.tensor_scalar(wmean[:, k:k + 1], bank[7][:, k:k + 1], 1.0 / (HT * P * P), floor, ALU.mult, ALU.max))
            dve_p(dve.reciprocal(winv[:, :], wmean[:, :]))
            for k, (w, dst, _) in enumerate(ternary):
                dve_p(dve.tensor_scalar(w, w, winv[:, k:k + 1], MAGIC, ALU.mult, ALU.add))
                dve_p(dve.tensor_scalar(w, w, MAGIC, 1.0, ALU.subtract, ALU.min))
                dve_p(dve.tensor_scalar(dst, w, -1.0, None, ALU.max))
            dve_p(dve.tensor_scalar(half_ws2[:, :], wmean[:, 1:2], 0.5, None, ALU.mult))
            dve_p(dve.tensor_scalar(conv_w[:, :, :], conv_w[:, :, :], wmean[:, 0:1], 0.5, ALU.mult, ALU.mult))
            dve_p(dve.tensor_scalar(lstm_wh[:, 0:3 * P], lstm_wh[:, 0:3 * P], 0.5, None, ALU.mult))
            dve_p(dve.tensor_scalar(lstm_wx[:, 3 * P:4 * P], lstm_wx[:, 3 * P:4 * P], 2.0, None, ALU.mult))
            dve_p(dve.tensor_scalar(ffn3_wv[:, :], ffn3_wv[:, :], 0.5, None, ALU.mult))
            dve_p(dve.tensor_scalar(leak_b_half[:, :], leak_b[:, :], 0.5, None, ALU.mult))
            dve_p(dve.tensor_scalar(leak[:, :], alpha[:, :], -1.0, 1.0, ALU.mult, ALU.add))
            dve_p(dve.tensor_scalar(sel_rows[:, :], group_of, row_mod[:, 0:1], None, ALU.is_equal))
            dve_p(dve.tensor_copy(sel_lstm[:, 0:3 * N], sel_rows[:, 0:3 * N]))
            dve_p(dve.tensor_scalar(sel_lstm[:, 3 * N:4 * N], sel_rows[:, 3 * N:4 * N], 2.0, None, ALU.mult))
            for rows, dst in ((rows_lstm, lstm_bias), (rows_ffn2, ffn2_bias)):
                dve_p(dve.tensor_scalar(dst[96:128, :], rows[96:128, :], 1.0, None, ALU.mult))
                dve_p(dve.tensor_copy(part_bf, rows))
                dve_p(dve.tensor_copy(dst[0:32, :], part_bf[0:32, :]))
                dve_p(dve.tensor_tensor(rows, rows, part_bf, ALU.subtract))
                dve_p(dve.tensor_copy(part_bf, rows))
                dve_p(dve.tensor_copy(dst[32:64, :], part_bf[32:64, :]))
                dve_p(dve.tensor_tensor(rows, rows, part_bf, ALU.subtract))
                dve_p(dve.tensor_copy(dst[64:96, :], rows[64:96, :]))

            s_pa, s_aa, s_da, s_ga = sem("s_pa"), sem("s_aa"), sem("s_da"), sem("s_ga")
            logits = bank[0][:, 0:NTILE * E]
            s_cr = sem("s_cr")
            cond_rep = big[:, 0:TOK]
            dve.wait_ge(s_small, val(16 * len(small)))
            dve.tensor_copy(cond_rep.rearrange("p (n k) -> p n k", k=T),
                            condT[:, :].rearrange("p (n o) -> p n o", o=1).to_broadcast([P, N, T])).then_inc(s_cr, 1)
            pe.wait_ge(s_cr, val(1))
            for i in range(NTILE):
                if i % 8 == 0:
                    pe.wait_ge(s_x[i // 8], 16)
                pe.matmul(logits[:, i * E:(i + 1) * E], xT[:, i * P:(i + 1) * P], wr_x[:, :], start=True, stop=False)
                mm = pe.matmul(logits[:, i * E:(i + 1) * E], cond_rep[:, i * P:(i + 1) * P], wr_t[:, :],
                               start=False, stop=True)
            mm.then_inc(s_pa, 1)

            sig = sb0("sig", [P, NTILE, E])
            sel = sb0("sel", [P, NTILE, E])
            cmp = x1_flat[:, 0:NTILE * E * E].rearrange("p (i e f) -> p i e f", i=NTILE, e=E)
            rank = sb0("rank", [P, NTILE, E])
            den, dpos, half_w = sb0("den", [P, NTILE, 1]), sb0("dpos", [P, NTILE, 1]), sb0("half_w", [P, NTILE, 1])
            gates = sb0("gates", [P, NTILE, E])
            gatesT = sb0("gatesT", [P, 2, P])
            all3 = [P, NTILE, E]

            act.wait_ge(s_pa, val(1))
            act.activation(sig[:, :, :].rearrange("p i e -> p (i e)"), logits, ACT.Exp, scale=-1.0).then_inc(s_aa, 1)

            step_a = [0]

            def dve_a(ins):
                step_a[0] += 1
                ins.then_inc(s_da, 1)
                dve.wait_ge(s_da, val(step_a[0]))

            dve.wait_ge(s_aa, val(1))
            dve_a(dve.tensor_scalar(sig[:, :, :], sig[:, :, :], 1.0, None, ALU.add))
            dve_a(dve.reciprocal(sig[:, :, :], sig[:, :, :]))
            dve.wait_ge(s_small, val(16 * len(small)))
            dve_a(dve.tensor_tensor(sel[:, :, :], sig[:, :, :],
                                    rbias[:, :].rearrange("p (o e) -> p o e", o=1).to_broadcast(all3), ALU.add))
            for e in range(E):
                if e:
                    dve.tensor_tensor(cmp[:, :, e, 0:e], sel[:, :, 0:e], sel[:, :, e:e + 1].to_broadcast([P, NTILE, e]),
                                      ALU.is_ge).then_inc(s_da, 1)
                    step_a[0] += 1
                last = dve.tensor_tensor(cmp[:, :, e, e:E], sel[:, :, e:E],
                                         sel[:, :, e:e + 1].to_broadcast([P, NTILE, E - e]), ALU.is_gt)
                if e < E - 1:
                    last.then_inc(s_da, 1)
                    step_a[0] += 1
            dve_a(last)
            dve_a(dve.tensor_reduce(rank[:, :, :], cmp[:, :, :, :], X, ALU.add))
            dve_a(dve.tensor_scalar(rank[:, :, :], rank[:, :, :], 1.5, None, ALU.is_lt))
            dve_a(dve.tensor_tensor(gates[:, :, :], sig[:, :, :], rank[:, :, :], ALU.mult))
            dve_a(dve.tensor_reduce(den[:, :, :], gates[:, :, :], X, ALU.add))
            dve_a(dve.tensor_scalar(dpos[:, :, :], den[:, :, :], 1e-9, 0.25, ALU.is_gt, ALU.mult))
            dve_a(dve.tensor_scalar(den[:, :, :], den[:, :, :], 1e-9, None, ALU.add))
            dve_a(dve.reciprocal(den[:, :, :], den[:, :, :]))
            dve_a(dve.tensor_tensor(den[:, :, :], den[:, :, :], dpos[:, :, :], ALU.mult))
            dve_a(dve.tensor_scalar(half_w[:, :, :], dpos[:, :, :], -0.5, 0.125, ALU.mult, ALU.add))
            dve_a(dve.tensor_tensor(gates[:, :, :], gates[:, :, :], den[:, :, :].to_broadcast(all3), ALU.mult))
            dve_a(dve.tensor_tensor(rank[:, :, :], rank[:, :, :], half_w[:, :, :].to_broadcast(all3), ALU.mult))
            dve_a(dve.tensor_tensor(gates[:, :, :], gates[:, :, :], rank[:, :, :], ALU.add))
            pe.wait_ge(s_da, val(step_a[0]))
            pe.wait_ge(s_id, val(ID_READY))
            gates_flat = gates[:, :, :].rearrange("p i e -> p (i e)")
            for h in range(2):
                pe.transpose(bank[1][:, h * P:(h + 1) * P], gates_flat[:, h * P:(h + 1) * P], ident[:, :]).then_inc(s_pa, 1)
            act.wait_ge(s_pa, val(3))
            act.copy(gatesT[:, :, :].rearrange("p h k -> p (h k)"), bank[1][:, 0:2 * P]).then_inc(s_aa, 1)
            sp.wait_ge(s_aa, val(2))
            for h in range(2):
                sp.dma_start(g_dram[h * P:(h + 1) * P, :], gatesT[:, h, :]).then_inc(s_ga, 16)
            dve.wait_ge(s_sw2, val(16))
            dve.tensor_scalar(sw2[:, :], sw2[:, :], 1.0 / 16.0, None, ALU.mult).then_inc(s_sw2, 1)

            cst = sb0("cst", [P, CHUNK])
            th = [sb0(f"th{k}", [P, CHUNK]) for k in range(2)]
            pb = [sb0(f"pb{k}", [P, CHUNK]) for k in range(2)]
            qb = [sb0(f"qb{k}", [P, CHUNK]) for k in range(2)]
            gl = [sb0(f"gl{k}", [P, CHUNK]) for k in range(2)]
            gg = [sb0(f"gg{k}", [P, CHUNK]) for k in range(2)]
            score = sb0("score", [P, NTILE, E])
            s_ab, s_th, s_p, s_q, s_sh = sem("s_ab"), sem("s_th"), sem("s_p"), sem("s_q"), sem("s_sh")
            s_r, s_gelu, s_gg, s_ro = sem("s_r"), sem("s_gelu"), sem("s_gg"), sem("s_ro")
            s_gr, s_acc, s_tr, s_ct, s_sc, s_sce = ([sem("s_gr0"), sem("s_gr1")], sem("s_acc"), sem("s_tr"), sem("s_ct"),
                                                    sem("s_sc"), sem("s_sce"))
            NSH, NRO = HS_TILES, E
            UNITS = [u for j in range(NSH) for u in (("sh", j), ("ro", 2 * j), ("ro", 2 * j + 1))]
            LEAD = 2
            ab_bank, r_bank, acc_bank = [(bank[0], bank[1]), (bank[2], bank[3])], bank[4:6], bank[6:8]

            def first_products(c, u):
                kind, j = UNITS[u]
                xc = xT[:, ds(c * CHUNK, CHUNK)]
                if kind == "sh":
                    k = c * NSH + j
                    for b, w in zip(ab_bank[j % 2], (sw1, sw3)):
                        if b is ab_bank[j % 2][0] and not (below(c, 1) and j < 2):
                            pe.wait_ge(s_q, val(k - 1))
                        pe.matmul(b[:, :], w[:, j * P:(j + 1) * P], xc, start=True, stop=True).then_inc(s_ab, 1)
                else:
                    k = c * NRO + j
                    if not (below(c, 1) and j < 2):
                        pe.wait_ge(s_gelu, val(k - 1))
                    pe.matmul(r_bank[j % 2][:, :], rw1[:, j * P:(j + 1) * P], xc, start=True, stop=True).then_inc(s_r, 1)

            def second_product(c, par, u):
                kind, j = UNITS[u]
                a = acc_bank[par]
                if kind == "sh":
                    pe.wait_ge(s_q, val(c * NSH + j + 1))
                    if u == 0 and not (below(c, 2)):
                        pe.wait_ge(s_sce, val(c - 1))
                    pe.matmul(a[:, :], sw2[:, j * P:(j + 1) * P], qb[j % 2][:, :], start=(u == 0),
                              stop=False).then_inc(s_sh, 1)
                else:
                    pe.wait_ge(s_gg, val(c * NRO + j + 1))
                    pe.matmul(a[:, :], rw2[:, j * P:(j + 1) * P], gg[j % 2][:, :], start=False,
                              stop=(u == len(UNITS) - 1)).then_inc(s_ro, 1)

            def chunk_transposes(c, par):
                pe.wait_ge(s_acc, val(c + 1))
                for i in range(TILES_CHUNK):
                    mm = pe.transpose(acc_bank[par][:, i * P:(i + 1) * P], cst[:, i * P:(i + 1) * P], ident[:, :])
                mm.then_inc(s_tr, 1)

            def chunk_scores(c, par):
                pe.wait_ge(s_ct, val(c + 1))
                for i in range(TILES_CHUNK):
                    mm = pe.matmul(acc_bank[par][:, i * E:(i + 1) * E], cst[:, i * P:(i + 1) * P], gate_w[:, :],
                                   start=True, stop=True)
                mm.then_inc(s_sc, 1)

            def chunk_evacuate(c, par):
                act.wait_ge(s_ro, val((c + 1) * NRO))
                if not (below(c, 1)):
                    act.wait_ge(s_sc, val(c))
                act.copy(cst[:, :], acc_bank[par][:, :]).then_inc(s_acc, 1)

            def chunk_store_tokens(c, par):
                dve.wait_ge(s_tr, val(c + 1))
                dve.tensor_copy(ctok[:, ds(c * TILES_CHUNK, TILES_CHUNK), :].rearrange("p i k -> p (i k)"),
                                acc_bank[par][:, :]).then_inc(s_ct, 1)

            def chunk_store_scores(c, par):
                dve.wait_ge(s_sc, val(c + 1))
                dve.tensor_copy(score[:, ds(c * TILES_CHUNK, TILES_CHUNK), :].rearrange("p i k -> p (i k)"),
                                acc_bank[par][:, 0:TILES_CHUNK * E]).then_inc(s_sce, 1)

            def load_gate_rows(c, par):
                if not (below(c, 2)):
                    sp.wait_ge(s_gg, val((c - 1) * NRO))
                src = g_dram[ds(c * TILES_CHUNK * E, TILES_CHUNK * E), :].rearrange("r k -> (r k)")
                sp.dma_start(gate_rows[par].rearrange("p i e k -> p (i e k)"),
                             src.partition_broadcast(P)).then_inc(s_gr[par], 16)

            def chunk(c, par, first=False, last=False):
                n = len(UNITS)
                for u in range(n):
                    if u + LEAD < n:
                        first_products(c, u + LEAD)
                    elif not last:
                        first_products(c + 1, u + LEAD - n)
                    second_product(c, par, u)
                    if not first and u == 4:
                        chunk_transposes(c - 1, 1 - par)
                    if not first and u == 7:
                        chunk_scores(c - 1, 1 - par)
                for u, (kind, j) in enumerate(UNITS):
                    if kind == "sh":
                        k = c * NSH + j
                        act.wait_ge(s_ab, val(2 * k + 1))
                        if not (first and j < 2):
                            act.wait_ge(s_p, val(k - 1))
                        act.activation(th[j % 2][:, :], ab_bank[j % 2][0][:, :], ACT.Tanh, scale=0.5).then_inc(s_th, 1)
                    else:
                        k = c * NRO + j
                        act.wait_ge(s_r, val(k + 1))
                        if not (first and j < 2):
                            act.wait_ge(s_gg, val(k - 1))
                        act.activation(gl[j % 2][:, :], r_bank[j % 2][:, :], ACT.Gelu).then_inc(s_gelu, 1)
                    if not first and u == 2:
                        chunk_evacuate(c - 1, 1 - par)
                for u, (kind, j) in enumerate(UNITS):
                    if kind == "sh":
                        k = c * NSH + j
                        dve.wait_ge(s_th, val(k + 1))
                        dve.scalar_tensor_tensor(pb[j % 2][:, :], th[j % 2][:, :], 1.0, ab_bank[j % 2][0][:, :],
                                                 ALU.add, ALU.mult).then_inc(s_p, 1)
                        dve.wait_ge(s_p, val(k + 1))
                        dve.wait_ge(s_ab, val(2 * k + 2))
                        if not (first and j < 2):
                            dve.wait_ge(s_sh, val(k - 1))
                        dve.tensor_tensor(qb[j % 2][:, :], pb[j % 2][:, :], ab_bank[j % 2][1][:, :],
                                          ALU.mult).then_inc(s_q, 1)
                    else:
                        k = c * NRO + j
                        dve.wait_ge(s_gelu, val(k + 1))
                        if j == 0:
                            dve.wait_ge(s_gr[par], val(16 * (turn(c) + 1)))
                        if not (first and j < 2):
                            dve.wait_ge(s_ro, val(k - 1))
                        dve.tensor_tensor(gg[j % 2][:, :].rearrange("p (i k) -> p i k", k=P),
                                          gl[j % 2][:, :].rearrange("p (i k) -> p i k", k=P),
                                          gate_rows[par][:, :, j, :], ALU.mult).then_inc(s_gg, 1)
                    if not first and u == 6:
                        chunk_store_tokens(c - 1, 1 - par)
                    if not first and u == 9:
                        chunk_store_scores(c - 1, 1 - par)
                if not last:
                    load_gate_rows(c + 1, 1 - par)

            pe.wait_ge(s_wmoe, val(16 * len(moe)))
            pe.wait_ge(s_sw2, val(17))
            pe.wait_ge(s_aa, val(2))
            sp.wait_ge(s_ga, val(32))
            load_gate_rows(0, 0)
            for u in range(LEAD):
                first_products(0, u)
            chunk(0, 0, first=True)
            with nc.Fori(0, (NCHUNK - 2) // 2) as i:
                chunk(Lin(i, 2, 1), 1)
                chunk(Lin(i, 2, 2), 0)
            chunk(NCHUNK - 1, 1, last=True)
            chunk_evacuate(NCHUNK - 1, 1)
            chunk_transposes(NCHUNK - 1, 1)
            chunk_store_tokens(NCHUNK - 1, 1)
            chunk_scores(NCHUNK - 1, 1)
            chunk_store_scores(NCHUNK - 1, 1)

            s_dc, s_ac, s_pc, s_vc = sem("s_dc"), sem("s_ac"), sem("s_pc"), sem("s_vc")
            smax, ssum = sb0("smax", [P, NTILE, 1]), sb0("ssum", [P, NTILE, 1])
            probT = sb0("probT", [P, 2, P])
            topv = sb0("topv", [P, 2, SEQ_TILE, CAP])
            topi = sb0("topi", [P, 2, SEQ_TILE, CAP], U32)
            topf = sb0("topf", [P, 2, SEQ_TILE, CAP])
            step_c = [0]

            def dve_c(ins):
                step_c[0] += 1
                ins.then_inc(s_dc, 1)
                dve.wait_ge(s_dc, val(step_c[0]))

            dve.wait_ge(s_sce, val(NCHUNK))
            dve_c(dve.tensor_reduce(smax[:, :, :], score[:, :, :], X, ALU.max))
            dve_c(dve.tensor_tensor(score[:, :, :], score[:, :, :], smax[:, :, :].to_broadcast(all3), ALU.subtract))
            act.wait_ge(s_dc, val(step_c[0]))
            act.activation(sel[:, :, :].rearrange("p i e -> p (i e)"), score[:, :, :].rearrange("p i e -> p (i e)"),
                           ACT.Exp).then_inc(s_ac, 1)
            dve.wait_ge(s_ac, val(1))
            dve_c(dve.tensor_reduce(ssum[:, :, :], sel[:, :, :], X, ALU.add))
            dve_c(dve.reciprocal(ssum[:, :, :], ssum[:, :, :]))
            dve_c(dve.tensor_tensor(sel[:, :, :], sel[:, :, :], ssum[:, :, :].to_broadcast(all3), ALU.mult))
            pe.wait_ge(s_dc, val(step_c[0]))
            prob_flat = sel[:, :, :].rearrange("p i e -> p (i e)")
            for h in range(2):
                mm = pe.transpose(bank[0][:, h * P:(h + 1) * P], prob_flat[:, h * P:(h + 1) * P], ident[:, :])
            mm.then_inc(s_pc, 1)
            dve.wait_ge(s_pc, val(1))
            dve_c(dve.tensor_copy(probT[:, :, :].rearrange("p h k -> p (h k)"), bank[0][:, 0:2 * P]))
            for h in range(2):
                for b in range(SEQ_TILE):
                    seq = probT[:, h, b * T:(b + 1) * T]
                    dve_c(dve.max(topv[:, h, b, :], seq))
                    dve.max_index(topi[:, h, b, :], topv[:, h, b, :], seq).then_inc(s_dc, 1)
                    step_c[0] += 1
            dve.wait_ge(s_dc, val(step_c[0]))
            dve.wait_ge(s_id, val(CONSTS_READY))
            dve_c(dve.tensor_copy(topf[:, :, :, :], topi[:, :, :, :]))
            dve_c(dve.tensor_tensor(topf[:, :, :, :], topf[:, :, :, :], seq_off[:, :, :, :], ALU.add))
            sp.wait_ge(s_dc, val(step_c[0]))
            for dram, src in ((i_dram, topf), (v_dram, topv)):
                rows = dram.rearrange("i (e k) -> (i e) k", e=E)
                for h in range(2):
                    sp.dma_start(rows[h * P:(h + 1) * P, :],
                                 src[:, h, :, :].rearrange("p b j -> p (b j)")).then_inc(s_vc, 16)
            sp.wait_ge(s_vc, val(64))
            slot_rows = [sb0(f"slot_rows{k}", [2 * NTILE, P]) for k in range(2)]
            slot_cols = sb0("slot_cols", [P, 2, 2 * NTILE])
            s_sr = sem("s_sr")
            for k, dram in enumerate((i_dram, v_dram)):
                act.wait_ge(s_vc, val(64))
                act.dma_start(slot_rows[k][:, :], dram.rearrange("i (h k) -> (i h) k", h=2)).then_inc(s_sr, 16)
            pe.wait_ge(s_sr, val(32))
            for k in range(2):
                mm = pe.transpose(bank[4][:, k * 2 * NTILE:(k + 1) * 2 * NTILE], slot_rows[k][:, :],
                                  ident[0:2 * NTILE, 0:2 * NTILE])
            mm.then_inc(s_sr, 1)

            HALF_TILES = 4
            NHALF = NTILE // HALF_TILES
            cgt = [sb0(f"cgt{k}", [P, HALF_TILES, C]) for k in range(2)]
            onehot = [sb0(f"onehot{k}", [P, HALF_TILES * SLOT_TILE]) for k in range(2)]
            s_ld, s_oh, s_ga2, s_gx = [sem("s_ld0"), sem("s_ld1")], sem("s_oh"), sem("s_ga2"), sem("s_gx")
            def gather_loads(k, par):
                if not (below(k, 2)):
                    sp.wait_ge(s_ga2, val(2 * k - 2))
                rows = i_dram[ds(k * HALF_TILES, HALF_TILES), :].rearrange("i s -> (i s)")
                sp.dma_start(onehot[par][:, :], rows.partition_broadcast(P)).then_inc(s_ld[par], 16)
                sp.dma_start(cgt[par][:, :, :], ctok[:, ds(k * HALF_TILES, HALF_TILES), :]).then_inc(s_ld[par], 16)

            def gather_step(g, par):
                k = g * 2 + par
                group_x = big[:, ds(g * (E * SLOT_GE), E * SLOT_GE)].rearrange("p (e k) -> p e k", e=E)
                dve.wait_ge(s_ld[par], val(32 * (g + 1)))
                dve.tensor_scalar(onehot[par][:, :], onehot[par][:, :], part[:, 0:1], None,
                                  ALU.is_equal).then_inc(s_oh, 1)
                pe.wait_ge(s_oh, val(k + 1))
                for b in range(2):
                    dst = bank[2 * par + b]
                    if not below(k, 2):
                        pe.wait_ge(s_gx, val(2 * (k - 2) + b + 1))
                    for i in range(2):
                        tile = 2 * b + i
                        mm = pe.matmul(dst[:, i * SLOT_TILE:(i + 1) * SLOT_TILE], cgt[par][:, tile, :],
                                       onehot[par][:, tile * SLOT_TILE:(tile + 1) * SLOT_TILE],
                                       start=True, stop=True)
                    mm.then_inc(s_ga2, 1)
                    act.wait_ge(s_ga2, val(2 * k + b + 1))
                    for i in range(2):
                        at = (par * HALF_TILES + 2 * b + i) * SLOT_E
                        cp = act.copy(group_x[:, :, at:at + SLOT_E],
                                      dst[:, i * SLOT_TILE:(i + 1) * SLOT_TILE].rearrange("p (e k) -> p e k", e=E))
                    cp.then_inc(s_gx, 1)

            pe.wait_ge(s_sce, val(NCHUNK))
            dve.wait_ge(s_sr, val(33))
            dve.tensor_copy(slot_cols[:, :, :].rearrange("p a b -> p (a b)"), bank[4][:, 0:4 * NTILE]).then_inc(s_sr, 1)
            gather_loads(0, 0)

            def gather_pair(i, last=False):
                gather_loads(i * 2 + 1, 1)
                gather_step(i, 0)
                if not last:
                    gather_loads(i * 2 + 2, 0)
                gather_step(i, 1)

            gather_pair(0)
            with nc.Fori(0, NHALF // 2 - 2) as i:
                gather_pair(Lin(i, 1, 1))
            gather_pair(NHALF // 2 - 1, last=True)

            hb = th + pb
            yT = ctok[:, 0:2 * TILES_GROUP, :].rearrange("p i k -> p (i k)").rearrange(
                "p (i e k) -> p i e k", i=TILES_GROUP, e=E)
            ysl = ctok[:, 2 * TILES_GROUP:4 * TILES_GROUP, :]
            scat = sb0("scat", [P, 2 * TILES_GROUP, P])
            s_h, s_hg, s_y2, s_y, s_ye, s_yt, s_yl, s_st, s_so, s_res = (sem(n) for n in (
                "s_h", "s_hg", "s_y2", "s_y", "s_ye", "s_yt", "s_yl", "s_st", "s_so", "s_res"))
            U2 = 2 * E
            h_bank, y_bank, m_bank = bank[0:4], bank[4:6], bank[6:8]

            def isfirst(g, cond):
                return below(g, 1) and cond

            def expert_up(g, u):
                w = g * U2 + u
                e, b = u // 2, u % 2
                if not isfirst(g, u < 4):
                    pe.wait_ge(s_hg, val(w - 3))
                for i in range(2):
                    ht = 2 * b + i
                    mm = pe.matmul(h_bank[u % 4][:, i * SLOT_GE:(i + 1) * SLOT_GE], w1[:, e, ht * P:(ht + 1) * P],
                                   big[:, ds(g * (E * SLOT_GE) + e * SLOT_GE, SLOT_GE)], start=True, stop=True)
                mm.then_inc(s_h, 1)

            def expert_down(g, u):
                w = g * U2 + u
                e, b = u // 2, u % 2
                pe.wait_ge(s_hg, val(w + 1))
                if b == 0 and not isfirst(g, e < 2):
                    pe.wait_ge(s_ye, val(g * E + e - 1))
                for i in range(2):
                    ht = 2 * b + i
                    mm = pe.matmul(y_bank[e % 2][:, 0:SLOT_GE], w2[:, e, ht, :], hb[u % 4][:, i * SLOT_GE:(i + 1) * SLOT_GE],
                                   start=(ht == 0), stop=(ht == HT - 1))
                mm.then_inc(s_y2, 1)

            def group(g, last=False):
                for u in range(U2):
                    if u + LEAD < U2:
                        expert_up(g, u + LEAD)
                    elif not last:
                        expert_up(g + 1, u + LEAD - U2)
                    expert_down(g, u)
                for u in range(U2):
                    act.wait_ge(s_h, val(g * U2 + u + 1))
                    if not isfirst(g, u < 4):
                        act.wait_ge(s_y2, val(g * U2 + u - 3))
                    act.activation(hb[u % 4][:, :], h_bank[u % 4][:, :], ACT.Gelu).then_inc(s_hg, 1)
                for k in range(2 * TILES_GROUP):
                    if k == 0 and not isfirst(g, True):
                        dve.wait_ge(s_so, val(2 * g))
                    col = g * (2 * TILES_GROUP) + k
                    sc_ap = slot_cols[:, :, :].rearrange("p a b -> p (a b)")
                    last_s = dve.tensor_scalar(scat[:, k, :], iota_tok[:, :], sc_ap[:, ds(col, 1)],
                                               sc_ap[:, ds(col + 2 * NTILE, 1)], ALU.is_equal, ALU.mult)
                    if k % E == E - 1:
                        last_s.then_inc(s_st, 1)
                    if k % 2 == 1:
                        e = k // 2
                        dve.wait_ge(s_y2, val(g * U2 + 2 * e + 2))
                        if e == 0 and not isfirst(g, True):
                            dve.wait_ge(s_yt, val(4 * g))
                        dve.tensor_copy(yT[:, :, e, :], y_bank[e % 2][:, 0:SLOT_GE].rearrange("p (i k) -> p i k", k=SLOT_E)
                                        ).then_inc(s_ye, 1)
                pe.wait_ge(s_ye, val((g + 1) * E))
                yflat = yT[:, :, :, :].rearrange("p i e k -> p (i e k)")
                for b in range(4):
                    m = m_bank[b % 2]
                    if b >= 2:
                        pe.wait_ge(s_yl, val(4 * g + b - 1))
                    elif not isfirst(g, True):
                        pe.wait_ge(s_res, val(2 * g - 1 + b))
                    for i in range(4):
                        mm = pe.transpose(m[:, i * P:(i + 1) * P], yflat[:, (4 * b + i) * P:(4 * b + i + 1) * P], ident[:, :])
                    mm.then_inc(s_yt, 1)
                    act.wait_ge(s_yt, val(4 * g + b + 1))
                    if b == 0 and not isfirst(g, True):
                        act.wait_ge(s_so, val(2 * g))
                    act.copy(ysl[:, 4 * b:4 * b + 4, :].rearrange("p i k -> p (i k)"), m[:, :]).then_inc(s_yl, 1)
                for b in range(2):
                    m = m_bank[b]
                    pe.wait_ge(s_yl, val(4 * g + 4))
                    pe.wait_ge(s_st, val(2 * (g + 1)))
                    for i in range(4):
                        tile = 4 * b + i
                        for h in range(2):
                            mm = pe.matmul(m[:, i * P:(i + 1) * P], ysl[:, 2 * tile + h, :], scat[:, 2 * tile + h, :],
                                           start=(h == 0), stop=(h == 1))
                    mm.then_inc(s_so, 1)
                    dve.wait_ge(s_so, val(2 * g + b + 1))
                    n0 = g * (TILES_GROUP * SEQ_TILE) + b * 16
                    dve.tensor_tensor(x1[:, :, ds(n0, 16)].rearrange("p t n -> p n t"),
                                      xT[:, ds(n0 * T, 16 * T)].rearrange("p (n t) -> p n t", t=T),
                                      m[:, :].rearrange("p (n t) -> p n t", t=T), ALU.add).then_inc(s_res, 1)

            pe.wait_ge(s_wffn, val(32))
            pe.wait_ge(s_gx, val(2 * NHALF))
            pe.wait_ge(s_sr, val(34))
            for u in range(LEAD):
                expert_up(0, u)
            group(0)
            with nc.Fori(0, GROUPS - 2) as i:
                group(Lin(i, 1, 1))
            group(GROUPS - 1, last=True)

        with ExitStack() as layers:
            def sb1(name, shape, dt=F32):
                return layers.enter_context(nc.sbuf_tensor(name, shape, dt))

            tg, tc = sb1("tg", [P, 4, N]), sb1("tc", [P, N])
            lp, lq, cell, hL = sb1("lp", [P, N]), sb1("lq", [P, N]), sb1("cell", [P, N]), sb1("hL", [P, N])
            mx1, m1, sc1 = sb1("mx1", [P, 1]), sb1("m1", [P, 1]), sb1("sc1", [P, 1])
            mx2, m2, sc2, m2w = sb1("mx2", [P, 1]), sb1("m2", [P, 1]), sb1("sc2", [P, 1]), sb1("m2w", [P, 1])
            v1, xq, xqT = sb1("v1", [P, N]), sb1("xq", [P, N]), sb1("xqT", [P, N])
            u_sb, z_conv, y_part, y_full = (sb1(n, [P, HT, N]) for n in ("u_sb", "z_conv", "y_part", "y_full"))
            th1, hs = sb1("th_ffn1", [P, HT, N]), sb1("hs", [P, HT, N])
            v2, q2 = sb1("v2", [P, HT * P]), sb1("q2", [P, HT * P], BF16)
            q2T = sb1("q2T", [P, HT, N], BF16)
            ys = sb1("ys", [P, C])
            h2 = sb1("h2", [P, N])
            g2 = sb1("g2", [P, HT, N])
            g3, p3, pre3, h3, h3_prev = (sb1(n, [P, N]) for n in ("g3", "p3", "pre3", "h3", "h3_prev"))
            leaked, z_half, diff = (sb1(n, [P, N]) for n in ("leaked", "z_half", "diff"))
            xr_mul, xk_mul = sb1("xr_mul", [P, N]), sb1("xk_mul", [P, N])
            xr, xk, tr, kr, kk, o1 = (sb1(n, [P, N]) for n in ("xr", "xk", "tr", "kr", "kk", "o1"))
            magic, halves, leak_full = sb1("magic", [P, 1]), sb1("halves", [P, N]), sb1("leak_full", [P, N])
            mu_r_full, mu_k_full = sb1("mu_r_full", [P, N]), sb1("mu_k_full", [P, N])
            pool_tick = sb1("pool_tick", [P, 2])
            ident_bf = sb1("ident_bf", [P, P], BF16)

            s_state = sem("s_state")
            pool_states = [(cell, 0.0), (magic, MAGIC), (h3_prev, 0.0), (halves, 0.5), (pool_tick, 0.0)]
            dve_states = [(h2, condT[:, :]), (h3, condT[:, :]), (ident_bf, ident[:, :])] + [
                (dst, col[:, 0:1].to_broadcast([P, N])) for dst, col in
                ((leak_full, leak), (mu_r_full, mu_r), (mu_k_full, mu_k))]
            pool.wait_ge(s_res, 2 * GROUPS)
            for dst, value in pool_states:
                pool.memset(dst[:, :], value).then_inc(s_state, 1)
            for dst, src in dve_states:
                dve.tensor_copy(dst[:, :], src).then_inc(s_state, 1)
            dve.tensor_scalar(hL[:, :], condT[:, :], 2.0, None, ALU.mult).then_inc(s_state, 1)
            STATES = len(pool_states) + len(dve_states) + 1
            for eng in (pe, act, dve, pool):
                eng.wait_ge(s_state, STATES)
                eng.wait_ge(s_res, 2 * GROUPS)

            B_GATE, B_U, B_V, B_F2, B_TR, B_R2, B_R3, B_Q = bank
            ps_V2 = B_R3[:, 0:2 * P]
            ps_y = B_TR[:, 0:P]
            ps_ysT = B_TR[:, P:2 * P]
            ps_tr1 = B_Q[:, 0:P]
            ps_tr2 = B_R2[:, 0:P]
            ps_r2 = B_R3[:, 2 * P:3 * P]
            ps_F2down = B_R2[:, P:2 * P]
            ps_r3 = B_R3[:, 3 * P:4 * P]
            ps_r = B_TR[:, 2 * P:3 * P]
            ps_k = B_TR[:, 3 * P:4 * P]
            ps_v = B_Q[:, P:2 * P]
            q2_ps = ps_V2.bitcast(BF16)

            def flat(a):
                return a[:, :, :].rearrange("p f n -> p (f n)")

            def x_at(step):
                return x1[:, ds(step, 1), :].rearrange("p o n -> p (o n)")

            stages = {}
            counter = {}

            def stage(eng, *waits, first=0, last=T - 1, edges=()):
                def declare(f):
                    name = f.__name__.rstrip("_")
                    counter[name] = sem("t_" + name)
                    stages[name] = (eng, waits, edges, f, first, last)
                    return f
                return declare

            def run(name, t):
                eng, waits, edges, f, first, last = stages[name]
                if isinstance(t, int) and not first <= t <= last:
                    return
                if eng is pool:
                    pool.wait_ge(s_state, STATES)
                for other, offset in waits if isinstance(t, Lin) else waits + edges:
                    step = t + offset
                    if isinstance(step, int):
                        if step < stages[other][4]:
                            continue
                        step = min(step, stages[other][5])
                    eng.wait_ge(counter[other], val(step + 1 - stages[other][4]))
                f(t).then_inc(counter[name], 1)

            @stage(pe, ("tg", -1))
            def gates_x(t):
                pe.matmul(B_GATE[:, :], lstm_bias[:, :], sel_lstm[:, :], start=True, stop=False, skip_group_check=True)
                for q in range(4):
                    mm = pe.matmul(B_GATE[:, q * N:(q + 1) * N], lstm_wx[:, q * P:(q + 1) * P], x_at(t),
                                   start=False, stop=False, skip_group_check=True)
                return mm

            @stage(pe, ("hL", -1))
            def gates_h(t):
                for q in range(4):
                    mm = pe.matmul(B_GATE[:, q * N:(q + 1) * N], lstm_wh[:, q * P:(q + 1) * P], hL[:, :],
                                   start=False, stop=True, skip_group_check=True)
                return mm

            @stage(act, ("gates_h", 0), ("hL", -1))
            def tg_(t):
                return act.activation(flat(tg), B_GATE[:, :], ACT.Tanh, scale=0.5)

            @stage(dve, ("tg", 0), ("cell", -1))
            def lp_(t):
                return dve.scalar_tensor_tensor(lp[:, :], tg[:, 1, :], 1.0, cell[:, :], ALU.add, ALU.mult)

            @stage(dve, ("tg", 0), ("cell", -1))
            def lq_(t):
                return dve.scalar_tensor_tensor(lq[:, :], tg[:, 0, :], 1.0, tg[:, 3, :], ALU.add, ALU.mult)

            @stage(dve, ("lp", 0), ("lq", 0), ("tc", -1))
            def cell_(t):
                return dve.scalar_tensor_tensor(cell[:, :], lp[:, :], 0.5, lq[:, :], ALU.mult, ALU.add)

            @stage(act, ("cell", 0), ("hL", -1))
            def tc_(t):
                return act.activation(tc[:, :], cell[:, :], ACT.Tanh, scale=0.5)

            @stage(dve, ("tc", 0), ("tr1", -1), ("gates_h", 0))
            def hL_(t):
                return dve.scalar_tensor_tensor(hL[:, :], tg[:, 2, :], 1.0, tc[:, :], ALU.add, ALU.mult)

            @stage(pe, ("hL", 0), ("v1", -1), ("o1", -9))
            def tr1(t):
                return pe.transpose(ps_tr1, hL[:, :], ident[:, :])

            @stage(dve, ("tr1", 0), ("m1", -1))
            def mx1_(t):
                return dve.tensor_reduce(mx1[:, :], ps_tr1, X, ALU.max, apply_absolute_value=True)

            @stage(dve, ("mx1", 0), ("xq", -1))
            def m1_(t):
                return dve.tensor_scalar(m1[:, :], mx1[:, :], 2e-5, 1.0 / 127.0, ALU.max, ALU.mult)

            @stage(dve, ("m1", 0), ("v1", -1))
            def sc1_(t):
                return dve.reciprocal(sc1[:, :], m1[:, :])

            @stage(act, ("sc1", 0), ("xq", -1))
            def v1_(t):
                return act.activation(v1[:, :], ps_tr1, ACT.Identity, bias=magic[:, 0:1], scale=sc1[:, 0:1])

            @stage(dve, ("v1", 0), ("tr2", -1))
            def xq_(t):
                return dve.tensor_scalar(xq[:, :], v1[:, :], MAGIC, m1[:, 0:1], ALU.subtract, ALU.mult)

            @stage(pe, ("xq", 0), ("x3", -5))
            def tr2(t):
                return pe.transpose(ps_tr2, xq[:, :], ident[:, :])

            @stage(act, ("tr2", 0), ("u", -1))
            def xqT_(t):
                return act.copy(xqT[:, :], ps_tr2)

            @stage(pe, ("xqT", 0), ("u_sb", -1))
            def u(t):
                for f in range(HT):
                    mm = pe.matmul(B_U[:, f * N:(f + 1) * N], ffn1_w1[:, f * P:(f + 1) * P], xqT[:, :],
                                   start=True, stop=True)
                return mm

            @stage(act, ("u", 0), ("y_part", -1), ("z_conv", -1))
            def u_sb_(t):
                return act.copy(flat(u_sb), B_U[:, :])

            @stage(dve, ("u_sb", 0), ("y_part", -1), ("hs", -2), first=1, last=T)
            def y_full_(t):
                if isinstance(t, int) and t == T:
                    return dve.tensor_copy(y_full[:, :, :], y_part[:, :, :])
                for f in range(HT):
                    op = dve.scalar_tensor_tensor(y_full[:, f, :], u_sb[:, f, :], conv_w[:, f, 2:3], y_part[:, f, :],
                                                  ALU.mult, ALU.add)
                return op

            @stage(dve, ("u_sb", 0), ("z_conv", -1), ("y_full", 0))
            def y_part_(t):
                for f in range(HT):
                    if isinstance(t, int) and t == 0:
                        op = dve.tensor_scalar(y_part[:, f, :], u_sb[:, f, :], conv_w[:, f, 1:2], conv_b[:, f:f + 1],
                                               ALU.mult, ALU.add)
                    else:
                        op = dve.scalar_tensor_tensor(y_part[:, f, :], u_sb[:, f, :], conv_w[:, f, 1:2],
                                                      z_conv[:, f, :], ALU.mult, ALU.add)
                return op

            @stage(pool, ("u_sb", 0), ("y_part", 0))
            def z_conv_(t):
                pool.tensor_tensor(pool_tick[:, 0:1], pool_tick[:, 1:2], pool_tick[:, 1:2], ALU.add)
                for f in range(HT):
                    op = pool.tensor_scalar(z_conv[:, f, :], u_sb[:, f, :], conv_w[:, f, 0:1], conv_b[:, f:f + 1],
                                            ALU.mult, ALU.add)
                return op

            @stage(act, ("y_full", 1), ("hs", -1))
            def th1_(t):
                return act.activation(flat(th1), flat(y_full), ACT.Tanh, scale=0.5)

            @stage(dve, ("th1", 0), ("V", -1))
            def hs_(t):
                return dve.scalar_tensor_tensor(flat(hs), flat(th1), 1.0, flat(y_full), ALU.add, ALU.mult)

            @stage(pe, ("hs", 0), ("v2", -1))
            def V(t):
                for f in range(HT):
                    mm = pe.transpose(B_V[:, f * P:(f + 1) * P], hs[:, f, :], ident[:, :])
                return mm

            @stage(dve, ("V", 0), ("m2", -1))
            def mx2_(t):
                return dve.tensor_reduce(mx2[:, :], B_V[:, :], X, ALU.max, apply_absolute_value=True)

            @stage(dve, ("mx2", 0), ("m2w", -1))
            def m2_(t):
                return dve.tensor_scalar(m2[:, :], mx2[:, :], 2e-5, 1.0 / 127.0, ALU.max, ALU.mult)

            @stage(dve, ("m2", 0), ("v2", -1))
            def sc2_(t):
                return dve.reciprocal(sc2[:, :], m2[:, :])

            @stage(act, ("sc2", 0), ("q2", -1))
            def v2_(t):
                return act.activation(v2[:, :], B_V[:, :], ACT.Identity, bias=magic[:, 0:1], scale=sc2[:, 0:1])

            @stage(dve, ("v2", 0), ("V2", -1))
            def q2_(t):
                return dve.tensor_scalar(q2[:, :], v2[:, :], MAGIC, 127.0, ALU.subtract, ALU.min)

            @stage(dve, ("m2", 0), ("ys", -1))
            def m2w_(t):
                return dve.tensor_tensor(m2w[:, :], m2[:, :], half_ws2[:, :], ALU.mult)

            @stage(pe, ("q2", 0), ("q2T", -1), ("h2", -1),
                   edges=(("g3", -3),))
            def V2(t):
                for f in range(HT):
                    mm = pe.transpose(q2_ps[:, f * P:(f + 1) * P], q2[:, f * P:(f + 1) * P], ident_bf[:, :])
                return mm

            @stage(act, ("V2", 0), ("y", -1))
            def q2T_(t):
                return act.copy(flat(q2T), q2_ps)

            @stage(pe, ("q2T", 0), ("ys", -1), ("kr", -4), ("tr", -4),
                   edges=(("x2", -1),))
            def y(t):
                for f in range(HT):
                    mm = pe.matmul(ps_y, q2T[:, f, :], ffn1_w2[:, f, :], start=(f == 0), stop=(f == HT - 1))
                return mm

            @stage(act, ("y", 0), ("m2w", 0), ("ysT", -1))
            def ys_(t):
                return act.activation(ys[:, :], ps_y, ACT.Copy, scale=m2w[:, 0:1])

            @stage(pe, ("ys", 0), ("x2", -1),
                   edges=(("kr", -4), ("tr", -4),))
            def ysT(t):
                return pe.transpose(ps_ysT, ys[:, :], ident[:, :])

            @stage(dve, ("ysT", 0))
            def x2(t):
                return dve.tensor_tensor(x_at(t), x_at(t), ps_ysT, ALU.add)

            @stage(pe, ("x2", 0), ("h2", -1), ("g3", -2),
                   edges=(("q2T", 0),))
            def r2(t):
                pe.matmul(ps_r2, rnn_wx[:, :], x_at(t), start=True, stop=False)
                return pe.matmul(ps_r2, rnn_wh[:, :], h2[:, :], start=False, stop=True)

            @stage(act, ("r2", 0), ("F2up", -1))
            def h2_(t):
                return act.activation(h2[:, :], ps_r2, ACT.Tanh, bias=rnn_b[:, 0:1])

            @stage(pe, ("g2", -1))
            def F2bias(t):
                return pe.matmul(B_F2[:, :], ffn2_bias[:, :], sel_rows[:, :], start=True, stop=False,
                                 skip_group_check=True)

            @stage(pe, ("h2", 0))
            def F2up(t):
                for f in range(HT):
                    mm = pe.matmul(B_F2[:, f * N:(f + 1) * N], ffn2_w1[:, f * P:(f + 1) * P], h2[:, :],
                                   start=False, stop=True, skip_group_check=True)
                return mm

            @stage(act, ("F2up", 0), ("F2down", -1))
            def g2_(t):
                return act.activation(flat(g2), B_F2[:, :], ACT.Gelu)

            @stage(pe, ("g2", 0), ("x3", -1), ("xqT", 4))
            def F2down(t):
                for f in range(HT):
                    mm = pe.matmul(ps_F2down, ffn2_w2[:, f, :], g2[:, f, :], start=(f == 0), stop=(f == HT - 1))
                return mm

            @stage(dve, ("F2down", 0))
            def x3(t):
                return dve.scalar_tensor_tensor(x_at(t), ps_F2down, ffn2_b2[:, 0:1], x_at(t), ALU.add, ALU.add)

            @stage(pe, ("x3", 0), ("h3", -1), ("g3", -1), ("q2T", 2),
                   edges=(("h2", 1),))
            def r3(t):
                pe.matmul(ps_r3, leak_wz[:, :], x_at(t), start=True, stop=False)
                return pe.matmul(ps_r3, leak_wh[:, :], h3[:, :], start=False, stop=True)

            @stage(act, ("r3", 0), ("p3", -1))
            def g3_(t):
                return act.activation(g3[:, :], ps_r3, ACT.Tanh, bias=leak_b_half[:, 0:1], scale=0.5)

            @stage(pool, ("x3", 0), ("p3", -1))
            def z_half_(t):
                return pool.tensor_tensor(z_half[:, :], x_at(t), halves[:, :], ALU.mult)

            @stage(pool, ("h3", -1), ("pre3", -1))
            def leaked_(t):
                return pool.tensor_tensor(leaked[:, :], h3[:, :], leak_full[:, :], ALU.mult)

            @stage(dve, ("g3", 0), ("z_half", 0), ("pre3", -1))
            def p3_(t):
                return dve.scalar_tensor_tensor(p3[:, :], g3[:, :], 1.0, z_half[:, :], ALU.add, ALU.mult)

            @stage(dve, ("p3", 0), ("leaked", 0), ("h3", -1))
            def pre3_(t):
                return dve.tensor_tensor(pre3[:, :], p3[:, :], leaked[:, :], ALU.add)

            @stage(act, ("pre3", 0), ("r3", 0), ("leaked", 0), ("h3_prev", -1))
            def h3_(t):
                return act.activation(h3[:, :], pre3[:, :], ACT.Tanh)

            @stage(pool, ("h3", 0), ("h3_prev", -1), ("xr", -1), ("xk", -1))
            def diff_(t):
                return pool.tensor_tensor(diff[:, :], h3[:, :], h3_prev[:, :], ALU.subtract)

            @stage(dve, ("diff", 0), ("rk", -1))
            def xr_(t):
                return dve.scalar_tensor_tensor(xr[:, :], diff[:, :], mu_r[:, 0:1], h3_prev[:, :], ALU.mult, ALU.add)

            @stage(dve, ("diff", 0), ("rk", -1))
            def xk_(t):
                return dve.scalar_tensor_tensor(xk[:, :], diff[:, :], mu_k[:, 0:1], h3_prev[:, :], ALU.mult, ALU.add)

            @stage(pool, ("xr", 0), ("xk", 0))
            def h3_prev_(t):
                return pool.tensor_copy(h3_prev[:, :], h3[:, :])

            @stage(pe, ("xr", 0), ("xk", 0), ("tr", -1), ("kr", -1), ("x2", 3),
                   edges=(("ys", 3),))
            def rk(t):
                pe.matmul(ps_r, ffn3_wr[:, :], xr[:, :], start=True, stop=True)
                return pe.matmul(ps_k, ffn3_wk[:, :], xk[:, :], start=True, stop=True)

            @stage(act, ("rk", 0), ("kk", -1))
            def kr_(t):
                return act.activation(kr[:, :], ps_k, ACT.Relu)

            @stage(act, ("rk", 0), ("o1", -1))
            def tr_(t):
                return act.activation(tr[:, :], ps_r, ACT.Tanh, scale=0.5)

            @stage(pool, ("kr", 0), ("v", -1))
            def kk_(t):
                return pool.tensor_tensor(kk[:, :], kr[:, :], kr[:, :], ALU.mult)

            @stage(pe, ("kk", 0), ("o1", -1), ("v1", 8), ("mx1", 8))
            def v(t):
                return pe.matmul(ps_v, ffn3_wv[:, :], kk[:, :], start=True, stop=True)

            @stage(dve, ("v", 0), ("tr", 0), ("out", -1))
            def o1_(t):
                return dve.scalar_tensor_tensor(o1[:, :], tr[:, :], 1.0, ps_v, ALU.add, ALU.mult)

            @stage(pool, ("o1", 0))
            def out_(t):
                return pool.tensor_tensor(x_at(t), x_at(t), o1[:, :], ALU.add)

            ORDER = [
                ("y_full", 3), ("h3", 8), ("F2down", 7), ("v1", 2), ("r2", 6), ("rk", 9), ("q2", 5), ("v", 10),
                ("x3", 7), ("xq", 2), ("h2", 6), ("gates_h", 0), ("m2w", 5), ("th1", 4), ("kr", 9), ("o1", 10),
                ("leaked", 7), ("tg", 0), ("hs", 4), ("diff", 8), ("V2", 5), ("tr2", 2), ("y_part", 3), ("F2up", 6),
                ("lq", 0), ("q2T", 5), ("kk", 9), ("tr", 9), ("xqT", 2), ("V", 4), ("y", 5), ("g2", 6), ("ys", 5),
                ("r3", 7), ("lp", 0), ("g3", 7), ("z_half", 7), ("tr1", 1), ("xr", 8), ("u", 2), ("F2bias", 5),
                ("cell", 0), ("mx2", 4), ("tc", 0), ("mx1", 1), ("ysT", 5), ("xk", 8), ("z_conv", 3), ("m2", 4),
                ("p3", 7), ("hL", 0), ("m1", 1), ("h3_prev", 8), ("out", 10), ("sc2", 4), ("x2", 5), ("gates_x", -1),
                ("u_sb", 2), ("v2", 4), ("pre3", 7), ("sc1", 1)]
            AHEAD, LAST_LAG = -min(lag for _, lag in ORDER), max(lag for _, lag in ORDER)
            s_out = sem("s_out")

            def iteration(i):
                for name, lag in ORDER:
                    run(name, i - lag)
                t = i - dict(ORDER)["out"]
                if isinstance(t, Lin) or 0 <= t < T:
                    sp.wait_ge(counter["out"], val(t + 1))
                    sp.dma_start(out[:, ds(t, 1), :], x1[:, ds(t, 1), :]).then_inc(s_out, 16)

            FIRST, END = LAST_LAG + 3, T - 1 - AHEAD
            for i in range(-AHEAD, FIRST):
                iteration(i)
            with nc.Fori(0, END - FIRST) as j:
                iteration(Lin(j, 1, FIRST))
            for i in range(END, T + LAST_LAG):
                iteration(i)
            sp.wait_ge(s_out, 16 * T)


def kernel(**inputs):
    import numpy as np
    import concourse.bacc as bacc
    from concourse.bass_utils import run_bass_kernel_spmd

    i = {k: np.asarray(v) for k, v in inputs.items()}
    wr = i["L0_cond_W_router"]
    arrays = {
        "xT": i["x"].transpose(2, 0, 1).reshape(C, TOK),
        "condT": i["cond_1024"].T,
        "wr_x": wr[:, :C].T,
        "wr_t": wr[:, C:].T,
        "router_bias": i["L0_cond_router_bias"],
        "s_w1T": i["L0_cond_s_w1"].reshape(-1, C).T,
        "s_w3T": i["L0_cond_s_w3"].reshape(-1, C).T,
        "s_w2T": i["L0_cond_s_w2"].transpose(0, 2, 1).reshape(HS_TILES, P, C).transpose(1, 0, 2).reshape(P, -1),
        "r_w1T": i["L0_cond_r_w1"].reshape(-1, C).T,
        "r_w2T": i["L0_cond_r_w2"].transpose(2, 0, 1).reshape(P, -1),
        "gate_w": i["L0_ffn_gate_w"],
        "f_w1": i["L0_ffn_w1"].transpose(1, 0, 2),
        "f_w2": i["L0_ffn_w2"].reshape(E, HT, P, C).transpose(2, 0, 1, 3),
    }
    lw, cw = i["L3_cond_W"], i["L1_ffn_conv_w"]

    def column(a):
        return a.reshape(-1, P).T

    def hidden_rows(a):
        return a.T.reshape(HT, P, C).transpose(1, 0, 2)

    arrays.update({
        "lstm_wx": i["L1_cond_Wx"], "lstm_wh": i["L1_cond_Wh"], "lstm_b": i["L1_cond_b"].reshape(4, P),
        "ffn1_w1": i["L1_ffn_w1"].T, "ffn1_w2": hidden_rows(i["L1_ffn_w2"]).reshape(P, -1),
        "conv_w": cw.reshape(HT, P, 3).transpose(1, 0, 2), "conv_b": column(i["L1_ffn_conv_b"]),
        "rnn_wx": i["L2_cond_Wx"], "rnn_wh": i["L2_cond_Wh"], "rnn_b": column(i["L2_cond_b"]),
        "ffn2_w1": i["L2_ffn_W1"].T, "ffn2_b1": i["L2_ffn_b1"].reshape(HT, P),
        "ffn2_w2": hidden_rows(i["L2_ffn_W2"]), "ffn2_b2": column(i["L2_ffn_b2"]),
        "leak_wh": lw[:, :C].T, "leak_wz": lw[:, C:].T, "leak_b": column(i["L3_cond_b"]),
        "alpha": column(i["L3_cond_alpha"]),
        "ffn3_wr": i["L3_ffn_W_r"].T, "ffn3_wk": i["L3_ffn_W_k"].T, "ffn3_wv": i["L3_ffn_W_v"].T,
        "mu_r": column(i["L3_ffn_mu_r"]), "mu_k": column(i["L3_ffn_mu_k"]),
    })
    arrays = {k: np.ascontiguousarray(a) for k, a in arrays.items()}
    nc = bacc.Bacc("TRN2", target_bir_lowering=False, num_devices=1)
    aps = {k: nc.dram_tensor("in_" + k, a.shape, mybir.dt.from_np(a.dtype), kind="ExternalInput").ap() for k, a in arrays.items()}
    out = nc.dram_tensor("outT", (C, T, N), F32, kind="ExternalOutput").ap()
    build_program(nc, aps, out)
    r = run_bass_kernel_spmd(nc, [{"in_" + k: a for k, a in arrays.items()}], core_ids=[0])
    return np.ascontiguousarray(r.results[0]["outT"].transpose(2, 1, 0))
```

```python
from contextlib import ExitStack

import concourse.bass as bass
from concourse import mybir

F32 = mybir.dt.float32
BF16 = mybir.dt.bfloat16
F32R = mybir.dt.float32r
U32 = mybir.dt.uint32
ALU = mybir.AluOpType
ACT = mybir.ActivationFunctionType
X = mybir.AxisListType.X

N, T, C = 128, 32, 128
P = 128
TOK = N * T
NTILE = TOK // P
SEQ_TILE = P // T
E = 8
BANK = 512

HS_TILES = 4
CHUNK = 512
NCHUNK = TOK // CHUNK
TILES_CHUNK = CHUNK // P

CAP = 2 * T // E
H0 = 512
HT = H0 // P
SLOT_TILE = SEQ_TILE * E * CAP
SLOT_E = SEQ_TILE * CAP
GROUPS = 4
TILES_GROUP = NTILE // GROUPS
SLOT_GE = TILES_GROUP * SLOT_E

MAGIC = 1.5 * 2.0 ** 23


class Lin:

    def __init__(self, i, a, b):
        self.i, self.a, self.b = i, a, b

    def __add__(self, n):
        return Lin(self.i, self.a, self.b + n)

    def __sub__(self, n):
        return Lin(self.i, self.a, self.b - n)

    def __mul__(self, n):
        return Lin(self.i, self.a * n, self.b * n)

    __radd__, __rmul__ = __add__, __mul__


def val(x):
    return x.i * x.a + x.b if isinstance(x, Lin) else x


def below(x, n):
    return isinstance(x, int) and x < n


def turn(x):
    return Lin(x.i, x.a // 2, x.b // 2) if isinstance(x, Lin) else x // 2


def ds(start, size):
    return bass.ds(val(start), size)


def build_program(nc, t, out):
    ctx = ExitStack()

    def sb(name, shape, dt=F32):
        return ctx.enter_context(nc.sbuf_tensor(name, shape, dt))

    def sem(name):
        return ctx.enter_context(nc.semaphore(name))

    with ctx:
        pe, act, dve, pool, sp = nc.tensor, nc.scalar, nc.vector, nc.gpsimd, nc.sync
        bank = [ctx.enter_context(nc.psum_tensor(f"bank{i}", [P, BANK], F32)) for i in range(8)]

        xT = sb("xT", [P, TOK])
        x1 = sb("x1", [P, T, N])
        condT = sb("condT", [P, N])
        ident = sb("ident", [P, P])

        lstm_wx, lstm_wh = sb("lstm_wx", [P, 4 * P]), sb("lstm_wh", [P, 4 * P])
        ffn1_w1, ffn1_w2 = sb("ffn1_w1", [P, HT * P], BF16), sb("ffn1_w2", [P, HT, C], BF16)
        ffn2_w1, ffn2_w2 = sb("ffn2_w1", [P, HT * P]), sb("ffn2_w2", [P, HT, C])
        rnn_wx, rnn_wh, leak_wz, leak_wh, ffn3_wr, ffn3_wk, ffn3_wv = (sb(n, [P, P]) for n in (
            "rnn_wx", "rnn_wh", "leak_wz", "leak_wh", "ffn3_wr", "ffn3_wk", "ffn3_wv"))
        rnn_b, ffn2_b2, leak_b, alpha, mu_r, mu_k = (sb(n, [P, 1]) for n in (
            "rnn_b", "ffn2_b2", "leak_b", "alpha", "mu_r", "mu_k"))
        conv_w, conv_b = sb("conv_w", [P, HT, 3]), sb("conv_b", [P, HT])
        lstm_bias, ffn2_bias = sb("lstm_bias", [P, P], BF16), sb("ffn2_bias", [P, P], BF16)
        sel_lstm, sel_rows = sb("sel_lstm", [P, 4 * N], BF16), sb("sel_rows", [P, 4 * N], BF16)
        leak, leak_b_half, half_ws2 = sb("leak", [P, 1]), sb("leak_b_half", [P, 1]), sb("half_ws2", [P, 1])
        wsum, wmean, winv = sb("wsum", [P, 4]), sb("wmean", [P, 4]), sb("winv", [P, 4])
        row_mod = sb("row_mod", [P, 1])
        late = {"lstm_wx": lstm_wx, "lstm_wh": lstm_wh, "ffn1_w1": ffn1_w1, "ffn1_w2": ffn1_w2,
                "ffn2_w1": ffn2_w1, "ffn2_w2": ffn2_w2, "rnn_wx": rnn_wx, "rnn_wh": rnn_wh, "leak_wz": leak_wz,
                "leak_wh": leak_wh, "ffn3_wr": ffn3_wr, "ffn3_wk": ffn3_wk, "ffn3_wv": ffn3_wv, "rnn_b": rnn_b,
                "ffn2_b2": ffn2_b2, "leak_b": leak_b, "alpha": alpha, "mu_r": mu_r, "mu_k": mu_k,
                "conv_w": conv_w, "conv_b": conv_b}

        with ExitStack() as layer0:
            def sb0(name, shape, dt=F32):
                return layer0.enter_context(nc.sbuf_tensor(name, shape, dt))

            wr_x, wr_t = sb0("wr_x", [P, E]), sb0("wr_t", [P, E])
            rbias = sb0("rbias", [P, E])
            gate_w = sb0("gate_w", [P, E])
            w1 = sb0("w1", [P, E, H0])
            w2 = sb0("w2", [P, E, HT, C])
            big = sb0("big", [P, E * N * CAP])
            W_MOE = HS_TILES * P
            sw1, sw3, rw1 = big[:, 0:W_MOE], big[:, W_MOE:2 * W_MOE], big[:, 2 * W_MOE:2 * W_MOE + E * P]
            sw2, rw2 = big[:, 4 * W_MOE:5 * W_MOE], big[:, 5 * W_MOE:5 * W_MOE + E * P]
            gate_rows = [big[:, k * CHUNK * E:(k + 1) * CHUNK * E].rearrange("p (i e k) -> p i e k", i=TILES_CHUNK, e=E)
                         for k in range(2)]
            ctok = sb0("ctok", [P, NTILE, C])

            x1_flat = x1[:, :, :].rearrange("p t n -> p (t n)")
            w2_raw, w1_raw = x1_flat[:, 2048:2560], x1_flat[:, 3520:4032]
            group_of = x1_flat[:, 2560:3072]
            scratch = x1_flat[:, 3072:3328].rearrange("p (k n) -> p k n", k=2)
            ones = x1_flat[:, 3328:3456]
            part_bf = x1_flat[:, 3456:3520].bitcast(BF16)

            g_dram = nc.dram_tensor("gates_scratch", [NTILE * E, P], F32, kind="Internal").ap()
            v_dram = nc.dram_tensor("topv_scratch", [NTILE, SLOT_TILE], F32, kind="Internal").ap()
            i_dram = nc.dram_tensor("topi_scratch", [NTILE, SLOT_TILE], F32, kind="Internal").ap()

            s_small, s_x = sem("s_small"), [sem(f"s_xin{i}") for i in range(4)]
            s_wmoe, s_gw, s_wffn, s_sw2 = [sem(f"s_wmoe{k}") for k in range(5)], sem("s_gw"), sem("s_wffn"), sem("s_sw2")
            small = [(wr_x[:, :], t["wr_x"]), (wr_t[:, :], t["wr_t"]), (condT[:, :], t["condT"]),
                     (rbias[:, :], t["router_bias"].partition_broadcast(P))]
            def load_x(i):
                sp.dma_start(xT[:, i * 1024:(i + 1) * 1024], t["xT"][:, i * 1024:(i + 1) * 1024]).then_inc(s_x[i], 16)

            def load_small(k):
                sp.dma_start(*small[k]).then_inc(s_small, 16)

            load_small(0)
            load_x(0)
            for k in (1, 2, 3):
                load_small(k)
            for i in (1, 2, 3):
                load_x(i)
            moe = [(sw1, t["s_w1T"]), (sw3, t["s_w3T"]), (sw2, t["s_w2T"]), (rw1, t["r_w1T"]), (rw2, t["r_w2T"])]
            for (dst, src), done in zip(moe, s_wmoe):
                sp.dma_start(dst[:, :], src).then_inc(done, 16)
            sp.dma_start(gate_w[:, :], t["gate_w"]).then_inc(s_gw, 16)

            s_id = sem("s_id")
            iota_tok = sb0("iota_tok", [P, P])
            part = sb0("part", [P, 1])
            seq_off = sb0("seq_off", [P, 2, SEQ_TILE, CAP])
            pool.memset(ident[:, :], 0.0).then_inc(s_id, 1)
            pool.wait_ge(s_id, val(1))
            pool.affine_select(out=ident[:, :], in_=ident[:, :], compare_op=ALU.not_equal, fill=1.0,
                               base=0, pattern=[[-1, P]], channel_multiplier=1).then_inc(s_id, 1)
            pool.iota(iota_tok[:, :], [[1, P]], base=0, channel_multiplier=0,
                      allow_small_or_imprecise_dtypes=True).then_inc(s_id, 1)
            pool.iota(part[:, :], [[0, 1]], base=0, channel_multiplier=1,
                      allow_small_or_imprecise_dtypes=True).then_inc(s_id, 1)
            pool.iota(seq_off[:, :, :, :], [[0, 2], [T, SEQ_TILE], [0, CAP]], base=0, channel_multiplier=0,
                      allow_small_or_imprecise_dtypes=True).then_inc(s_id, 1)
            ID_READY, CONSTS_READY = 2, 5

            s_w1, s_prep, s_pw = sem("s_w1"), sem("s_prep"), sem("s_pw")
            for name, dst in late.items():
                if name not in ("ffn1_w1", "ffn1_w2"):
                    sp.dma_start(dst[:, :] if len(dst.shape) == 2 else dst[:, :, :], t[name]).then_inc(s_w1, 16)
            sp.dma_start(w1_raw, t["ffn1_w1"]).then_inc(s_w1, 16)
            sp.dma_start(w2_raw, t["ffn1_w2"]).then_inc(s_w1, 16)
            n_pool = [0]

            def prep_pool(ins):
                n_pool[0] += 1
                ins.then_inc(s_pw, 1)

            rows_lstm, rows_ffn2 = scratch[:, 0, :], scratch[:, 1, :]
            for r in (rows_lstm, rows_ffn2):
                prep_pool(pool.memset(r, 0.0))
            prep_pool(pool.memset(row_mod[:, :], 99.0))
            prep_pool(pool.iota(group_of, [[1, 4], [0, N]], base=0, channel_multiplier=0,
                                allow_small_or_imprecise_dtypes=True))
            prep_pool(pool.memset(ones[:, :], 1.0))
            pool.wait_ge(s_pw, n_pool[0])
            for k in range(3):
                prep_pool(pool.iota(row_mod[32 * k:32 * k + 32, :], [[0, 1]], base=0, channel_multiplier=1,
                                    allow_small_or_imprecise_dtypes=True))
            pool.wait_ge(s_pw, n_pool[0])
            sp.wait_ge(s_pw, n_pool[0])
            for k in range(3):
                sp.dma_start(rows_lstm[32 * k:32 * k + 4, :], t["lstm_b"]).then_inc(s_w1, 16)
                sp.dma_start(rows_ffn2[32 * k:32 * k + 4, :], t["ffn2_b1"]).then_inc(s_w1, 16)
            n_late = 16 * (len(late) + 6)

            step_p, step_s = [0], [0]
            s_sum = sem("s_sum")

            def dve_p(ins):
                step_s[0] += 1
                ins.then_inc(s_sum, 1)
                dve.wait_ge(s_sum, step_s[0])

            def pool_p(ins):
                step_p[0] += 1
                ins.then_inc(s_prep, 1)
                pool.wait_ge(s_prep, step_p[0])

            ternary = [(w1_raw, ffn1_w1[:, :], 1e-5), (w2_raw, ffn1_w2[:, :, :].rearrange("p f c -> p (f c)"), 1e-5),
                       (ffn2_w1[:, :], ffn2_w1[:, :], 1e-8),
                       (ffn2_w2[:, :, :].rearrange("p f c -> p (f c)"), ffn2_w2[:, :, :].rearrange("p f c -> p (f c)"), 1e-8)]

            def weight_sums():
                dve.wait_ge(s_w1, n_late)
                for k, (w, _, _) in enumerate(ternary):
                    dve_p(dve.tensor_reduce(wsum[:, k:k + 1], w, X, ALU.add, apply_absolute_value=True))

            def weight_total():
                pe.wait_ge(s_pw, n_pool[0])
                pe.wait_ge(s_sum, len(ternary))
                pe.matmul(bank[7][:, 2 * P:2 * P + 4], ones[:, :], wsum[:, :], start=True, stop=True).then_inc(s_pw, 1)

            def weight_means():
                dve.wait_ge(s_pw, n_pool[0] + 1)
                for k, (_, _, floor) in enumerate(ternary):
                    dve_p(dve.tensor_scalar(wmean[:, k:k + 1], bank[7][:, 2 * P + k:2 * P + k + 1], 1.0 / (HT * P * P),
                                            floor, ALU.mult, ALU.max))
                dve_p(dve.reciprocal(winv[:, :], wmean[:, :]))

            MEANS = 2 * len(ternary) + 1

            def prepare_weights():
                pool.wait_ge(s_sum, MEANS)
                pool.wait_ge(s_w1, n_late)
                for k, (w, dst, _) in enumerate(ternary):
                    pool_p(pool.tensor_scalar(w, w, winv[:, k:k + 1], MAGIC, ALU.mult, ALU.add))
                    pool_p(pool.tensor_scalar(w, w, MAGIC, 1.0, ALU.subtract, ALU.min))
                    pool_p(pool.tensor_scalar(dst, w, -1.0, None, ALU.max))
                pool_p(pool.tensor_scalar(half_ws2[:, :], wmean[:, 1:2], 0.5, None, ALU.mult))
                pool_p(pool.tensor_scalar(conv_w[:, :, :], conv_w[:, :, :], wmean[:, 0:1], 0.5, ALU.mult, ALU.mult))
                pool_p(pool.tensor_scalar(lstm_wh[:, 0:3 * P], lstm_wh[:, 0:3 * P], 0.5, None, ALU.mult))
                pool_p(pool.tensor_scalar(lstm_wx[:, 3 * P:4 * P], lstm_wx[:, 3 * P:4 * P], 2.0, None, ALU.mult))
                pool_p(pool.tensor_scalar(ffn3_wv[:, :], ffn3_wv[:, :], 0.5, None, ALU.mult))
                pool_p(pool.tensor_scalar(leak_b_half[:, :], leak_b[:, :], 0.5, None, ALU.mult))
                pool_p(pool.tensor_scalar(leak[:, :], alpha[:, :], -1.0, 1.0, ALU.mult, ALU.add))
                pool_p(pool.tensor_scalar(sel_rows[:, :], group_of, row_mod[:, 0:1], None, ALU.is_equal))
                pool_p(pool.tensor_copy(sel_lstm[:, 0:3 * N], sel_rows[:, 0:3 * N]))
                pool_p(pool.tensor_scalar(sel_lstm[:, 3 * N:4 * N], sel_rows[:, 3 * N:4 * N], 2.0, None, ALU.mult))
                for rows, dst in ((rows_lstm, lstm_bias), (rows_ffn2, ffn2_bias)):
                    pool_p(pool.tensor_scalar(dst[96:128, :], rows[96:128, :], 1.0, None, ALU.mult))
                    pool_p(pool.tensor_copy(part_bf, rows))
                    pool_p(pool.tensor_copy(dst[0:32, :], part_bf[0:32, :]))
                    pool_p(pool.tensor_tensor(rows, rows, part_bf, ALU.subtract))
                    pool_p(pool.tensor_copy(part_bf, rows))
                    pool_p(pool.tensor_copy(dst[32:64, :], part_bf[32:64, :]))
                    pool_p(pool.tensor_tensor(rows, rows, part_bf, ALU.subtract))
                    pool_p(pool.tensor_copy(dst[64:96, :], rows[64:96, :]))

            cst = x1_flat[:, 1024:1536]
            th = [sb0(f"th{k}", [P, CHUNK]) for k in range(2)]
            pb = [sb0(f"pb{k}", [P, CHUNK]) for k in range(2)]
            gl = [x1_flat[:, k * CHUNK:(k + 1) * CHUNK] for k in range(2)]
            hidden = [sb0(f"hidden{k}", [P, CHUNK]) for k in range(3)]
            score = sb0("score", [P, NTILE, E])
            sig = sb0("sig", [P, NTILE, E])
            sel = sb0("sel", [P, NTILE, E])
            rank = sb0("rank", [P, NTILE, E])
            den, dpos, half_w = sb0("den", [P, NTILE, 1]), sb0("dpos", [P, NTILE, 1]), sb0("half_w", [P, NTILE, 1])
            gates = sb0("gates", [P, NTILE, E])
            gatesT = sb0("gatesT", [P, 2, P])
            smax, ssum = sb0("smax", [P, NTILE, 1]), sb0("ssum", [P, NTILE, 1])
            probT = sb0("probT", [P, 2, P])
            topv = sb0("topv", [P, 2, SEQ_TILE, CAP])
            topi = sb0("topi", [P, 2, SEQ_TILE, CAP], U32)
            topf = sb0("topf", [P, 2, SEQ_TILE, CAP])
            slot_rows = [[sb0(f"slot_rows{h}{k}", [NTILE, P]) for k in range(2)] for h in range(2)]
            slot_cols = sb0("slot_cols", [P, 2, 2 * NTILE])

            stage_b = layer0.enter_context(ExitStack())

            def sbb(name, shape, dt=F32):
                return stage_b.enter_context(nc.sbuf_tensor(name, shape, dt))

            sw1_hl, sw3_hl = ([sbb(f"{n}_{k}", [P, W_MOE], F32R) for k in ("high", "low")] for n in ("sw1", "sw3"))
            rw1_hl = [sbb(f"rw1_{k}", [P, E * P], F32R) for k in ("high", "low")]
            sw2_hl = [sbb(f"sw2_{k}", [P, W_MOE], F32R) for k in ("high", "low")]
            rw2_hl = [sbb(f"rw2_{k}", [P, E * P], F32R) for k in ("high", "low")]
            hidden_hl = [[sbb(f"hidden{u}_{k}", [P, CHUNK], F32R) for k in ("high", "low")] for u in range(3)]
            x_hl = [[sbb(f"x{par}_{k}", [P, CHUNK], F32R) for k in ("high", "low")] for par in range(2)]
            s_split, s_whi, s_xs = sem("s_split"), sem("s_whi"), sem("s_xs")

            def split(hl, src, done, count):
                high, low = hl
                dve.tensor_copy(high[:, :], src).then_inc(done, 1)
                dve.wait_ge(done, val(count))
                return dve.tensor_tensor(low[:, :], src, high[:, :].bitcast(F32), ALU.subtract).then_inc(done, 1)

            def split_chunk(c, par):
                if not below(c, 2):
                    dve.wait_ge(s_r, val((c - 1) * NRO))
                split(x_hl[par], xT[:, ds(c * CHUNK, CHUNK)], s_xs, 2 * c + 1)

            def product(dst, w_hl, cols, v_hl, start, stop):
                (wh, wl), (vh, vl) = w_hl, v_hl
                pe.matmul(dst, wh[:, cols], vh[:, :], start=start, stop=False)
                pe.matmul(dst, wh[:, cols], vl[:, :], start=False, stop=False)
                return pe.matmul(dst, wl[:, cols], vh[:, :], start=False, stop=stop)

            s_ab, s_th, s_p, s_q = sem("s_ab"), sem("s_th"), sem("s_p"), sem("s_q")
            s_r, s_gelu, s_gg = sem("s_r"), sem("s_gelu"), sem("s_gg")
            s_hi, s_lo, s_down = sem("s_hi"), sem("s_lo"), sem("s_down")
            s_gr, s_acc, s_tr, s_ct, s_sc, s_sce = ([sem("s_gr0"), sem("s_gr1")], sem("s_acc"), sem("s_tr"), sem("s_ct"),
                                                    sem("s_sc"), sem("s_sce"))
            NSH, NRO = HS_TILES, E
            UNITS = [u for j in range(NSH) for u in (("sh", j), ("ro", 2 * j), ("ro", 2 * j + 1))]
            FIRST_UNITS = [("sh", j) for j in range(NSH)] + [("ro", j) for j in range(NRO)]
            NUNITS, LEAD_B, LEAD = len(UNITS), 3, 2
            ab_bank, r_bank, acc_bank = [(bank[0], bank[1]), (bank[2], bank[3])], bank[4:6], bank[6:8]

            def first_products(c, par, unit, last=False):
                kind, j = unit
                cols = slice(j * P, (j + 1) * P)
                if unit == UNITS[0]:
                    pe.wait_ge(s_xs, val(2 * c + 2))
                if kind == "sh":
                    k = c * NSH + j
                    for b, w in zip(ab_bank[j % 2], (sw1_hl, sw3_hl)):
                        if b is ab_bank[j % 2][0] and not (below(c, 1) and j < 2):
                            pe.wait_ge(s_q, val(k - 1))
                        product(b[:, :], w, cols, x_hl[par], True, True).then_inc(s_ab, 1)
                else:
                    k = c * NRO + j
                    if not (below(c, 1) and j < 2):
                        pe.wait_ge(s_gelu, val(k - 1))
                    else:
                        pe.wait_ge(s_aa, 2)
                    product(r_bank[j % 2][:, :], rw1_hl, cols, x_hl[par], True, True).then_inc(s_r, 1)

            s_gr_first = [sem(f"s_gr_first{k}") for k in range(NRO // 2)]

            def hidden_free(c, u):
                if not (below(c, 1) and u < 3):
                    dve.wait_ge(s_lo, val(c * NUNITS + (u - 2)))

            def hidden_high(c, u, unit):
                kind, j = unit
                if kind == "sh":
                    act.wait_ge(s_q, val(c * NSH + j + 1))
                else:
                    act.wait_ge(s_gg, val(c * NRO + j + 1))
                if not (below(c, 1) and u < 3):
                    act.wait_ge(s_down, val(c * NUNITS + (u - 2)))
                act.copy(hidden_hl[u % 3][0][:, :], hidden[u % 3][:, :]).then_inc(s_hi, 1)

            def hidden_low(c, u):
                pool.wait_ge(s_hi, val(c * NUNITS + (u + 1)))
                pool.tensor_tensor(hidden_hl[u % 3][1][:, :], hidden[u % 3][:, :], hidden_hl[u % 3][0][:, :].bitcast(F32),
                                   ALU.subtract).then_inc(s_lo, 1)

            def second_product(c, par, u, unit):
                kind, j = unit
                if u == 0 and not (below(c, 2)):
                    pe.wait_ge(s_sce, val(c - 1))
                pe.wait_ge(s_lo, val(c * NUNITS + (u + 1)))
                product(acc_bank[par][:, :], sw2_hl if kind == "sh" else rw2_hl, slice(j * P, (j + 1) * P),
                        hidden_hl[u % 3], u == 0, u == NUNITS - 1).then_inc(s_down, 1)

            def chunk_transposes(c, par):
                pe.wait_ge(s_acc, val(c + 1))
                for i in range(TILES_CHUNK):
                    mm = pe.transpose(acc_bank[par][:, i * P:(i + 1) * P], cst[:, i * P:(i + 1) * P], ident[:, :])
                mm.then_inc(s_tr, 1)

            def chunk_scores(c, par, last=False):
                if not last:
                    pe.wait_ge(s_ct, val(c + 1))
                dst = bank[0] if last else acc_bank[par]
                for i in range(TILES_CHUNK):
                    mm = pe.matmul(dst[:, i * E:(i + 1) * E], cst[:, i * P:(i + 1) * P], gate_w[:, :],
                                   start=True, stop=True)
                mm.then_inc(s_sc, 1)

            def chunk_evacuate(c, par):
                act.wait_ge(s_down, val((c + 1) * NUNITS))
                if not (below(c, 1)):
                    act.wait_ge(s_sc, val(c))
                act.copy(cst[:, :], acc_bank[par][:, :]).then_inc(s_acc, 1)

            def chunk_store_tokens(c, par):
                dve.wait_ge(s_tr, val(c + 1))
                dve.tensor_copy(ctok[:, ds(c * TILES_CHUNK, TILES_CHUNK), :].rearrange("p i k -> p (i k)"),
                                acc_bank[par][:, :]).then_inc(s_ct, 1)

            def chunk_store_scores(c, par, last=False):
                src = bank[0] if last else acc_bank[par]
                dve.wait_ge(s_sc, val(c + 1))
                dve.tensor_copy(score[:, ds(c * TILES_CHUNK, TILES_CHUNK), :].rearrange("p i k -> p (i k)"),
                                src[:, 0:TILES_CHUNK * E]).then_inc(s_sce, 1)

            def load_gate_rows(c, par):
                if not (below(c, 2)):
                    sp.wait_ge(s_gg, val((c - 1) * NRO))
                src = g_dram[ds(c * TILES_CHUNK * E, TILES_CHUNK * E), :].rearrange("r k -> (r k)")
                sp.dma_start(gate_rows[par].rearrange("p i e k -> p (i e k)"),
                             src.partition_broadcast(P)).then_inc(s_gr[par], 16)

            def shared_on_vector(c, u, j):
                k = c * NSH + j
                dve.wait_ge(s_th, val(k + 1))
                dve.scalar_tensor_tensor(pb[j % 2][:, :], th[j % 2][:, :], 1.0, ab_bank[j % 2][0][:, :],
                                         ALU.add, ALU.mult).then_inc(s_p, 1)
                dve.wait_ge(s_p, val(k + 1))
                dve.wait_ge(s_ab, val(2 * k + 2))
                hidden_free(c, u)
                dve.tensor_tensor(hidden[u % 3][:, :], pb[j % 2][:, :], ab_bank[j % 2][1][:, :], ALU.mult).then_inc(s_q, 1)

            def chunk(c, par, first=False, last=False):
                n = len(UNITS)
                units = FIRST_UNITS if first else UNITS
                for u in range(n):
                    if first and u in (0, 1, 4):
                        pe.wait_ge(s_split, {0: 3, 1: 4, 4: 5}[u])
                    if u + LEAD_B < n:
                        first_products(c, par, units[u + LEAD_B])
                    elif not last:
                        first_products(c + 1, 1 - par, UNITS[u + LEAD_B - n])
                    second_product(c, par, u, units[u])
                    if first and u == 0:
                        pe.wait_ge(s_da, val(GATES_READY))
                        for h in range(2):
                            pe.transpose(bank[7][:, h * P:(h + 1) * P], gates_flat[:, h * P:(h + 1) * P],
                                         ident[:, :]).then_inc(s_pa, 1)
                    if first and u == 8:
                        weight_total()
                    if not first and u == 4:
                        chunk_transposes(c - 1, 1 - par)
                    if last and u == 7:
                        pe.wait_ge(s_ct, val(c))
                        choice_transpose(0, acc_bank[1 - par][:, P:2 * P])
                    if not first and u == 7:
                        chunk_scores(c - 1, 1 - par)
                if first:
                    pe.wait_ge(s_sum, MEANS)
                for u, (kind, j) in enumerate(units):
                    if kind == "sh":
                        k = c * NSH + j
                        act.wait_ge(s_ab, val(2 * k + 1))
                        if not (first and j < 2):
                            act.wait_ge(s_p, val(k - 1))
                        act.activation(th[j % 2][:, :], ab_bank[j % 2][0][:, :], ACT.Tanh, scale=0.5).then_inc(s_th, 1)
                    else:
                        k = c * NRO + j
                        act.wait_ge(s_r, val(k + 1))
                        if not (first and j < 2):
                            act.wait_ge(s_gg, val(k - 1))
                        act.activation(gl[j % 2][:, :], r_bank[j % 2][:, :], ACT.Gelu).then_inc(s_gelu, 1)
                    if u:
                        hidden_high(c, u - 1, units[u - 1])
                        if first and u < 3:
                            split_moe(u + 2)
                    elif not first:
                        hidden_high(c - 1, n - 1, UNITS[n - 1])
                    if not first and u == 2:
                        chunk_evacuate(c - 1, 1 - par)
                    if last and u == 3:
                        choice_exp(0)
                    if first and u == 2:
                        act.wait_ge(s_pa, val(7))
                        act.copy(gatesT[:, :, :].rearrange("p h k -> p (h k)"), bank[7][:, 0:2 * P]).then_inc(s_aa, 1)
                        sp.wait_ge(s_aa, val(3))
                        for h in range(2):
                            sp.dma_start(g_dram[h * P:(h + 1) * P, :], gatesT[:, h, :]).then_inc(s_ga, 16)
                        sp.wait_ge(s_ga, val(32))
                        sp.wait_ge(s_split, 5)
                        for e in range(0, NRO, 2):
                            for i in range(TILES_CHUNK):
                                src = g_dram[i * E + e:i * E + e + 2, :].rearrange("r k -> (r k)")
                                sp.dma_start(gate_rows[0][:, i, e:e + 2, :].rearrange("p e k -> p (e k)"),
                                             src.partition_broadcast(P)).then_inc(s_gr_first[e // 2], 16)
                if last:
                    hidden_high(c, n - 1, units[n - 1])
                for u in range(n):
                    hidden_low(c, u)
                    if first and u < 2:
                        split_moe_low(u + 3)
                for u, (kind, j) in enumerate(units):
                    if kind == "sh":
                        if not (first and j < 3):
                            shared_on_vector(c, u, j)
                    else:
                        k = c * NRO + j
                        dve.wait_ge(s_gelu, val(k + 1))
                        if first and j % 2 == 0:
                            dve.wait_ge(s_gr_first[j // 2], 16 * TILES_CHUNK)
                        elif j == 0:
                            dve.wait_ge(s_gr[par], val(16 * turn(c) if par == 0 else 16 * (turn(c) + 1)))
                        hidden_free(c, u)
                        dve.tensor_tensor(hidden[u % 3][:, :].rearrange("p (i k) -> p i k", k=P),
                                          gl[j % 2][:, :].rearrange("p (i k) -> p i k", k=P),
                                          gate_rows[par][:, :, j, :], ALU.mult).then_inc(s_gg, 1)
                    if u == (8 if first else 3) and not last:
                        split_chunk(c + 1, 1 - par)
                    if first and u == 6:
                        weight_sums()
                    if first and u == 10:
                        weight_means()
                    if not first and u == 6:
                        chunk_store_tokens(c - 1, 1 - par)
                    if not first and u == 9:
                        chunk_store_scores(c - 1, 1 - par)
                    if last and u == 1:
                        choice_scores(0)
                    if last and u == 5:
                        choice_probs(0)
                    if last and u >= 9:
                        choice_tables(0, acc_bank[1 - par][:, P:2 * P], {9: (0,), 10: (1,), 11: (2, 3)}[u])
                if not last:
                    load_gate_rows(c + 1, 1 - par)
                sp.dma_start(w1[:, ds(c, 1), :], t["f_w1"][:, ds(c, 1), :]).then_inc(s_wffn, 16)
                sp.dma_start(w2[:, ds(c, 1), :, :], t["f_w2"][:, ds(c, 1), :, :]).then_inc(s_wffn, 16)

            s_pad, s_pa, s_aa, s_da, s_ga = sem("s_pad"), sem("s_pa"), sem("s_aa"), sem("s_da"), sem("s_ga")
            ctok_flat = ctok[:, :, :].rearrange("p i c -> p (i c)")
            PAD = 4 * (P + 32)
            wrx_pad, wrt_pad = ctok_flat[:, 0:PAD], ctok_flat[:, PAD:2 * PAD]
            cond_logit = ctok_flat[:, 2 * PAD:2 * PAD + 32]
            logit = [ctok_flat[:, 2048 + g * CHUNK:2048 + (g + 1) * CHUNK] for g in range(2)]
            dve.memset(ctok_flat[:, 0:2 * PAD], 0.0).then_inc(s_pad, 1)
            dve.wait_ge(s_pad, 1)
            dve.wait_ge(s_small, val(16 * len(small)))
            for pad, w in ((wrx_pad, wr_x), (wrt_pad, wr_t)):
                dve.tensor_copy(pad.rearrange("p (k s) -> p k s", k=4)[:, :, 0:E],
                                w[:, :].rearrange("p (o e) -> p o e", o=1).to_broadcast([P, 4, E])).then_inc(s_pad, 1)
            pe.wait_ge(s_pad, 3)
            pe.wait_ge(s_small, val(16 * len(small)))
            SEQ_CHUNK = CHUNK // T
            for g in range(2):
                for k in range(4):
                    c = 4 * g + k
                    mm = pe.matmul(bank[2][:, g * SEQ_CHUNK:(g + 1) * SEQ_CHUNK], wrt_pad[:, k * P:(k + 1) * P],
                                   condT[:, c * SEQ_CHUNK:(c + 1) * SEQ_CHUNK], start=(k == 0), stop=(k == 3))
            mm.then_inc(s_pa, 1)
            for g in range(2):
                for k in range(4):
                    c = 4 * g + k
                    if c % 2 == 0:
                        pe.wait_ge(s_x[c // 2], 16)
                    mm = pe.matmul(bank[g][:, :], wrx_pad[:, k * P:(k + 1) * P], xT[:, c * CHUNK:(c + 1) * CHUNK],
                                   start=(k == 0), stop=(k == 3))
                mm.then_inc(s_pa, 1)
            dve.wait_ge(s_x[0], 16)
            split_chunk(0, 0)
            dve.wait_ge(s_pa, 1)
            dve.tensor_copy(cond_logit, bank[2][:, 0:2 * SEQ_CHUNK]).then_inc(s_pad, 1)
            dve.wait_ge(s_pad, 4)
            pe.wait_ge(s_id, val(ID_READY))
            for g in range(2):
                dve.wait_ge(s_pa, 2 + g)
                dve.tensor_tensor(logit[g].rearrange("p (s k) -> p s k", k=T), bank[g][:, :].rearrange("p (s k) -> p s k", k=T),
                                  cond_logit[:, g * SEQ_CHUNK:(g + 1) * SEQ_CHUNK].rearrange("p (s o) -> p s o", o=1)
                                  .to_broadcast([P, SEQ_CHUNK, T]), ALU.add).then_inc(s_pad, 1)
                pe.wait_ge(s_pad, 5 + g)
                for q in range(TILES_CHUNK):
                    mm = pe.transpose(bank[4 + g][:, q * P:(q + 1) * P], logit[g][:, q * P:(q + 1) * P], ident[:, :])
                mm.then_inc(s_pa, 1)

            cmp = x1_flat[:, 0:NTILE * E * E].rearrange("p (i e f) -> p i e f", i=NTILE, e=E)
            all3 = [P, NTILE, E]

            for g in range(2):
                act.wait_ge(s_pa, 4 + g)
                act.activation(sig[:, 16 * g:16 * (g + 1), :].rearrange("p (k q) e -> p q k e", k=4),
                               bank[4 + g][:, :].rearrange("p (q k s) -> p q k s", q=4, k=4)[:, :, :, 0:E],
                               ACT.Exp, scale=-1.0).then_inc(s_aa, 1)

            MOE = ((sw1_hl, sw1), (sw3_hl, sw3), (sw2_hl, sw2), (rw1_hl, rw1), (rw2_hl, rw2))

            def split_moe(k):
                hl, w = MOE[k]
                act.wait_ge(s_wmoe[k], 16)
                if hl is sw2_hl:
                    act.mul(w[:, :], w[:, :], 1.0 / 16.0).then_inc(s_sw2, 1)
                    act.wait_ge(s_sw2, 1)
                act.copy(hl[0][:, :], w[:, :]).then_inc(s_whi, 1)

            def split_moe_low(k):
                hl, w = MOE[k]
                pool.wait_ge(s_wmoe[k], 16)
                pool.wait_ge(s_whi, k + 1)
                pool.tensor_tensor(hl[1][:, :], w[:, :], hl[0][:, :].bitcast(F32), ALU.subtract).then_inc(s_split, 1)

            for k in range(3):
                split_moe(k)
                split_moe_low(k)

            step_a = [0]

            def dve_a(ins):
                step_a[0] += 1
                ins.then_inc(s_da, 1)
                dve.wait_ge(s_da, val(step_a[0]))

            dve.wait_ge(s_aa, val(2))
            dve_a(dve.tensor_scalar(sig[:, :, :], sig[:, :, :], 1.0, None, ALU.add))
            dve_a(dve.reciprocal(sig[:, :, :], sig[:, :, :]))
            dve.wait_ge(s_small, val(16 * len(small)))
            dve_a(dve.tensor_tensor(sel[:, :, :], sig[:, :, :],
                                    rbias[:, :].rearrange("p (o e) -> p o e", o=1).to_broadcast(all3), ALU.add))
            for e in range(E):
                if e:
                    dve.tensor_tensor(cmp[:, :, e, 0:e], sel[:, :, 0:e], sel[:, :, e:e + 1].to_broadcast([P, NTILE, e]),
                                      ALU.is_ge).then_inc(s_da, 1)
                    step_a[0] += 1
                last = dve.tensor_tensor(cmp[:, :, e, e:E], sel[:, :, e:E],
                                         sel[:, :, e:e + 1].to_broadcast([P, NTILE, E - e]), ALU.is_gt)
                if e < E - 1:
                    last.then_inc(s_da, 1)
                    step_a[0] += 1
            dve_a(last)
            shared_on_vector(0, 0, 0)
            dve_a(dve.tensor_reduce(rank[:, :, :], cmp[:, :, :, :], X, ALU.add))
            dve_a(dve.tensor_scalar(rank[:, :, :], rank[:, :, :], 1.5, None, ALU.is_lt))
            dve_a(dve.tensor_tensor(gates[:, :, :], sig[:, :, :], rank[:, :, :], ALU.mult))
            dve_a(dve.tensor_reduce(den[:, :, :], gates[:, :, :], X, ALU.add))
            shared_on_vector(0, 1, 1)
            dve_a(dve.tensor_scalar(dpos[:, :, :], den[:, :, :], 1e-9, 0.25, ALU.is_gt, ALU.mult))
            dve_a(dve.tensor_scalar(den[:, :, :], den[:, :, :], 1e-9, None, ALU.add))
            dve_a(dve.reciprocal(den[:, :, :], den[:, :, :]))
            dve_a(dve.tensor_tensor(den[:, :, :], den[:, :, :], dpos[:, :, :], ALU.mult))
            dve_a(dve.tensor_scalar(half_w[:, :, :], dpos[:, :, :], -0.5, 0.125, ALU.mult, ALU.add))
            dve_a(dve.tensor_tensor(gates[:, :, :], gates[:, :, :], den[:, :, :].to_broadcast(all3), ALU.mult))
            dve_a(dve.tensor_tensor(rank[:, :, :], rank[:, :, :], half_w[:, :, :].to_broadcast(all3), ALU.mult))
            dve_a(dve.tensor_tensor(gates[:, :, :], gates[:, :, :], rank[:, :, :], ALU.add))
            s_dc, s_ac, s_pc, s_vc = sem("s_dc"), sem("s_ac"), sem("s_pc"), sem("s_vc")
            s_sr, s_srt, s_slots = sem("s_sr"), sem("s_srt"), sem("s_slots")
            HALF = NTILE // 2
            SCORES, PROBS, TURNED, TABLES = 2, 5, 6, 16
            step_c = [0]

            def dve_c(ins):
                step_c[0] += 1
                ins.then_inc(s_dc, 1)
                dve.wait_ge(s_dc, val(step_c[0]))

            def tiles_of(a, h):
                return a[:, h * HALF:(h + 1) * HALF, :]

            def choice_scores(h):
                dve.wait_ge(s_sce, (h + 1) * NCHUNK // 2)
                sc, mx = tiles_of(score, h), tiles_of(smax, h)
                dve_c(dve.tensor_reduce(mx, sc, X, ALU.max))
                dve_c(dve.tensor_tensor(sc, sc, mx.to_broadcast([P, HALF, E]), ALU.subtract))

            def choice_exp(h):
                act.wait_ge(s_dc, h * TABLES + SCORES)
                act.activation(tiles_of(sel, h).rearrange("p i e -> p (i e)"),
                               tiles_of(score, h).rearrange("p i e -> p (i e)"), ACT.Exp).then_inc(s_ac, 1)

            def choice_probs(h):
                ex, sm = tiles_of(sel, h), tiles_of(ssum, h)
                dve.wait_ge(s_ac, h + 1)
                dve_c(dve.tensor_reduce(sm, ex, X, ALU.add))
                dve_c(dve.reciprocal(sm, sm))
                dve_c(dve.tensor_tensor(ex, ex, sm.to_broadcast([P, HALF, E]), ALU.mult))

            def choice_transpose(h, dst):
                pe.wait_ge(s_dc, h * TABLES + PROBS)
                pe.transpose(dst[:, 0:P], tiles_of(sel, h).rearrange("p i e -> p (i e)"), ident[:, :]).then_inc(s_pc, 1)

            def choice_tables(h, src, sequences=range(SEQ_TILE)):
                if 0 in sequences:
                    dve.wait_ge(s_pc, h + 1)
                    dve_c(dve.tensor_copy(probT[:, h, :], src[:, 0:P]))
                for b in sequences:
                    seq = probT[:, h, b * T:(b + 1) * T]
                    dve_c(dve.max(topv[:, h, b, :], seq))
                    dve.max_index(topi[:, h, b, :], topv[:, h, b, :], seq).then_inc(s_dc, 1)
                    step_c[0] += 1
                if SEQ_TILE - 1 not in sequences:
                    return
                dve.wait_ge(s_dc, val(step_c[0]))
                dve.wait_ge(s_id, val(CONSTS_READY))
                dve_c(dve.tensor_copy(topf[:, h, :, :], topi[:, h, :, :]))
                dve_c(dve.tensor_tensor(topf[:, h, :, :], topf[:, h, :, :], seq_off[:, h, :, :], ALU.add))
                assert step_c[0] == (h + 1) * TABLES

            def choice_store(h):
                sp.wait_ge(s_dc, (h + 1) * TABLES)
                for dram, src in ((i_dram, topf), (v_dram, topv)):
                    sp.dma_start(dram.rearrange("i (e k) -> (i e) k", e=E)[h * P:(h + 1) * P, :],
                                 src[:, h, :, :].rearrange("p b j -> p (b j)")).then_inc(s_vc, 16)

            def load_slots(h):
                for k, dram in enumerate((i_dram, v_dram)):
                    rows = dram.rearrange("i (u k) -> (i u) k", u=2)[h * NTILE:(h + 1) * NTILE, :]
                    sp.dma_start(slot_rows[h][k][:, :], rows).then_inc(s_sr, 16)

            def slots_transpose(h, dst):
                pe.wait_ge(s_sr, 32 * (h + 1))
                for k in range(2):
                    mm = pe.transpose(dst[:, k * NTILE:(k + 1) * NTILE], slot_rows[h][k][:, :], ident[0:NTILE, 0:NTILE])
                mm.then_inc(s_srt, 1)

            def slots_copy(h, src):
                dve.wait_ge(s_srt, h + 1)
                dve.tensor_copy(slot_cols[:, :, h * NTILE:(h + 1) * NTILE],
                                src[:, 0:2 * NTILE].rearrange("p (k c) -> p k c", k=2)).then_inc(s_slots, 1)
                dve.wait_ge(s_slots, h + 1)

            gates_flat = gates[:, :, :].rearrange("p i e -> p (i e)")
            GATES_READY = step_a[0]
            shared_on_vector(0, 2, 2)
            pe.wait_ge(s_gw, 16)
            pe.wait_ge(s_split, 2)
            for u in range(LEAD_B):
                first_products(0, 0, FIRST_UNITS[u])
            chunk(0, 0, first=True)
            with nc.Fori(0, (NCHUNK - 2) // 2) as i:
                chunk(Lin(i, 2, 1), 1)
                chunk(Lin(i, 2, 2), 0)
            chunk(NCHUNK - 1, 1, last=True)
            chunk_evacuate(NCHUNK - 1, 1)
            chunk_transposes(NCHUNK - 1, 1)
            chunk_scores(NCHUNK - 1, 1, last=True)
            chunk_store_scores(NCHUNK - 1, 1, last=True)
            choice_scores(1)
            chunk_store_tokens(NCHUNK - 1, 1)

            choice_store(0)
            prepare_weights()
            hb = th + pb
            stage_b.close()

            HALF_TILES = 4
            h_bank, y_bank, m_bank = bank[0:4], bank[4:6], bank[6:8]
            cgt = [sb0(f"cgt{k}", [P, HALF_TILES, C]) for k in range(2)]
            onehot = [sb0(f"onehot{k}", [P, HALF_TILES * SLOT_TILE]) for k in range(2)]
            s_ld, s_oh, s_ga2, s_gx = [sem("s_ld0"), sem("s_ld1")], sem("s_oh"), sem("s_ga2"), sem("s_gx")
            s_res = sem("s_res")
            onehot0 = [big[:, E * SLOT_GE + par * HALF_TILES * SLOT_TILE:E * SLOT_GE + (par + 1) * HALF_TILES * SLOT_TILE]
                       for par in range(2)]

            def gather_loads_first(par):
                rows = i_dram[par * HALF_TILES:(par + 1) * HALF_TILES, :].rearrange("i s -> (i s)")
                sp.dma_start(onehot0[par], rows.partition_broadcast(P)).then_inc(s_ld[par], 16)

            def gather_loads(g, par):
                k = g * 2 + par
                sp.wait_ge(s_ga2, val(2 * k - 2))
                rows = i_dram[ds(k * HALF_TILES, HALF_TILES), :].rearrange("i s -> (i s)")
                sp.dma_start(onehot[par][:, :], rows.partition_broadcast(P)).then_inc(s_ld[par], 16)
                sp.dma_start(cgt[par][:, :, :], ctok[:, ds(k * HALF_TILES, HALF_TILES), :]).then_inc(s_ld[par], 16)

            def gather_onehot(g, par):
                dve.wait_ge(s_ld[par], val(32 * g + 16))
                dst = onehot0[par] if below(g, 1) else onehot[par][:, :]
                dve.tensor_scalar(dst, dst, part[:, 0:1], None,
                                  ALU.is_equal).then_inc(s_oh, 1)

            def gather_product(g, par, b):
                k = g * 2 + par
                dst = m_bank[b]
                pe.wait_ge(s_oh, val(k + 1))
                if not below(k, 1):
                    pe.wait_ge(s_gx, val(2 * (k - 1) + b + 1))
                if par == 0 and not below(g, 2):
                    pe.wait_ge(s_res, val(2 * (g - 2) + b + 1))
                for i in range(2):
                    tile = 2 * b + i
                    slots = slice(tile * SLOT_TILE, (tile + 1) * SLOT_TILE)
                    if below(g, 1):
                        tokens, chosen = ctok[:, par * HALF_TILES + tile, :], onehot0[par][:, slots]
                    else:
                        tokens, chosen = cgt[par][:, tile, :], onehot[par][:, slots]
                    mm = pe.matmul(dst[:, i * SLOT_TILE:(i + 1) * SLOT_TILE], tokens, chosen, start=True, stop=True)
                mm.then_inc(s_ga2, 1)

            def gather_copy(g, par, b):
                group_x = big[:, ds(g * (E * SLOT_GE), E * SLOT_GE)].rearrange("p (e k) -> p e k", e=E)
                act.wait_ge(s_ga2, val(2 * (g * 2 + par) + b + 1))
                for i in range(2):
                    at = (par * HALF_TILES + 2 * b + i) * SLOT_E
                    cp = act.copy(group_x[:, :, at:at + SLOT_E],
                                  m_bank[b][:, i * SLOT_TILE:(i + 1) * SLOT_TILE].rearrange("p (e k) -> p e k", e=E))
                cp.then_inc(s_gx, 1)

            for eng in (pe, dve):
                eng.wait_ge(s_down, NCHUNK * NUNITS)
            choice_exp(1)
            sp.wait_ge(s_vc, val(32))
            sp.wait_ge(s_gg, (NCHUNK - 1) * NRO)
            for par in range(2):
                gather_loads_first(par)
            load_slots(0)
            sp.wait_ge(s_ct, NCHUNK)
            sp.wait_ge(s_down, NCHUNK * NUNITS)
            choice_store(1)
            pe.wait_ge(s_sce, NCHUNK)
            pe.wait_ge(s_ct, NCHUNK)
            for par in range(2):
                gather_onehot(0, par)
                for b in range(2):
                    gather_product(0, par, b)
                    gather_copy(0, par, b)
                if par == 0:
                    choice_probs(1)
                    choice_transpose(1, y_bank[1])
            choice_tables(1, y_bank[1])
            slots_transpose(0, y_bank[0])
            slots_copy(0, y_bank[0])

            yT = sb0("yT", [P, TILES_GROUP, E, SLOT_E])
            ysl = sb0("ysl", [P, 2 * TILES_GROUP, P])
            w1_hl = [[sb0(f"w1_{k}{b}", [P, H0], F32R) for k in ("high", "low")] for b in range(2)]
            xin_hl = [[sb0(f"xin_{k}{b}", [P, SLOT_GE], F32R) for k in ("high", "low")] for b in range(2)]
            s_es = sem("s_es")
            scat = sb0("scat", [P, 2 * TILES_GROUP, P])
            s_h, s_hg, s_y2, s_y, s_ye, s_yt, s_yl, s_st, s_so = (sem(n) for n in (
                "s_h", "s_hg", "s_y2", "s_y", "s_ye", "s_yt", "s_yl", "s_st", "s_so"))
            U2 = 2 * E

            def isfirst(g, cond):
                return below(g, 1) and cond

            def expert_split(g, e):
                k = g * E + e
                if e == 0:
                    dve.wait_ge(s_gx, val(4 * (g + 1)))
                if not isfirst(g, e < 2):
                    dve.wait_ge(s_h, val(2 * k - 2))
                (wh, wl), (xh, xl) = w1_hl[e % 2], xin_hl[e % 2]
                w, x = w1[:, e, :], big[:, ds(g * (E * SLOT_GE) + e * SLOT_GE, SLOT_GE)]
                dve.tensor_copy(wh[:, :], w).then_inc(s_es, 1)
                dve.tensor_copy(xh[:, :], x).then_inc(s_es, 1)
                dve.wait_ge(s_es, val(4 * k + 1))
                dve.tensor_tensor(wl[:, :], w, wh[:, :].bitcast(F32), ALU.subtract).then_inc(s_es, 1)
                dve.wait_ge(s_es, val(4 * k + 2))
                dve.tensor_tensor(xl[:, :], x, xh[:, :].bitcast(F32), ALU.subtract).then_inc(s_es, 1)

            def expert_up(g, u):
                w = g * U2 + u
                e, b = u // 2, u % 2
                if b == 0:
                    pe.wait_ge(s_es, val(4 * (g * E + e + 1)))
                if not isfirst(g, u < 4):
                    pe.wait_ge(s_hg, val(w - 3))
                for i in range(2):
                    ht = 2 * b + i
                    mm = product(h_bank[u % 4][:, i * SLOT_GE:(i + 1) * SLOT_GE], w1_hl[e % 2],
                                 slice(ht * P, (ht + 1) * P), xin_hl[e % 2], True, True)
                mm.then_inc(s_h, 1)

            def expert_down(g, u):
                w = g * U2 + u
                e, b = u // 2, u % 2
                pe.wait_ge(s_hg, val(w + 1))
                if b == 0 and not isfirst(g, e < 2):
                    pe.wait_ge(s_ye, val(g * E + e - 1))
                for i in range(2):
                    ht = 2 * b + i
                    mm = pe.matmul(y_bank[e % 2][:, 0:SLOT_GE], w2[:, e, ht, :], hb[u % 4][:, i * SLOT_GE:(i + 1) * SLOT_GE],
                                   start=(ht == 0), stop=(ht == HT - 1))
                mm.then_inc(s_y2, 1)

            GATHER_AFTER = {3: (0, 0), 5: (0, 1), 9: (1, 0), 11: (1, 1)}

            def group(g, first=False, last=False):
                if not last:
                    for par in range(2):
                        gather_loads(g + 1, par)
                if first:
                    sp.wait_ge(s_vc, 64)
                    load_slots(1)
                for u in range(U2):
                    if u + LEAD < U2:
                        expert_up(g, u + LEAD)
                    expert_down(g, u)
                    if u in GATHER_AFTER and not last:
                        gather_product(g + 1, *GATHER_AFTER[u])
                    if first and u == 12:
                        pe.wait_ge(s_gx, 7)
                        slots_transpose(1, m_bank[0])
                for u in range(U2):
                    act.wait_ge(s_h, val(g * U2 + u + 1))
                    if not isfirst(g, u < 4):
                        act.wait_ge(s_y2, val(g * U2 + u - 3))
                    act.activation(hb[u % 4][:, :], h_bank[u % 4][:, :], ACT.Gelu).then_inc(s_hg, 1)
                    if u - 2 in GATHER_AFTER and not last:
                        gather_copy(g + 1, *GATHER_AFTER[u - 2])
                for k in range(2 * TILES_GROUP):
                    if k in (2, 6) and not last:
                        gather_onehot(g + 1, k // 4)
                    if first and k == 14:
                        slots_copy(1, m_bank[0])
                    if k == 0 and not isfirst(g, True):
                        dve.wait_ge(s_so, val(2 * g))
                    col = g * (2 * TILES_GROUP) + k
                    sc_ap = slot_cols[:, :, :].rearrange("p a b -> p (a b)")
                    last_s = dve.tensor_scalar(scat[:, k, :], iota_tok[:, :], sc_ap[:, ds(col, 1)],
                                               sc_ap[:, ds(col + 2 * NTILE, 1)], ALU.is_equal, ALU.mult)
                    if k % E == E - 1:
                        last_s.then_inc(s_st, 1)
                    if k % 2 == 1:
                        e = k // 2
                        if e + 2 < E:
                            expert_split(g, e + 2)
                        elif not last:
                            expert_split(g + 1, e + 2 - E)
                        dve.wait_ge(s_y2, val(g * U2 + 2 * e + 2))
                        if e == 0 and not isfirst(g, True):
                            dve.wait_ge(s_yt, val(4 * g))
                        dve.tensor_copy(yT[:, :, e, :], y_bank[e % 2][:, 0:SLOT_GE].rearrange("p (i k) -> p i k", k=SLOT_E)
                                        ).then_inc(s_ye, 1)
                pe.wait_ge(s_ye, val((g + 1) * E))
                yflat = yT[:, :, :, :].rearrange("p i e k -> p (i e k)")
                for b in range(4):
                    m = m_bank[b % 2]
                    if b >= 2:
                        pe.wait_ge(s_yl, val(4 * g + b - 1))
                    elif last:
                        pe.wait_ge(s_res, val(2 * g - 1 + b))
                    else:
                        pe.wait_ge(s_gx, val(4 * g + 7 + b))
                    if first and b == 0:
                        pe.wait_ge(s_slots, 2)
                    for i in range(4):
                        mm = pe.transpose(m[:, i * P:(i + 1) * P], yflat[:, (4 * b + i) * P:(4 * b + i + 1) * P], ident[:, :])
                    mm.then_inc(s_yt, 1)
                    act.wait_ge(s_yt, val(4 * g + b + 1))
                    if b == 0 and not isfirst(g, True):
                        act.wait_ge(s_so, val(2 * g))
                    act.copy(ysl[:, 4 * b:4 * b + 4, :].rearrange("p i k -> p (i k)"), m[:, :]).then_inc(s_yl, 1)
                    if b % 2 == 1 and not last:
                        expert_up(g + 1, b // 2)
                for b in range(2):
                    m = m_bank[b]
                    pe.wait_ge(s_yl, val(4 * g + 4))
                    pe.wait_ge(s_st, val(2 * (g + 1)))
                    for i in range(4):
                        tile = 4 * b + i
                        for h in range(2):
                            mm = pe.matmul(m[:, i * P:(i + 1) * P], ysl[:, 2 * tile + h, :], scat[:, 2 * tile + h, :],
                                           start=(h == 0), stop=(h == 1))
                    mm.then_inc(s_so, 1)
                    dve.wait_ge(s_so, val(2 * g + b + 1))
                    if first and b == 0:
                        dve.wait_ge(s_prep, step_p[0])
                    n0 = g * (TILES_GROUP * SEQ_TILE) + b * 16
                    dve.tensor_tensor(x1[:, :, ds(n0, 16)].rearrange("p t n -> p n t"),
                                      xT[:, ds(n0 * T, 16 * T)].rearrange("p (n t) -> p n t", t=T),
                                      m[:, :].rearrange("p (n t) -> p n t", t=T), ALU.add).then_inc(s_res, 1)

            pe.wait_ge(s_wffn, 32 * E)
            pe.wait_ge(s_dc, TABLES + TURNED)
            pe.wait_ge(s_slots, 1)
            for e in range(2):
                expert_split(0, e)
            for u in range(LEAD):
                expert_up(0, u)
            group(0, first=True)
            with nc.Fori(0, GROUPS - 2) as i:
                group(Lin(i, 1, 1))
            group(GROUPS - 1, last=True)

        with ExitStack() as layers:
            def sb1(name, shape, dt=F32):
                return layers.enter_context(nc.sbuf_tensor(name, shape, dt))

            tg, tc = sb1("tg", [P, 4, N]), sb1("tc", [P, N])
            lp, lq, cell, hL = sb1("lp", [P, N]), sb1("lq", [P, N]), sb1("cell", [P, N]), sb1("hL", [P, N])
            mx1, m1, sc1 = sb1("mx1", [P, 1]), sb1("m1", [P, 1]), sb1("sc1", [P, 1])
            mx2, m2, sc2, m2w = sb1("mx2", [P, 1]), sb1("m2", [P, 1]), sb1("sc2", [P, 1]), sb1("m2w", [P, 1])
            v1, q1, q1T = sb1("v1", [P, N]), sb1("q1", [P, N], BF16), sb1("q1T", [P, N], BF16)
            u_int, m_row = sb1("u_int", [P, HT, N]), sb1("m_row", [P, N])
            u_sb, z_conv, y_part, y_full = (sb1(n, [P, HT, N]) for n in ("u_sb", "z_conv", "y_part", "y_full"))
            th1, hs = sb1("th_ffn1", [P, HT, N]), sb1("hs", [P, HT, N])
            v2, q2 = sb1("v2", [P, HT * P]), sb1("q2", [P, HT * P], BF16)
            q2T = sb1("q2T", [P, HT, N], BF16)
            ys = sb1("ys", [P, C])
            h2 = sb1("h2", [P, N])
            g2 = sb1("g2", [P, HT, N])
            g3, p3, pre3, h3, h3_prev = (sb1(n, [P, N]) for n in ("g3", "p3", "pre3", "h3", "h3_prev"))
            leaked, z_half, diff = (sb1(n, [P, N]) for n in ("leaked", "z_half", "diff"))
            xr, xk, tr, kr, kk, o1 = (sb1(n, [P, N]) for n in ("xr", "xk", "tr", "kr", "kk", "o1"))
            magic, halves, units = sb1("magic", [P, 1]), sb1("halves", [P, N]), sb1("units", [P, N])
            leak_full = sb1("leak_full", [P, N])
            pool_tick = sb1("pool_tick", [P, 2])
            ident_bf = sb1("ident_bf", [P, P], BF16)

            s_state = sem("s_state")
            pool_states = [(cell, 0.0), (magic, MAGIC), (h3_prev, 0.0), (halves, 0.5), (units, 1.0), (pool_tick, 0.0)]
            dve_states = [(h2, condT[:, :]), (h3, condT[:, :]), (ident_bf, ident[:, :]),
                          (leak_full, leak[:, 0:1].to_broadcast([P, N]))]
            pool.wait_ge(s_res, 2 * GROUPS)
            for dst, value in pool_states:
                pool.memset(dst[:, :], value).then_inc(s_state, 1)
            for dst, src in dve_states:
                dve.tensor_copy(dst[:, :], src).then_inc(s_state, 1)
            dve.tensor_scalar(hL[:, :], condT[:, :], 2.0, None, ALU.mult).then_inc(s_state, 1)
            STATES = len(pool_states) + len(dve_states) + 1
            for eng in (pe, act, dve, pool):
                eng.wait_ge(s_state, STATES)
                eng.wait_ge(s_res, 2 * GROUPS)

            B_GATE, B_U, B_V, B_F2, B_TR, B_R2, B_R3, B_Q = bank
            ps_V2 = B_TR[:, 0:2 * P]
            ps_y = B_TR[:, 2 * P:3 * P]
            ps_ysT = B_R3[:, 0:P]
            ps_tr1 = B_R2[:, 0:P]
            q1_ps = B_R2[:, P:P + P // 2].bitcast(BF16)
            ps_ms = B_Q[:, 0:P]
            ps_r2 = B_R3[:, P:2 * P]
            ps_F2down = B_TR[:, 3 * P:4 * P]
            ps_r3 = B_R2[:, 2 * P:3 * P]
            ps_r = B_Q[:, P:2 * P]
            ps_k = B_Q[:, 2 * P:3 * P]
            ps_v = B_R3[:, 2 * P:3 * P]
            q2_ps = ps_V2.bitcast(BF16)

            def flat(a):
                return a[:, :, :].rearrange("p f n -> p (f n)")

            def x_at(step):
                return x1[:, ds(step, 1), :].rearrange("p o n -> p (o n)")

            stages = {}
            counter = {}

            def stage(eng, *waits, first=0, last=T - 1, edges=()):
                def declare(f):
                    name = f.__name__.rstrip("_")
                    counter[name] = sem("t_" + name)
                    stages[name] = (eng, waits, edges, f, first, last)
                    return f
                return declare

            def run(name, t):
                eng, waits, edges, f, first, last = stages[name]
                if isinstance(t, int) and not first <= t <= last:
                    return
                if eng is pool:
                    pool.wait_ge(s_state, STATES)
                for other, offset in waits if isinstance(t, Lin) else waits + edges:
                    step = t + offset
                    if isinstance(step, int):
                        if step < stages[other][4]:
                            continue
                        step = min(step, stages[other][5])
                    eng.wait_ge(counter[other], val(step + 1 - stages[other][4]))
                f(t).then_inc(counter[name], 1)

            @stage(pe, ("tg", -1))
            def gates_x(t):
                pe.matmul(B_GATE[:, :], lstm_bias[:, :], sel_lstm[:, :], start=True, stop=False, skip_group_check=True)
                for q in range(4):
                    mm = pe.matmul(B_GATE[:, q * N:(q + 1) * N], lstm_wx[:, q * P:(q + 1) * P], x_at(t),
                                   start=False, stop=False, skip_group_check=True)
                return mm

            @stage(pe, ("hL", -1))
            def gates_h(t):
                for q in range(4):
                    mm = pe.matmul(B_GATE[:, q * N:(q + 1) * N], lstm_wh[:, q * P:(q + 1) * P], hL[:, :],
                                   start=False, stop=True, skip_group_check=True)
                return mm

            @stage(act, ("gates_h", 0), ("hL", -1))
            def tg_(t):
                return act.activation(flat(tg), B_GATE[:, :], ACT.Tanh, scale=0.5)

            @stage(dve, ("tg", 0), ("cell", -1))
            def lp_(t):
                return dve.scalar_tensor_tensor(lp[:, :], tg[:, 1, :], 1.0, cell[:, :], ALU.add, ALU.mult)

            @stage(dve, ("tg", 0), ("cell", -1))
            def lq_(t):
                return dve.scalar_tensor_tensor(lq[:, :], tg[:, 0, :], 1.0, tg[:, 3, :], ALU.add, ALU.mult)

            @stage(dve, ("lp", 0), ("lq", 0), ("tc", -1))
            def cell_(t):
                return dve.scalar_tensor_tensor(cell[:, :], lp[:, :], 0.5, lq[:, :], ALU.mult, ALU.add)

            @stage(act, ("cell", 0), ("hL", -1))
            def tc_(t):
                return act.activation(tc[:, :], cell[:, :], ACT.Tanh, scale=0.5)

            @stage(dve, ("tc", 0), ("tr1", -1), ("gates_h", 0))
            def hL_(t):
                return dve.scalar_tensor_tensor(hL[:, :], tg[:, 2, :], 1.0, tc[:, :], ALU.add, ALU.mult)

            @stage(pe, ("hL", 0), ("v1", -1), ("q1T", -1),
                   edges=(("g3", -7),))
            def tr1(t):
                return pe.transpose(ps_tr1, hL[:, :], ident[:, :])

            @stage(dve, ("tr1", 0), ("m1", -1))
            def mx1_(t):
                return dve.tensor_reduce(mx1[:, :], ps_tr1, X, ALU.max, apply_absolute_value=True)

            @stage(dve, ("mx1", 0), ("ms", -1))
            def m1_(t):
                return dve.tensor_scalar(m1[:, :], mx1[:, :], 2e-5, 1.0 / 127.0, ALU.max, ALU.mult)

            @stage(dve, ("m1", 0), ("v1", -1))
            def sc1_(t):
                return dve.reciprocal(sc1[:, :], m1[:, :])

            @stage(act, ("sc1", 0), ("q1", -1))
            def v1_(t):
                return act.activation(v1[:, :], ps_tr1, ACT.Identity, bias=magic[:, 0:1], scale=sc1[:, 0:1])

            @stage(dve, ("v1", 0), ("tr2", -1))
            def q1_(t):
                return dve.tensor_scalar(q1[:, :], v1[:, :], MAGIC, 127.0, ALU.subtract, ALU.min)

            @stage(pe, ("q1", 0), ("g3", -6),
                   edges=(("v1", 0),))
            def tr2(t):
                return pe.transpose(q1_ps, q1[:, :], ident_bf[:, :])

            @stage(act, ("tr2", 0), ("u", -1))
            def q1T_(t):
                return act.copy(q1T[:, :], q1_ps)

            @stage(pe, ("q1T", 0), ("u_int", -1))
            def u(t):
                for f in range(HT):
                    mm = pe.matmul(B_U[:, f * N:(f + 1) * N], ffn1_w1[:, f * P:(f + 1) * P], q1T[:, :],
                                   start=True, stop=True)
                return mm

            @stage(act, ("u", 0), ("u_sb", -1))
            def u_int_(t):
                return act.copy(flat(u_int), B_U[:, :])

            @stage(pe, ("m1", 0), ("m_row", -1), ("kr", -8), ("tr", -8))
            def ms(t):
                return pe.transpose(ps_ms, m1[:, 0:1].to_broadcast([P, P]), ident[:, :])

            @stage(act, ("ms", 0), ("u_sb", -1))
            def m_row_(t):
                return act.copy(m_row[:, :], ps_ms)

            @stage(pool, ("u_int", 0), ("m_row", 0), ("y_part", -1), ("z_conv", -1))
            def u_sb_(t):
                return pool.tensor_tensor(u_sb[:, :, :], u_int[:, :, :],
                                          m_row[:, :].rearrange("p (o n) -> p o n", o=1).to_broadcast([P, HT, N]), ALU.mult)

            @stage(dve, ("u_sb", 0), ("y_part", -1), ("hs", -2), first=1, last=T)
            def y_full_(t):
                if isinstance(t, int) and t == T:
                    return dve.tensor_copy(y_full[:, :, :], y_part[:, :, :])
                for f in range(HT):
                    op = dve.scalar_tensor_tensor(y_full[:, f, :], u_sb[:, f, :], conv_w[:, f, 2:3], y_part[:, f, :],
                                                  ALU.mult, ALU.add)
                return op

            @stage(dve, ("u_sb", 0), ("z_conv", -1), ("y_full", 0))
            def y_part_(t):
                for f in range(HT):
                    if isinstance(t, int) and t == 0:
                        op = dve.tensor_scalar(y_part[:, f, :], u_sb[:, f, :], conv_w[:, f, 1:2], conv_b[:, f:f + 1],
                                               ALU.mult, ALU.add)
                    else:
                        op = dve.scalar_tensor_tensor(y_part[:, f, :], u_sb[:, f, :], conv_w[:, f, 1:2],
                                                      z_conv[:, f, :], ALU.mult, ALU.add)
                return op

            @stage(pool, ("u_sb", 0), ("y_part", 0))
            def z_conv_(t):
                pool.tensor_tensor(pool_tick[:, 0:1], pool_tick[:, 1:2], pool_tick[:, 1:2], ALU.add)
                for f in range(HT):
                    op = pool.tensor_scalar(z_conv[:, f, :], u_sb[:, f, :], conv_w[:, f, 0:1], conv_b[:, f:f + 1],
                                            ALU.mult, ALU.add)
                return op

            @stage(act, ("y_full", 1), ("hs", -1))
            def th1_(t):
                return act.activation(flat(th1), flat(y_full), ACT.Tanh, scale=0.5)

            @stage(dve, ("th1", 0), ("V", -1))
            def hs_(t):
                return dve.scalar_tensor_tensor(flat(hs), flat(th1), 1.0, flat(y_full), ALU.add, ALU.mult)

            @stage(pe, ("hs", 0), ("v2", -1))
            def V(t):
                for f in range(HT):
                    mm = pe.transpose(B_V[:, f * P:(f + 1) * P], hs[:, f, :], ident[:, :])
                return mm

            @stage(dve, ("V", 0), ("m2", -1))
            def mx2_(t):
                return dve.tensor_reduce(mx2[:, :], B_V[:, :], X, ALU.max, apply_absolute_value=True)

            @stage(dve, ("mx2", 0), ("m2w", -1))
            def m2_(t):
                return dve.tensor_scalar(m2[:, :], mx2[:, :], 2e-5, 1.0 / 127.0, ALU.max, ALU.mult)

            @stage(dve, ("m2", 0), ("v2", -1))
            def sc2_(t):
                return dve.reciprocal(sc2[:, :], m2[:, :])

            @stage(act, ("sc2", 0), ("q2", -1))
            def v2_(t):
                return act.activation(v2[:, :], B_V[:, :], ACT.Identity, bias=magic[:, 0:1], scale=sc2[:, 0:1])

            @stage(dve, ("v2", 0), ("V2", -1))
            def q2_(t):
                return dve.tensor_scalar(q2[:, :], v2[:, :], MAGIC, 127.0, ALU.subtract, ALU.min)

            @stage(act, ("m2", 0), ("ys", -1))
            def m2w_(t):
                return act.activation(m2w[:, :], m2[:, :], ACT.Copy, scale=half_ws2[:, 0:1])

            @stage(pe, ("q2", 0), ("q2T", -1), ("x3", -2),
                   edges=(("ys", -1),))
            def V2(t):
                for f in range(HT):
                    mm = pe.transpose(q2_ps[:, f * P:(f + 1) * P], q2[:, f * P:(f + 1) * P], ident_bf[:, :])
                return mm

            @stage(act, ("V2", 0), ("y", -1))
            def q2T_(t):
                return act.copy(flat(q2T), q2_ps)

            @stage(pe, ("q2T", 0), ("ys", -1),
                   edges=(("x3", -2),))
            def y(t):
                for f in range(HT):
                    mm = pe.matmul(ps_y, q2T[:, f, :], ffn1_w2[:, f, :], start=(f == 0), stop=(f == HT - 1))
                return mm

            @stage(act, ("y", 0), ("m2w", 0), ("ysT", -1))
            def ys_(t):
                return act.activation(ys[:, :], ps_y, ACT.Copy, scale=m2w[:, 0:1])

            @stage(pe, ("ys", 0), ("x2", -1), ("o1", -4),
                   edges=(("h2", -1),))
            def ysT(t):
                return pe.transpose(ps_ysT, ys[:, :], ident[:, :])

            @stage(dve, ("ysT", 0))
            def x2(t):
                return dve.tensor_tensor(x_at(t), x_at(t), ps_ysT, ALU.add)

            @stage(pe, ("x2", 0), ("h2", -1),
                   edges=(("o1", -4),))
            def r2(t):
                pe.matmul(ps_r2, rnn_wx[:, :], x_at(t), start=True, stop=False)
                return pe.matmul(ps_r2, rnn_wh[:, :], h2[:, :], start=False, stop=True)

            @stage(act, ("r2", 0), ("F2up", -1))
            def h2_(t):
                return act.activation(h2[:, :], ps_r2, ACT.Tanh, bias=rnn_b[:, 0:1])

            @stage(pe, ("g2", -1))
            def F2bias(t):
                return pe.matmul(B_F2[:, :], ffn2_bias[:, :], sel_rows[:, :], start=True, stop=False,
                                 skip_group_check=True)

            @stage(pe, ("h2", 0))
            def F2up(t):
                for f in range(HT):
                    mm = pe.matmul(B_F2[:, f * N:(f + 1) * N], ffn2_w1[:, f * P:(f + 1) * P], h2[:, :],
                                   start=False, stop=True, skip_group_check=True)
                return mm

            @stage(act, ("F2up", 0), ("F2down", -1))
            def g2_(t):
                return act.activation(flat(g2), B_F2[:, :], ACT.Gelu)

            @stage(pe, ("g2", 0), ("x3", -1), ("ys", 1),
                   edges=(("q2T", 1),))
            def F2down(t):
                for f in range(HT):
                    mm = pe.matmul(ps_F2down, ffn2_w2[:, f, :], g2[:, f, :], start=(f == 0), stop=(f == HT - 1))
                return mm

            @stage(dve, ("F2down", 0))
            def x3(t):
                return dve.scalar_tensor_tensor(x_at(t), ps_F2down, ffn2_b2[:, 0:1], x_at(t), ALU.add, ALU.add)

            @stage(pe, ("x3", 0), ("h3", -1), ("g3", -1), ("v1", 6),
                   edges=(("q1T", 5),))
            def r3(t):
                pe.matmul(ps_r3, leak_wz[:, :], x_at(t), start=True, stop=False)
                return pe.matmul(ps_r3, leak_wh[:, :], h3[:, :], start=False, stop=True)

            @stage(act, ("r3", 0), ("p3", -1))
            def g3_(t):
                return act.activation(g3[:, :], ps_r3, ACT.Tanh, bias=leak_b_half[:, 0:1], scale=0.5)

            @stage(pool, ("x3", 0), ("p3", -1))
            def z_half_(t):
                return pool.tensor_tensor(z_half[:, :], x_at(t), halves[:, :], ALU.mult)

            @stage(pool, ("h3", -1), ("pre3", -1))
            def leaked_(t):
                return pool.tensor_tensor(leaked[:, :], h3[:, :], leak_full[:, :], ALU.mult)

            @stage(dve, ("g3", 0), ("z_half", 0), ("pre3", -1))
            def p3_(t):
                return dve.scalar_tensor_tensor(p3[:, :], g3[:, :], 1.0, z_half[:, :], ALU.add, ALU.mult)

            @stage(pool, ("p3", 0), ("leaked", 0), ("h3", -1))
            def pre3_(t):
                return pool.tensor_tensor(pre3[:, :], p3[:, :], leaked[:, :], ALU.add)

            @stage(act, ("pre3", 0), ("r3", 0), ("leaked", 0), ("h3_prev", -1))
            def h3_(t):
                return act.activation(h3[:, :], pre3[:, :], ACT.Tanh)

            @stage(pool, ("h3", 0), ("h3_prev", -1), ("xr", -1), ("xk", -1))
            def diff_(t):
                return pool.tensor_tensor(diff[:, :], h3[:, :], h3_prev[:, :], ALU.subtract)

            @stage(dve, ("diff", 0), ("rk", -1))
            def xr_(t):
                return dve.scalar_tensor_tensor(xr[:, :], diff[:, :], mu_r[:, 0:1], h3_prev[:, :], ALU.mult, ALU.add)

            @stage(dve, ("diff", 0), ("rk", -1))
            def xk_(t):
                return dve.scalar_tensor_tensor(xk[:, :], diff[:, :], mu_k[:, 0:1], h3_prev[:, :], ALU.mult, ALU.add)

            @stage(pool, ("xr", 0), ("xk", 0))
            def h3_prev_(t):
                return pool.tensor_tensor(h3_prev[:, :], h3[:, :], units[:, :], ALU.mult)

            @stage(pe, ("xr", 0), ("xk", 0), ("tr", -1), ("kr", -1), ("m_row", 7))
            def rk(t):
                pe.matmul(ps_r, ffn3_wr[:, :], xr[:, :], start=True, stop=True)
                return pe.matmul(ps_k, ffn3_wk[:, :], xk[:, :], start=True, stop=True)

            @stage(act, ("rk", 0), ("kk", -1))
            def kr_(t):
                return act.activation(kr[:, :], ps_k, ACT.Relu)

            @stage(act, ("rk", 0), ("o1", -1))
            def tr_(t):
                return act.activation(tr[:, :], ps_r, ACT.Tanh, scale=0.5)

            @stage(pool, ("kr", 0), ("v", -1))
            def kk_(t):
                return pool.tensor_tensor(kk[:, :], kr[:, :], kr[:, :], ALU.mult)

            @stage(pe, ("kk", 0), ("o1", -1), ("h2", 3),
                   edges=(("x2", 3),))
            def v(t):
                return pe.matmul(ps_v, ffn3_wv[:, :], kk[:, :], start=True, stop=True)

            @stage(dve, ("v", 0), ("tr", 0), ("out", -1))
            def o1_(t):
                return dve.scalar_tensor_tensor(o1[:, :], tr[:, :], 1.0, ps_v, ALU.add, ALU.mult)

            @stage(pool, ("o1", 0))
            def out_(t):
                return pool.tensor_tensor(x_at(t), x_at(t), o1[:, :], ALU.add)

            ORDER = [
                ("sc2", 5), ("rk", 9), ("th1", 4), ("F2bias", 6), ("ysT", 6), ("F2down", 7), ("tg", 0), ("m1", 1),
                ("lp", 0), ("h3", 8), ("gates_x", -1), ("sc1", 1), ("u_int", 2), ("diff", 8), ("x2", 6), ("v2", 5),
                ("v1", 1), ("r2", 6), ("hs", 4), ("lq", 0), ("x3", 7), ("z_conv", 3), ("V", 4), ("q2", 5), ("r3", 7),
                ("kr", 9), ("u_sb", 2), ("xk", 8), ("cell", 0), ("m2w", 5), ("tr", 9), ("h2", 6), ("q1", 1),
                ("tc", 0), ("kk", 9), ("xr", 8), ("ms", 1), ("V2", 5), ("g3", 7), ("mx2", 4), ("z_half", 7),
                ("hL", 0), ("leaked", 7), ("y_full", 2), ("q2T", 5), ("F2up", 6), ("tr2", 1), ("p3", 7),
                ("h3_prev", 8), ("pre3", 7), ("m_row", 1), ("v", 9), ("q1T", 1), ("y", 5), ("o1", 9), ("g2", 6),
                ("m2", 4), ("gates_h", -1), ("y_part", 2), ("ys", 5), ("tr1", 0), ("u", 1), ("out", 9), ("mx1", 0)]
            AHEAD, LAST_LAG = -min(lag for _, lag in ORDER), max(lag for _, lag in ORDER)
            s_out = sem("s_out")

            def iteration(i):
                for name, lag in ORDER:
                    run(name, i - lag)
                t = i - dict(ORDER)["out"]
                if isinstance(t, Lin) or 0 <= t < T:
                    sp.wait_ge(counter["out"], val(t + 1))
                    sp.dma_start(out[:, ds(t, 1), :], x1[:, ds(t, 1), :]).then_inc(s_out, 16)

            FIRST, END = LAST_LAG + 3, T - 1 - AHEAD
            for i in range(-AHEAD, FIRST):
                iteration(i)
            with nc.Fori(0, END - FIRST) as j:
                iteration(Lin(j, 1, FIRST))
            for i in range(END, T + LAST_LAG):
                iteration(i)
            sp.wait_ge(s_out, 16 * T)


def kernel(**inputs):
    import numpy as np
    import concourse.bacc as bacc
    from concourse.bass_utils import run_bass_kernel_spmd

    i = {k: np.asarray(v) for k, v in inputs.items()}
    wr = i["L0_cond_W_router"]
    arrays = {
        "xT": i["x"].transpose(2, 0, 1).reshape(C, TOK),
        "condT": i["cond_1024"].T,
        "wr_x": wr[:, :C].T,
        "wr_t": wr[:, C:].T,
        "router_bias": i["L0_cond_router_bias"],
        "s_w1T": i["L0_cond_s_w1"].reshape(-1, C).T,
        "s_w3T": i["L0_cond_s_w3"].reshape(-1, C).T,
        "s_w2T": i["L0_cond_s_w2"].transpose(0, 2, 1).reshape(HS_TILES, P, C).transpose(1, 0, 2).reshape(P, -1),
        "r_w1T": i["L0_cond_r_w1"].reshape(-1, C).T,
        "r_w2T": i["L0_cond_r_w2"].transpose(2, 0, 1).reshape(P, -1),
        "gate_w": i["L0_ffn_gate_w"],
        "f_w1": i["L0_ffn_w1"].transpose(1, 0, 2),
        "f_w2": i["L0_ffn_w2"].reshape(E, HT, P, C).transpose(2, 0, 1, 3),
    }
    lw, cw = i["L3_cond_W"], i["L1_ffn_conv_w"]

    def column(a):
        return a.reshape(-1, P).T

    def hidden_rows(a):
        return a.T.reshape(HT, P, C).transpose(1, 0, 2)

    arrays.update({
        "lstm_wx": i["L1_cond_Wx"], "lstm_wh": i["L1_cond_Wh"], "lstm_b": i["L1_cond_b"].reshape(4, P),
        "ffn1_w1": i["L1_ffn_w1"].T, "ffn1_w2": hidden_rows(i["L1_ffn_w2"]).reshape(P, -1),
        "conv_w": cw.reshape(HT, P, 3).transpose(1, 0, 2), "conv_b": column(i["L1_ffn_conv_b"]),
        "rnn_wx": i["L2_cond_Wx"], "rnn_wh": i["L2_cond_Wh"], "rnn_b": column(i["L2_cond_b"]),
        "ffn2_w1": i["L2_ffn_W1"].T, "ffn2_b1": i["L2_ffn_b1"].reshape(HT, P),
        "ffn2_w2": hidden_rows(i["L2_ffn_W2"]), "ffn2_b2": column(i["L2_ffn_b2"]),
        "leak_wh": lw[:, :C].T, "leak_wz": lw[:, C:].T, "leak_b": column(i["L3_cond_b"]),
        "alpha": column(i["L3_cond_alpha"]),
        "ffn3_wr": i["L3_ffn_W_r"].T, "ffn3_wk": i["L3_ffn_W_k"].T, "ffn3_wv": i["L3_ffn_W_v"].T,
        "mu_r": column(i["L3_ffn_mu_r"]), "mu_k": column(i["L3_ffn_mu_k"]),
    })
    arrays = {k: np.ascontiguousarray(a) for k, a in arrays.items()}
    nc = bacc.Bacc("TRN2", target_bir_lowering=False, num_devices=1)
    aps = {k: nc.dram_tensor("in_" + k, a.shape, mybir.dt.from_np(a.dtype), kind="ExternalInput").ap() for k, a in arrays.items()}
    out = nc.dram_tensor("outT", (C, T, N), F32, kind="ExternalOutput").ap()
    build_program(nc, aps, out)
    r = run_bass_kernel_spmd(nc, [{"in_" + k: a for k, a in arrays.items()}], core_ids=[0])
    return np.ascontiguousarray(r.results[0]["outT"].transpose(2, 1, 0))
```
